# Optimizing a Trainium2 kernel written in Bass

```python
import numpy as np
import jax
import jax.numpy as jnp

def _softmax(x, axis=-1):
    return jax.nn.softmax(x, axis=axis)

def _gelu(x):
    return jax.nn.gelu(x, approximate=True)

def _silu(x):
    return jax.nn.silu(x)

def _sigmoid(x):
    return jax.nn.sigmoid(x)

def _layernorm(x, axis=-1, eps=1e-05):
    m = jnp.mean(x, axis=axis, keepdims=True)
    v = jnp.var(x, axis=axis, keepdims=True)
    return (x - m) / jnp.sqrt(v + eps)

def _scatter_add(tgt, idx, src, axis=0):
    return tgt.at[idx].add(src)

def _segment_sum(src, seg, n):
    return jax.ops.segment_sum(src, seg, n)
kernel_name = 'mk_xattn_ffn_d2_seqx_r4_09706e'

def setup_inputs(seed: int=0):
    np.random.seed(seed)
    _w = jnp.asarray

    def _rec_inputs():
        import jax
        import jax.numpy as jnp
        _rk = jax.random.key(seed)
        x = 7.22e-05 + 1 * jax.random.normal(jax.random.fold_in(_rk, 1), (4, 512, 512), jnp.float32)
        _lenS = 512 - jax.random.randint(jax.random.fold_in(_rk, 7), (4,), 0, max(1, 512 // 4) + 1, jnp.int32)
        _lenS2 = 512 - jax.random.randint(jax.random.fold_in(_rk, 8), (4,), 0, max(1, 512 // 4) + 1, jnp.int32)
        _ctx_512P = jax.random.normal(jax.random.fold_in(_rk, 11), (4, 16, 128), jnp.float32)
        _ctx_512c = jax.random.dirichlet(jax.random.fold_in(_rk, 511), 0.3 * jnp.ones((16,), jnp.float32), (4, 512))
        _ctx_512t = jnp.einsum('bsk,bkd->bsd', _ctx_512c, _ctx_512P)
        _ctx_512t = _ctx_512t * jax.lax.rsqrt(jnp.mean(jnp.square(_ctx_512t)) + 1e-12) * 0.953939
        ctx_512 = -0.000514642 + 1.00011 * (_ctx_512t + 0.3 * jax.random.normal(jax.random.fold_in(_rk, 611), (4, 512, 128), jnp.float32))
        return (x, ctx_512)
    x, ctx_512 = _rec_inputs()

    def _L0_xattn_setup():
        import jax, jax.numpy as jnp
        import numpy as np
        N_HEADS = 16
        N_KV_HEADS = 4
        ROPE_THETA = 10000.0
        EPS = 1e-05

        def _rms_norm(x, w):
            var = jnp.mean(x * x, axis=-1, keepdims=True)
            return x * jax.lax.rsqrt(var + EPS) * w

        def _rope_sin_cos(T, head_dim, dtype):
            inv_freq = 1.0 / ROPE_THETA ** (jnp.arange(0, head_dim, 2, dtype=jnp.float32) / head_dim)
            t = jnp.arange(T, dtype=jnp.float32)
            freqs = jnp.outer(t, inv_freq)
            emb = jnp.concatenate([freqs, freqs], -1)
            return (jnp.sin(emb).astype(dtype)[None, None], jnp.cos(emb).astype(dtype)[None, None])

        def _rotate_half(x):
            h = x.shape[-1] // 2
            x1, x2 = (x[..., :h], x[..., h:])
            return jnp.concatenate([-x2, x1], axis=-1)
        key = jax.random.key(seed)
        ks = jax.random.split(key, 6)
        B, T, C = (2, 512, 512)
        Ckv = C // N_HEADS * N_KV_HEADS
        return {'q': jax.random.normal(ks[0], (B, T, C), jnp.float32), 'k': jax.random.normal(ks[1], (B, T, Ckv), jnp.float32), 'v': jax.random.normal(ks[2], (B, T, Ckv), jnp.float32), 'q_norm_w': jnp.ones((C,), jnp.float32), 'k_norm_w': jnp.ones((Ckv,), jnp.float32), 'w_out': jax.random.normal(ks[3], (C, C), jnp.float32) * C ** (-0.5)}
    _L0_xattn_all = _L0_xattn_setup()
    _L0_xattn_in = {k: v for k, v in _L0_xattn_all.items() if k in ('q_norm_w', 'k_norm_w', 'w_out')}
    del _L0_xattn_all

    def _L0_ffn_setup():
        import jax, jax.numpy as jnp
        import numpy as np
        B, L, D = (2, 256, 512)
        E, TOP_K, RANK, DFF = (8, 2, 8, 1376)

        def _lora(x, A, Bm, scale):
            return x @ A @ Bm * scale

        def _expert_lora(x, A, Bm, w, scale):
            xA = jnp.einsum('bld,edr->bler', x, A)
            xAB = jnp.einsum('bler,erd->bled', xA, Bm) * scale
            return (xAB * w).sum(axis=2)
        key = jax.random.key(seed)
        ks = jax.random.split(key, 18)
        r = lambda k, s, sc: jax.random.normal(k, s, dtype=jnp.float32) * sc
        inv_d = 1.0 / np.sqrt(D)
        inv_f = 1.0 / np.sqrt(DFF)
        return {'x': r(ks[0], (B, L, D), 1.0), 'W_router': r(ks[1], (D, E), inv_d), 'W_gate': r(ks[2], (D, DFF), inv_d), 'W_up': r(ks[3], (D, DFF), inv_d), 'W_down': r(ks[4], (DFF, D), inv_f), 'sA_gate': r(ks[5], (D, RANK), inv_d), 'sB_gate': r(ks[6], (RANK, DFF), 0.02), 'sA_up': r(ks[7], (D, RANK), inv_d), 'sB_up': r(ks[8], (RANK, DFF), 0.02), 'sA_down': r(ks[9], (DFF, RANK), inv_f), 'sB_down': r(ks[10], (RANK, D), 0.02), 'A_gate': r(ks[11], (E, D, RANK), inv_d), 'B_gate': r(ks[12], (E, RANK, DFF), 0.02), 'A_up': r(ks[13], (E, D, RANK), inv_d), 'B_up': r(ks[14], (E, RANK, DFF), 0.02), 'A_down': r(ks[15], (E, DFF, RANK), inv_f), 'B_down': r(ks[16], (E, RANK, D), 0.02), 'expert_bias': jnp.zeros((E,), dtype=jnp.float32)}
    _L0_ffn_all = _L0_ffn_setup()
    _L0_ffn_in = {k: v for k, v in _L0_ffn_all.items() if k in ('W_router', 'W_gate', 'W_up', 'W_down', 'sA_gate', 'sB_gate', 'sA_up', 'sB_up', 'sA_down', 'sB_down', 'A_gate', 'B_gate', 'A_up', 'B_up', 'A_down', 'B_down', 'expert_bias')}
    del _L0_ffn_all

    def _L1_xattn_setup():
        import jax, jax.numpy as jnp
        import numpy as np
        EPS = 1e-06
        IMAGE_DIMS = 512
        key = jax.random.key(seed)
        k1, k2, k3 = jax.random.split(key, 3)
        B, I, J, D = (16, 512, 512, 128)
        p = jax.random.normal(k1, (B, I, J), dtype=jnp.float32)
        k_v = jax.random.normal(k2, (B, J, D), dtype=jnp.float32)
        W_k = jax.random.normal(k3, (D, D), dtype=jnp.float32) * (1.0 / np.sqrt(D))
        b_k = jnp.zeros((D,), dtype=jnp.float32)
        ln_gamma = jnp.ones((J,), dtype=jnp.float32)
        ln_beta = jnp.zeros((J,), dtype=jnp.float32)
        return {'p': p, 'k_v': k_v, 'W_k': W_k, 'b_k': b_k, 'ln_gamma': ln_gamma, 'ln_beta': ln_beta}
    _L1_xattn_all = _L1_xattn_setup()
    _L1_xattn_in = {k: v for k, v in _L1_xattn_all.items() if k in ('W_k', 'b_k', 'ln_gamma', 'ln_beta')}
    del _L1_xattn_all

    def _L1_ffn_setup():
        import jax, jax.numpy as jnp
        import numpy as np
        B, S, H = (2, 256, 512)
        E, K, F = (64, 8, 192)
        CAP = 128
        key = jax.random.key(seed)
        k1, k2, k3, k4, k5 = jax.random.split(key, 5)
        scale_h = 1.0 / np.sqrt(H)
        scale_f = 1.0 / np.sqrt(F)
        return {'hidden_states': jax.random.normal(k1, (B, S, H), jnp.float32), 'router_w': jax.random.normal(k2, (E, H), jnp.float32) * scale_h, 'w_gate': jax.random.normal(k3, (E, H, F), jnp.float32) * scale_h, 'w_up': jax.random.normal(k4, (E, H, F), jnp.float32) * scale_h, 'w_down': jax.random.normal(k5, (E, F, H), jnp.float32) * scale_f}
    _L1_ffn_all = _L1_ffn_setup()
    _L1_ffn_in = {k: v for k, v in _L1_ffn_all.items() if k in ('router_w', 'w_gate', 'w_up', 'w_down')}
    del _L1_ffn_all
    return {'x': x, 'ctx_512': ctx_512, 'L0_xattn_q_norm_w': _L0_xattn_in['q_norm_w'], 'L0_xattn_k_norm_w': _L0_xattn_in['k_norm_w'], 'L0_xattn_w_out': _L0_xattn_in['w_out'], 'L0_ffn_W_router': _L0_ffn_in['W_router'], 'L0_ffn_W_gate': _L0_ffn_in['W_gate'], 'L0_ffn_W_up': _L0_ffn_in['W_up'], 'L0_ffn_W_down': _L0_ffn_in['W_down'], 'L0_ffn_sA_gate': _L0_ffn_in['sA_gate'], 'L0_ffn_sB_gate': _L0_ffn_in['sB_gate'], 'L0_ffn_sA_up': _L0_ffn_in['sA_up'], 'L0_ffn_sB_up': _L0_ffn_in['sB_up'], 'L0_ffn_sA_down': _L0_ffn_in['sA_down'], 'L0_ffn_sB_down': _L0_ffn_in['sB_down'], 'L0_ffn_A_gate': _L0_ffn_in['A_gate'], 'L0_ffn_B_gate': _L0_ffn_in['B_gate'], 'L0_ffn_A_up': _L0_ffn_in['A_up'], 'L0_ffn_B_up': _L0_ffn_in['B_up'], 'L0_ffn_A_down': _L0_ffn_in['A_down'], 'L0_ffn_B_down': _L0_ffn_in['B_down'], 'L0_ffn_expert_bias': _L0_ffn_in['expert_bias'], 'L1_xattn_W_k': _L1_xattn_in['W_k'], 'L1_xattn_b_k': _L1_xattn_in['b_k'], 'L1_xattn_ln_gamma': _L1_xattn_in['ln_gamma'], 'L1_xattn_ln_beta': _L1_xattn_in['ln_beta'], 'L1_ffn_router_w': _L1_ffn_in['router_w'], 'L1_ffn_w_gate': _L1_ffn_in['w_gate'], 'L1_ffn_w_up': _L1_ffn_in['w_up'], 'L1_ffn_w_down': _L1_ffn_in['w_down']}

def reference(x, ctx_512, L0_xattn_q_norm_w, L0_xattn_k_norm_w, L0_xattn_w_out, L0_ffn_W_router, L0_ffn_W_gate, L0_ffn_W_up, L0_ffn_W_down, L0_ffn_sA_gate, L0_ffn_sB_gate, L0_ffn_sA_up, L0_ffn_sB_up, L0_ffn_sA_down, L0_ffn_sB_down, L0_ffn_A_gate, L0_ffn_B_gate, L0_ffn_A_up, L0_ffn_B_up, L0_ffn_A_down, L0_ffn_B_down, L0_ffn_expert_bias, L1_xattn_W_k, L1_xattn_b_k, L1_xattn_ln_gamma, L1_xattn_ln_beta, L1_ffn_router_w, L1_ffn_w_gate, L1_ffn_w_up, L1_ffn_w_down):
    import jax
    import jax.numpy as jnp

    def _L0_xattn_ref(q, k, v, q_norm_w, k_norm_w, w_out):
        import jax, jax.numpy as jnp
        import numpy as np
        N_HEADS = 16
        N_KV_HEADS = 4
        ROPE_THETA = 10000.0
        EPS = 1e-05

        def _rms_norm(x, w):
            var = jnp.mean(x * x, axis=-1, keepdims=True)
            return x * jax.lax.rsqrt(var + EPS) * w

        def _rope_sin_cos(T, head_dim, dtype):
            inv_freq = 1.0 / ROPE_THETA ** (jnp.arange(0, head_dim, 2, dtype=jnp.float32) / head_dim)
            t = jnp.arange(T, dtype=jnp.float32)
            freqs = jnp.outer(t, inv_freq)
            emb = jnp.concatenate([freqs, freqs], -1)
            return (jnp.sin(emb).astype(dtype)[None, None], jnp.cos(emb).astype(dtype)[None, None])

        def _rotate_half(x):
            h = x.shape[-1] // 2
            x1, x2 = (x[..., :h], x[..., h:])
            return jnp.concatenate([-x2, x1], axis=-1)
        B, T, C = q.shape
        hd = C // N_HEADS
        g = N_HEADS // N_KV_HEADS
        q = _rms_norm(q, q_norm_w)
        k = _rms_norm(k, k_norm_w)
        q = q.reshape(B, T, N_HEADS, hd).transpose(0, 2, 1, 3)
        k = k.reshape(B, T, N_KV_HEADS, hd).transpose(0, 2, 1, 3)
        v = v.reshape(B, T, N_KV_HEADS, hd).transpose(0, 2, 1, 3)
        sin, cos = _rope_sin_cos(T, hd, q.dtype)
        q = q * cos + _rotate_half(q) * sin
        k = k * cos + _rotate_half(k) * sin
        qg = q.reshape(B, N_KV_HEADS, g, T, hd)
        scale = 1.0 / jnp.sqrt(jnp.asarray(hd, q.dtype))
        scores = jnp.einsum('bgnqd,bgkd->bgnqk', qg, k) * scale
        causal = jnp.tril(jnp.ones((T, T), bool))
        scores = jnp.where(causal, scores, jnp.asarray(-1e+30, scores.dtype))
        attn = jax.nn.softmax(scores, axis=-1)
        out = jnp.einsum('bgnqk,bgkd->bgnqd', attn, v)
        out = out.reshape(B, N_HEADS, T, hd).transpose(0, 2, 1, 3).reshape(B, T, C)
        return out @ w_out.T

    def _L0_ffn_ref(x, W_router, W_gate, W_up, W_down, sA_gate, sB_gate, sA_up, sB_up, sA_down, sB_down, A_gate, B_gate, A_up, B_up, A_down, B_down, expert_bias):
        import jax, jax.numpy as jnp
        import numpy as np
        B, L, D = (2, 256, 512)
        E, TOP_K, RANK, DFF = (8, 2, 8, 1376)

        def _lora(x, A, Bm, scale):
            return x @ A @ Bm * scale

        def _expert_lora(x, A, Bm, w, scale):
            xA = jnp.einsum('bld,edr->bler', x, A)
            xAB = jnp.einsum('bler,erd->bled', xA, Bm) * scale
            return (xAB * w).sum(axis=2)
        scale = 1.0 / RANK
        logits = x @ W_router
        scores = jax.nn.sigmoid(logits)
        biased = scores + expert_bias
        _, topk_idx = jax.lax.top_k(biased, TOP_K)
        topk_scores = jnp.take_along_axis(scores, topk_idx, axis=-1)
        topk_w = topk_scores / (topk_scores.sum(-1, keepdims=True) + 1e-08)
        one_hot = jax.nn.one_hot(topk_idx, E, dtype=x.dtype)
        expert_weights = (one_hot * topk_w[..., None]).sum(axis=2)
        w = expert_weights[..., None]
        gate = x @ W_gate + _lora(x, sA_gate, sB_gate, scale) + _expert_lora(x, A_gate, B_gate, w, scale)
        up = x @ W_up + _lora(x, sA_up, sB_up, scale) + _expert_lora(x, A_up, B_up, w, scale)
        hidden = jax.nn.silu(gate) * up
        out = hidden @ W_down + _lora(hidden, sA_down, sB_down, scale) + _expert_lora(hidden, A_down, B_down, w, scale)
        return out

    def _L1_xattn_ref(p, k_v, W_k, b_k, ln_gamma, ln_beta):
        import jax, jax.numpy as jnp
        import numpy as np
        EPS = 1e-06
        IMAGE_DIMS = 512
        kv = k_v @ W_k.T + b_k
        out = jnp.einsum('bij,bjd->bid', p, kv)
        scale = IMAGE_DIMS ** (-0.5)
        sim = jnp.einsum('bid,bjd->bij', out, kv) * scale
        mu = jnp.mean(sim, axis=-1, keepdims=True)
        var = jnp.var(sim, axis=-1, keepdims=True)
        sim = (sim - mu) * jax.lax.rsqrt(var + EPS) * ln_gamma + ln_beta
        attn = jax.nn.softmax(sim, axis=-1)
        return attn

    def _L1_ffn_ref(hidden_states, router_w, w_gate, w_up, w_down):
        import jax, jax.numpy as jnp
        import numpy as np
        B, S, H = (2, 256, 512)
        E, K, F = (64, 8, 192)
        CAP = 128
        b, s, h = hidden_states.shape
        T = b * s
        xf = hidden_states.reshape(T, h)
        logits = xf @ router_w.T
        scores = jax.nn.softmax(logits.astype(jnp.float32), axis=-1)
        topk_w, topk_idx = jax.lax.top_k(scores, K)
        topk_w = topk_w / (topk_w.sum(axis=-1, keepdims=True) + 1e-20)
        slot_expert = topk_idx.reshape(-1)
        slot_token = jnp.repeat(jnp.arange(T), K)
        onehot = jax.nn.one_hot(slot_expert, E, dtype=jnp.int32)
        pos = (jnp.cumsum(onehot, axis=0) * onehot).sum(-1) - 1
        valid = pos < CAP
        dest = jnp.where(valid, slot_expert * CAP + pos, E * CAP)
        buf = jnp.zeros((E * CAP + 1, h), xf.dtype).at[dest].set(xf[slot_token])
        xb = buf[:E * CAP].reshape(E, CAP, h)
        gate = jnp.einsum('ech,ehf->ecf', xb, w_gate)
        up = jnp.einsum('ech,ehf->ecf', xb, w_up)
        hmid = jax.nn.silu(gate) * up
        yb = jnp.einsum('ecf,efh->ech', hmid, w_down).reshape(E * CAP, h)
        yb = jnp.concatenate([yb, jnp.zeros((1, h), yb.dtype)], axis=0)
        slot_out = yb[dest] * topk_w.reshape(-1)[:, None].astype(yb.dtype)
        out = jnp.zeros((T, h), yb.dtype).at[slot_token].add(slot_out)
        return out.reshape(b, s, h)
    x = x + _L0_xattn_ref(_layernorm(x, axis=-1), ctx_512, ctx_512, L0_xattn_q_norm_w, L0_xattn_k_norm_w, L0_xattn_w_out)
    x = x + _L0_ffn_ref(_layernorm(x, axis=-1), L0_ffn_W_router, L0_ffn_W_gate, L0_ffn_W_up, L0_ffn_W_down, L0_ffn_sA_gate, L0_ffn_sB_gate, L0_ffn_sA_up, L0_ffn_sB_up, L0_ffn_sA_down, L0_ffn_sB_down, L0_ffn_A_gate, L0_ffn_B_gate, L0_ffn_A_up, L0_ffn_B_up, L0_ffn_A_down, L0_ffn_B_down, L0_ffn_expert_bias)
    x = x + _L1_xattn_ref(_layernorm(x, axis=-1), ctx_512, L1_xattn_W_k, L1_xattn_b_k, L1_xattn_ln_gamma, L1_xattn_ln_beta)
    x = x + _L1_ffn_ref(_layernorm(x, axis=-1), L1_ffn_router_w, L1_ffn_w_gate, L1_ffn_w_up, L1_ffn_w_down)
    return x

_drawn_inputs = setup_inputs


def setup_inputs(seed=0):
    import zlib

    import numpy as np

    out = dict(_drawn_inputs(seed))
    spreads = {'L0_xattn_q_norm_w': (1.0, 0.2),
     'L0_xattn_k_norm_w': (1.0, 0.2),
     'L0_ffn_expert_bias': (0.0, 0.8),
     'L1_xattn_b_k': (0.0, 0.8),
     'L1_xattn_ln_gamma': (1.0, 0.6),
     'L1_xattn_ln_beta': (0.0, 0.8)}
    factors = {'L0_ffn_W_router': 6.946,
     'L0_ffn_sA_gate': 7.121,
     'L0_ffn_sB_gate': 7.737,
     'L0_ffn_sA_up': 7.365,
     'L0_ffn_sB_up': 7.389,
     'L0_ffn_sA_down': 8.0,
     'L0_ffn_sB_down': 7.377,
     'L0_ffn_A_gate': 7.261,
     'L0_ffn_B_gate': 6.292,
     'L0_ffn_A_up': 7.283,
     'L0_ffn_B_up': 6.488,
     'L0_ffn_A_down': 8.0,
     'L0_ffn_B_down': 8.0,
     'L1_xattn_W_k': 8.0}
    for name, (base, spread) in spreads.items():
        noise = np.random.default_rng([zlib.crc32(name.encode()), seed]).standard_normal(out[name].shape)
        drawn = base * np.exp(spread * noise) if base else spread * noise
        out[name] = jnp.asarray(drawn.astype(out[name].dtype))
    for name, factor in factors.items():
        out[name] = (out[name] * factor).astype(out[name].dtype)
    return out
```

```python
import concourse.bass as bass
from concourse import mybir

F32 = mybir.dt.float32
F32R = mybir.dt.float32r
BF16 = mybir.dt.bfloat16
U32 = mybir.dt.uint32
ALU = mybir.AluOpType
ACT = mybir.ActivationFunctionType
AX = mybir.AxisListType.X

P = 128
B, T, C = 4, 512, 512
NT = T // P
KC = C // P
H, G = 16, 4
HPG = H // G
HD = C // H
CKV = G * HD
ROT = HD // 2
E0, R0 = 8, 8
LR = R0 * (E0 + 1)
DFF = 1376
NF = -(-DFF // P)
PJ = E0 + 2 * LR
WG, WU, WD = 0, P, KC * 2 * P
WBG, WBU, WAD = WD + C, WD + C + P, WD + C + 2 * P
WCOLS = WAD + LR
E1, K1, F1, CAP = 64, 8, 192, 128
FH = F1 // 2
NTOK = B * T
ROWS = NTOK + P
HROW = C + E1
EPS_LN, EPS_RMS, EPS_SIM = 1e-5, 1e-5, 1e-6


class Chain:

    def __init__(self, engine, sem, per, base=0):
        self.engine, self.sem, self.per, self.base, self.n = engine, sem, per, base, 0

    def __call__(self, instruction):
        self.n += 1
        instruction.then_inc(self.sem, 1)
        self.engine.wait_ge(self.sem, self.base + self.n)

    def end(self):
        assert self.n == self.per, (self.sem, self.n, self.per)


def build(nc, x, ctx_in, w, out, hx):
    place = {"at": 16896}

    def sb(name, shape, dt=F32):
        size = 1
        for s in shape[1:]:
            size *= s
        size = -(-size * mybir.dt.size(dt) // 32) * 32
        t = nc.alloc_sbuf_tensor_at(name, shape, dt, offset=place["at"])
        place["at"] += size
        assert place["at"] <= 229344, (name, place["at"])
        return t

    def sem(name):
        return nc.alloc_semaphore(name)

    PS = nc.alloc_psum_tensor("PS", [P, 8 * 512], F32)

    def bank(i, a=0, b=512, parts=P):
        return PS[0:parts, i * 512 + a:i * 512 + b]

    ident = sb("ident", [P, P])
    identb = sb("identb", [P, P], BF16)
    mask_qk = sb("mask_qk", [P, P], BF16)
    mask_kq = sb("mask_kq", [P, P], BF16)
    zrow = sb("zrow", [1, 512], BF16)
    iota8 = sb("iota8", [P, E0])
    dummy = sb("dummy", [P, 1])
    revt = sb("revt", [E1, NTOK])
    KEY = sb("KEY", [E1, NTOK])
    mhalf = sb("mhalf", [P, 8])
    IDX = sb("IDX", [P, E1], U32)
    part3_base = place["at"]
    blockmask = sb("blockmask", [P, NT, P])
    sel = sb("sel", [P, HPG, P], F32R)
    cosw = sb("cosw", [P, NT, C])
    sinw = sb("sinw", [P, NT, C])
    cosk = sb("cosk", [P, NT, CKV])
    sink = sb("sink", [P, NT, CKV])
    woH = sb("woH", [P, KC, C], F32R)
    woL = sb("woL", [P, KC, C], F32R)
    acH = sb("acH", [P, KC, PJ], F32R)
    acL = sb("acL", [P, KC, PJ], F32R)
    bdH = sb("bdH", [LR, C], F32R)
    bdL = sb("bdL", [LR, C], F32R)
    wk = sb("wk", [CKV, CKV])
    bk_col = sb("bk_col", [P, 1])
    bk_row = sb("bk_row", [P, CKV])
    gam = sb("gam", [P, T])
    bet = sb("bet", [P, T])
    ebias = sb("ebias", [P, E0])
    rw = sb("rw", [P, KC, E1])
    X = sb("X", [P, NT, C])
    XIN = sb("XIN", [P, NT, C])
    CTX = sb("CTX", [P, NT, CKV])
    KVT = sb("KVT", [P, T])
    KV = sb("KV", [P, NT, CKV])
    ST6 = sb("ST6", [P, NT, 6])
    MV = sb("MV", [P, NT, 2])
    CST6 = sb("CST6", [P, NT, 6])
    CMV = sb("CMV", [P, NT, 2])
    sm = [sb(f"sm{i}", [P, NT]) for i in range(6)]
    XN = sb("XN", [P, NT, C])
    region = place["at"]
    QR = sb("QR", [P, NT, C])
    KR = sb("KR", [P, NT, CKV])
    KS = sb("KS", [P, NT, P])
    QS = [sb(f"QS{n}", [P, NT, P]) for n in range(HPG)]
    KST = sb("KST", [P, T], F32R)
    QST = [sb(f"QST{n}", [P, T], F32R) for n in range(HPG)]
    V5 = sb("V5", [P, NT, HD + 1])
    NM = sb("NM", [P, NT * HPG])
    NM2 = sb("NM2", [P, P])
    RM = sb("RM", [P, T], F32R)
    RD = sb("RD", [P, 2, 8])
    PT = sb("PT", [P, 10, P * HPG])
    O = sb("O", [P, NT, C])
    pt_at = [0, 4, 7, 9]

    def PTj(j):
        return PT[:, pt_at[j]:pt_at[j] + NT - j, :].rearrange("p a b -> p (a b)").rearrange(
            "p (n q) -> p n q", n=HPG)

    QA = PT[:, 0:4, :]
    QB = PT[:, 4:8, :]
    attn_end = place["at"]
    place["at"] = region
    OTH = sb("OTH", [P, KC, T], F32R)
    OTL = sb("OTL", [P, KC, T], F32R)
    assert place["at"] <= attn_end - 28672 - 4096
    place["at"] = region
    XTH = sb("XTH", [P, KC, T], F32R)
    XTL = sb("XTL", [P, KC, T], F32R)
    WRAW = [sb(f"WRAW{s}", [P, WCOLS]) for s in range(2)]
    WHI = [sb(f"WHI{s}", [P, WCOLS], F32R) for s in range(2)]
    WLO = [sb(f"WLO{s}", [P, WCOLS], F32R) for s in range(2)]
    SIL = sb("SIL", [P, T])
    HID = sb("HID", [P, T])
    HH = [sb(f"HH{s}", [P, T], F32R) for s in range(2)]
    HL = [sb(f"HL{s}", [P, T], F32R) for s in range(2)]
    PA = sb("PA", [P, NT, PJ])
    LG = sb("LG", [P, NT, 2, LR])
    LXH = sb("LXH", [LR, 2, T], F32R)
    LXL = sb("LXL", [LR, 2, T], F32R)
    LDH = sb("LDH", [LR, T], F32R)
    LDL = sb("LDL", [LR, T], F32R)
    r8 = [sb(f"r8_{i}", [P, NT, E0]) for i in range(4)]
    top2 = sb("top2", [P, NT, 8])
    top2i = sb("top2i", [P, NT, 8], U32)
    top2f = sb("top2f", [P, NT, 8])
    WX = sb("WX", [P, NT, LR])
    place["at"] = region + 2 * KC * T * 4
    XTF = sb("XTF", [P, KC, T])
    OT1 = sb("OT1", [P, T])
    Y = sb("Y", [P, NT, T])
    HN = sb("HN", [P, NT, HROW])
    SC = sb("SC", [P, NT, E1])
    SR = sb("SR", [P, NT, E1])
    MK = sb("MK", [P, NT, E1])
    t8 = sb("t8", [P, NT, 8])
    nmx = sb("nmx", [P, NT])
    ssum = sb("ssum", [P, NT])
    place["at"] = region
    wq_bc = sb("wq_bc", [P, C])
    wkn_bc = sb("wkn_bc", [P, CKV])
    cq = sb("cq", [P, NT, HD])
    sq = sb("sq", [P, NT, HD])
    ck = sb("ck", [P, NT, HD])
    sk = sb("sk", [P, NT, HD])
    wo_raw = sb("wo_raw", [P, KC, C])
    ac_raw = sb("ac_raw", [P, KC, PJ])
    bd_raw = sb("bd_raw", [LR, C])
    sel_raw = sb("sel_raw", [P, HPG, P])
    ZR = sb("ZR", [P, HROW])

    def rows(ap, n):
        return ap.rearrange("(t p) c -> p t c", p=P)

    def bcast(ap, n):
        return ap.rearrange("(a n) -> a n", a=1).broadcast_to([P, n])

    names = ("x_loaded ctx_loaded end_sp end_pool end_act end_dve end_pe alone_dve alone_pool alone_pe alone_sp "
             "qab_ready q_ready k_pre norm_in norm_out ctxT_ps ctxT_sb kv_ps kv_act kv_dve "
             "stack_ready stack_T stack_sb_a stack_sb_d v_ready s_ps s_max nm_ready mt_ps rm_ready "
             "st_ps pt_ready pv_ps o_ready "
             "oT_ps oT_hi oT_lo op_ps x1_ready "
             "xn_ready xT_ps xT_hi xT_lo pj_ps pa_ready sig_ready lg_ready lx_ps lx_hi lx_lo "
             "w_hi w_lo gate_ps up_ps sil_ready hid_ready hh_ready hl_ready dn_ps ha_ps "
             "ld_ready ld_ps ld_hi ld_lo ffn_ps x2_ready "
             "xn3_ready xT3_ps xT3_sb o1_ps o1_sb sim_ps y_ready e_ready x3_ready "
             "xn4_ready xT4_ps xT4_sb lgt_ps lgt_max lgt_exp mk_ready mk_ps key_ready "
             "hx_stored out_stored dve_step pool_step g_dve g_pool").split()
    S = {n: sem(n) for n in names}
    w_loaded = [sem("w_loaded0"), sem("w_loaded1")]
    M = {n: sem("m_" + n) for n in ("idx xgt_ps xgt_sb gu_ps sil wc hm hmt_ps hmt_sb y_ps y_sb added".split())}
    scattered = sem("scattered")
    setup_loaded, setup_dve, setup_act, dummy_rows = (sem(n) for n in (
        "setup_loaded", "setup_dve", "setup_act", "dummy_rows"))
    n_loads = [0]
    with nc.Block() as block:
        @block.sync
        def _(sp):
            loads = [(ident, w["ident"]), (identb, w["identb"]), (mask_qk, w["mask_qk"]),
                     (mask_kq, w["mask_kq"]), (iota8, w["iota8"]), (dummy, w["dummy"]),
                     (revt, w["revt"]), (blockmask, w["blockmask"]), (sel_raw, w["sel"]),
                     (cq, w["cos_q"]), (sq, w["sin_q"]), (ck, w["cos_k"]), (sk, w["sin_k"]),
                     (wo_raw, w["wo"]), (ac_raw, w["acat"]), (bd_raw, w["bdown"]),
                     (wk, w["wk"]), (rw, w["rw"])]
            for dst, src in loads:
                n = len(src.shape)
                sp.dma_start(dst[(slice(None),) * n], src).then_inc(setup_loaded, 16)
            sp.dma_start(bk_col[:, :], w["bk"].rearrange("(p a) -> p a", a=1)).then_inc(setup_loaded, 16)
            for dst, src, n in ((bk_row, w["bk"], CKV), (gam, w["gamma"], T), (bet, w["beta"], T),
                                (ebias, w["ebias"], E0), (wq_bc, w["wq"], C), (wkn_bc, w["wkn"], CKV)):
                sp.dma_start(dst[:, :], bcast(src, n)).then_inc(setup_loaded, 16)
            n_loads[0] = len(loads) + 7
            sp.wait_ge(setup_dve, 3)
            sp.dma_start(hx[NTOK:ROWS, :], ZR[:, :]).then_inc(dummy_rows, 16)
            sp.dma_start(out[NTOK:ROWS, :], ZR[:, 0:C]).then_inc(dummy_rows, 16)
            sp.wait_ge(dummy_rows, 32)

        @block.vector
        def _(dve):
            step = Chain(dve, setup_dve, None)
            step(dve.memset(ZR[:, :], 0.0))
            step(dve.memset(zrow[:, :], 0.0))
            step(dve.memset(mhalf[:, :], -0.5))
            dve.wait_ge(setup_loaded, 16 * n_loads[0])
            for t in range(NT):
                for tab_c, tab_s, wt, c_, s_, nh in ((cosw, sinw, wq_bc, cq, sq, H),
                                                     (cosk, sink, wkn_bc, ck, sk, G)):
                    def heads(ap, a, b):
                        return ap.rearrange("p (h d) -> p h d", h=nh)[:, :, a:b]

                    def table(ap, a, b):
                        return ap[:, t, a:b].unsqueeze(1).broadcast_to([P, nh, b - a])
                    step(dve.tensor_tensor(heads(tab_c[:, t, :], 0, HD), heads(wt[:, :], 0, HD),
                                           table(c_, 0, HD), ALU.mult))
                    step(dve.tensor_tensor(heads(tab_s[:, t, :], 0, ROT), heads(wt[:, :], ROT, HD),
                                           table(s_, 0, ROT), ALU.mult))
                    step(dve.tensor_tensor(heads(tab_s[:, t, :], ROT, HD), heads(wt[:, :], 0, ROT),
                                           table(s_, ROT, HD), ALU.mult))
            dve.wait_ge(setup_act, 4)
            step(dve.tensor_tensor(woL[:, :, :], wo_raw[:, :, :], woH[:, :, :], ALU.subtract))
            step(dve.tensor_tensor(acL[:, :, :], ac_raw[:, :, :], acH[:, :, :], ALU.subtract))
            step(dve.tensor_tensor(bdL[:, :], bd_raw[:, :], bdH[:, :], ALU.subtract))

        @block.gpsimd
        def _(pool):
            for name in S:
                if name not in BY_DMA:
                    pool.sem_inc(S[name], 1)
            for name in M:
                pool.sem_inc(M[name], 1)

        @block.scalar
        def _(act):
            act.wait_ge(setup_loaded, 16 * n_loads[0])
            for dst, src in ((woH, wo_raw), (acH, ac_raw), (sel, sel_raw)):
                act.activation(dst[:, :, :], src[:, :, :], ACT.Copy).then_inc(setup_act, 1)
            act.activation(bdH[:, :], bd_raw[:, :], ACT.Copy).then_inc(setup_act, 1)

    DVE_B, POOL_B, ACT_B, DVE_G, POOL_G = KSTEPS["dve"], KSTEPS["pool"], KSTEPS["act"], KSTEPS["g_dve"], KSTEPS["g_pool"]

    def batch_start(engine, b):
        for name in ("end_sp", "end_pool", "end_act", "end_dve", "end_pe"):
            engine.wait_ge(S[name], 1 + b)

    def alone(engine, name):
        engine.sem_inc(S["alone_" + name], 1)

    with nc.Block() as block:
        @block.sync
        def _(sp):
            with sp.Fori(0, B) as b:
                batch_start(sp, b)
                alone(sp, "sp")
                sp.dma_start(CTX[:, :, :], rows(ctx_in[bass.ds(b * T, T), :], NT)).then_inc(S["ctx_loaded"], 16)
                sp.dma_start(XIN[:, :, :], rows(x[bass.ds(b * T, T), :], NT)).then_inc(S["x_loaded"], 16)
                sp.wait_ge(S["x1_ready"], 1 + NT * (b + 1))

                def load_w(f, slot):
                    sp.wait_ge(S["w_hi"], 1 + b * NF + f - 1)
                    sp.wait_ge(S["w_lo"], 1 + b * NF + f - 1)
                    alone(sp, "sp")
                    sp.dma_start(WRAW[slot][:, :], w["ffn"][bass.ds(f * P, P), :]).then_inc(w_loaded[slot], 16)
                sp.dma_start(WRAW[0][:, :], w["ffn"][0:P, :]).then_inc(w_loaded[0], 16)
                sp.dma_start(WRAW[1][:, :], w["ffn"][P:2 * P, :]).then_inc(w_loaded[1], 16)
                with sp.Fori(1, NF // 2) as i:
                    load_w(2 * i, 0)
                    load_w(2 * i + 1, 1)
                load_w(NF - 1, 0)
                sp.wait_ge(S["key_ready"], 1 + b + 1)
                alone(sp, "sp")
                sp.dma_start(rows(hx[bass.ds(b * T, T), :], NT), HN[:, :, :]).then_inc(S["hx_stored"], 16)
                sp.dma_start(rows(out[bass.ds(b * T, T), :], NT), X[:, :, :]).then_inc(S["out_stored"], 16)
                sp.wait_ge(S["hx_stored"], 16 * (b + 1))
                sp.wait_ge(S["out_stored"], 16 * (b + 1))
                sp.sem_inc(S["end_sp"], 1)

        @block.gpsimd
        def _(pool):
            step = Chain(pool, S["pool_step"], POOL_B)
            with pool.Fori(0, B) as b:
                step.base, step.n = b * POOL_B, 0
                batch_start(pool, b)

                def power(i, n):
                    pool.wait_ge(S["norm_in"], 1 + 7 * b + n)
                    pool.tensor_tensor(sm[1][:, :], sm[0][:, :], mhalf[:, 0:NT], ALU.pow).then_inc(S["norm_out"], 1)
                for n in range(1, 4):
                    power(0, n)
                for t in range(NT):
                    pool.wait_ge(S["qab_ready"], 1 + NT * b + t + 1)
                    pool.tensor_tensor(QR[:, t, :], QA[:, t, :], QB[:, t, :], ALU.add).then_inc(S["q_ready"], 1)
                pool.wait_ge(S["q_ready"], 1 + NT * (b + 1))
                pool.wait_ge(S["k_pre"], 1 + b + 1)
                gstep = Chain(pool, S["g_pool"], POOL_G)
                alone(pool, "pool")
                with pool.Fori(0, G) as g:
                    gi = b * G + g
                    gstep.base, gstep.n = gi * POOL_G, 0
                    pool.wait_ge(S["stack_T"], 1 + 5 * gi)
                    kin = KR[:, :, bass.ds(g * HD, HD)].unsqueeze(2).broadcast_to([P, NT, 2, HD])
                    ks = KS[:, :, :].rearrange("p t (r s d) -> p t r s d", r=2, s=2)
                    alone(pool, "pool")
                    gstep(pool.tensor_copy(ks[:, :, :, 0, :].bitcast(F32R), kin))
                    alone(pool, "pool")
                    pool.tensor_tensor(ks[:, :, :, 1, :], kin, ks[:, :, :, 0, :], ALU.subtract).then_inc(S["stack_ready"], 1)
                    for n in range(HPG):
                        qin = QR[:, :, bass.ds(g * P + n * HD, HD)].unsqueeze(2).broadcast_to([P, NT, 2, HD])
                        qs = QS[n][:, :, :].rearrange("p t (s r d) -> p t s r d", r=2, s=2)
                        gstep(pool.tensor_copy(qs[:, :, 0, :, :].bitcast(F32R), qin))
                        alone(pool, "pool")
                        pool.tensor_tensor(qs[:, :, 1, :, :], qin, qs[:, :, 0, :, :], ALU.subtract).then_inc(S["stack_ready"], 1)
                    pool.wait_ge(S["pv_ps"], 1 + 2 * gi)
                    alone(pool, "pool")
                    gstep(pool.memset(V5[:, :, HD:HD + 1], 1.0))
                    alone(pool, "pool")
                    pool.tensor_copy(V5[:, :, 0:HD], CTX[:, :, bass.ds(g * HD, HD)]).then_inc(S["v_ready"], 1)
                gstep.end()
                pool.wait_ge(S["v_ready"], 1 + G * (b + 1))
                power(0, 4)
                def hidden(f, slot):
                    pool.wait_ge(S["hid_ready"], 1 + b * NF + f + 1)
                    pool.wait_ge(S["dn_ps"], 1 + b * NF + f - 1)
                    hid_split(slot)

                def hid_split(slot):
                    alone(pool, "pool")
                    pool.tensor_copy(HH[slot][:, :], HID[:, :]).then_inc(S["hh_ready"], 1)

                def hidden_tail(f, slot):
                    pool.wait_ge(S["hh_ready"], 1 + b * NF + f + 1)
                    pool.tensor_tensor(HL[slot][:, :], HID[:, :], HH[slot][:, :], ALU.subtract).then_inc(S["hl_ready"], 1)
                pool.wait_ge(S["hid_ready"], 1 + b * NF + 1)
                pool.wait_ge(S["dn_ps"], 1 + b * NF)
                hid_split(0)
                hidden_tail(0, 0)
                alone(pool, "pool")
                with pool.Fori(0, NF // 2) as i:
                    for d in (1, 2):
                        hidden(2 * i + d, d % 2)
                        hidden_tail(2 * i + d, d % 2)
                power(0, 5)
                power(0, 6)
                power(0, 7)
                pool.wait_ge(S["norm_out"], 1 + 7 * (b + 1))
                pool.sem_inc(S["end_pool"], 1)

        @block.scalar
        def _(act):
            with act.Fori(0, B) as b:
                batch_start(act, b)
                act.wait_ge(S["ctxT_ps"], 1 + b + 1)
                act.activation(XN[:, 0, :], bank(0), ACT.Copy).then_inc(S["ctxT_sb"], 1)
                act.wait_ge(S["kv_ps"], 1 + b + 1)
                act.activation(KVT[:, :], bank(1), ACT.Identity, bias=bk_col[:, 0:1]).then_inc(S["kv_act"], 1)
                with act.Fori(0, G) as g:
                    gi = b * G + g
                    for i, (item, dst) in enumerate(((0, KST), (1, QST[0]), (3, QST[2]))):
                        act.wait_ge(S["stack_T"], 1 + 5 * gi + item + 1)
                        act.activation(dst[:, :], bank(item), ACT.Copy).then_inc(S["stack_sb_a"], 1)
                    for j in range(NT):
                        act.wait_ge(S["st_ps"], 1 + NT * gi + j + 1)
                        n = (NT - j) * P
                        if j == 0:
                            src = PS[:, 4 * 512:8 * 512].rearrange("p (n q) -> p n q", n=HPG)
                        elif j == 1:
                            src = PS[:, 0:4 * 512].rearrange("p (n q) -> p n q", n=HPG)[:, :, 0:n]
                        elif j == 2:
                            src = PS[:, 4 * 512:6 * 512].rearrange("p (n q) -> p n q", n=HPG)
                        else:
                            src = bank(6).rearrange("p (n q) -> p n q", n=HPG)
                        act.activation(PTj(j), src, ACT.Exp).then_inc(S["pt_ready"], 1)
                for t in range(NT):
                    act.wait_ge(S["oT_ps"], 1 + NT * b + t + 1)
                    act.activation(OTH[:, :, t * P:(t + 1) * P], bank(t).rearrange("p (k q) -> p k q", k=KC),
                                   ACT.Copy).then_inc(S["oT_hi"], 1)
                act.wait_ge(S["op_ps"], 1 + NT * (b + 1))
                for t in range(NT):
                    act.wait_ge(S["xT_ps"], 1 + NT * b + t + 1)
                    act.activation(XTH[:, :, t * P:(t + 1) * P], bank(t).rearrange("p (k q) -> p k q", k=KC),
                                   ACT.Copy).then_inc(S["xT_hi"], 1)
                act.wait_ge(S["pa_ready"], 1 + b + 1)
                act.activation(r8[0][:, :, :], PA[:, :, 0:E0], ACT.Exp, scale=-1.0).then_inc(S["sig_ready"], 1)

                def whi(f, slot, loads):
                    act.wait_ge(w_loaded[slot], 16 * loads)
                    act.activation(WHI[slot][:, :], WRAW[slot][:, :], ACT.Copy).then_inc(S["w_hi"], 1)
                N0, N1 = NF // 2 + 1, NF // 2
                whi(0, 0, b * N0 + 1)
                for h in range(2):
                    act.wait_ge(S["lx_ps"], 1 + 2 * b + h + 1)
                    act.activation(LXH[:, h, :], bank(6 + h, parts=LR), ACT.Copy).then_inc(S["lx_hi"], 1)
                whi(1, 1, b * N1 + 1)

                def silu(f):
                    act.wait_ge(S["gate_ps"], 1 + b * NF + f + 1)
                    act.wait_ge(S["hid_ready"], 1 + b * NF + f)
                    act.activation(SIL[:, :], bank(0), ACT.Silu).then_inc(S["sil_ready"], 1)
                silu(0)
                with act.Fori(0, NF // 2 - 1) as i:
                    for d in (1, 2):
                        act.wait_ge(S["dn_ps"], 1 + b * NF + 2 * i + d)
                        whi(None, (d + 1) % 2, (b * N0 + i + 2) if d == 1 else (b * N1 + i + 2))
                        silu(2 * i + d)
                act.wait_ge(S["dn_ps"], 1 + b * NF + NF - 2)
                whi(None, 0, (b + 1) * N0)
                silu(NF - 2)
                silu(NF - 1)
                act.wait_ge(S["ld_ps"], 1 + b + 1)
                act.activation(LDH[:, :], bank(3, parts=LR), ACT.Copy).then_inc(S["ld_hi"], 1)
                for t in range(NT):
                    act.wait_ge(S["xT3_ps"], 1 + NT * b + t + 1)
                    act.activation(XTF[:, :, t * P:(t + 1) * P], bank(t).rearrange("p (k q) -> p k q", k=KC),
                                   ACT.Copy).then_inc(S["xT3_sb"], 1)
                act.wait_ge(S["o1_ps"], 1 + b + 1)
                act.activation(OT1[:, :], bank(4), ACT.Copy, scale=float(C) ** -0.5).then_inc(S["o1_sb"], 1)
                for t in range(NT):
                    act.wait_ge(S["y_ready"], 1 + NT * b + t + 1)
                    act.activation(Y[:, t, :], Y[:, t, :], ACT.Exp, bias=nmx[:, t:t + 1],
                                   accum_out=ssum[:, t:t + 1]).then_inc(S["e_ready"], 1)
                for t in range(NT):
                    act.wait_ge(S["xT4_ps"], 1 + NT * b + t + 1)
                    act.activation(XTF[:, :, t * P:(t + 1) * P], bank(4 + t).rearrange("p (k q) -> p k q", k=KC),
                                   ACT.Copy).then_inc(S["xT4_sb"], 1)
                act.wait_ge(S["lgt_max"], 1 + b + 1)
                act.activation(SC[:, :, :], SC[:, :, :], ACT.Exp).then_inc(S["lgt_exp"], 1)
                act.wait_ge(S["lgt_exp"], 1 + b + 1)
                act.sem_inc(S["end_act"], 1)

        @block.vector
        def _(dve):
            step = Chain(dve, S["dve_step"], DVE_B)
            gstep = Chain(dve, S["g_dve"], DVE_G)
            with dve.Fori(0, B) as b:
                step.base, step.n = b * DVE_B, 0
                batch_start(dve, b)

                def sig(instruction, name, value):
                    instruction.then_inc(S[name], 1)
                    dve.wait_ge(S[name], 1 + value)
                norms = [0]

                def inverse_root():
                    norms[0] += 1
                    dve.wait_ge(S["norm_out"], 1 + 7 * b + norms[0])

                def stats(src, s6, mv):
                    for t in range(NT):
                        step(dve.bn_stats(s6[:, t, :], src[:, t, :]))
                        alone(dve, "dve")
                        step(dve.bn_aggr(mv[:, t, :], s6[:, t, :]))

                def layer_norm(src, dst, eps, ready):
                    stats(src, ST6, MV)
                    sig(dve.tensor_scalar(sm[0][:, :], MV[:, :, 1], eps, None, ALU.add), "norm_in", 7 * b + norms[0] + 1)
                    inverse_root()
                    for t in range(NT):
                        sig(dve.tensor_scalar(dst[:, t, 0:C], src[:, t, :], MV[:, t, 0:1], sm[1][:, t:t + 1],
                                              ALU.subtract, ALU.mult), ready, NT * b + t + 1)

                dve.wait_ge(S["ctx_loaded"], 16 * (b + 1))
                stats(CTX, CST6, CMV)
                step(dve.tensor_tensor(sm[2][:, :], CMV[:, :, 0], CMV[:, :, 0], ALU.mult))
                step(dve.tensor_tensor(sm[2][:, :], sm[2][:, :], CMV[:, :, 1], ALU.add))
                sig(dve.tensor_scalar(sm[0][:, :], sm[2][:, :], EPS_RMS, None, ALU.add), "norm_in", 7 * b + 1)
                inverse_root()
                step(dve.tensor_copy(sm[4][:, :], sm[1][:, :]))
                dve.wait_ge(S["x_loaded"], 16 * (b + 1))
                stats(XIN, ST6, MV)
                sig(dve.tensor_scalar(sm[0][:, :], MV[:, :, 1], EPS_LN, None, ALU.add), "norm_in", 7 * b + 2)
                inverse_root()
                step(dve.tensor_copy(sm[2][:, :], sm[1][:, :]))
                step(dve.tensor_tensor(sm[3][:, :], sm[2][:, :], sm[2][:, :], ALU.mult))
                step(dve.tensor_tensor(sm[3][:, :], sm[3][:, :], MV[:, :, 1], ALU.mult))
                sig(dve.tensor_scalar(sm[0][:, :], sm[3][:, :], EPS_RMS, None, ALU.add), "norm_in", 7 * b + 3)
                inverse_root()
                step(dve.tensor_tensor(sm[3][:, :], sm[2][:, :], sm[1][:, :], ALU.mult))

                def rotary(xm, qa, qb, tab_c, tab_s, nh, last):
                    hv = lambda ap, a, z: ap.rearrange("p (h d) -> p h d", h=nh)[:, :, a:z]
                    step(dve.tensor_tensor(qa, xm, tab_c, ALU.mult))
                    step(dve.tensor_tensor(hv(qb, 0, ROT), hv(xm, ROT, HD), hv(tab_s, 0, ROT), ALU.mult))
                    last(dve.tensor_tensor(hv(qb, ROT, HD), hv(xm, 0, ROT), hv(tab_s, ROT, HD), ALU.mult))
                dve.wait_ge(S["kv_ps"], 1 + b + 1)
                for t in range(NT):
                    step(dve.tensor_scalar(XN[:, t, :], XIN[:, t, :], MV[:, t, 0:1], sm[3][:, t:t + 1],
                                           ALU.subtract, ALU.mult))
                    rotary(XN[:, t, :], QA[:, t, :], QB[:, t, :], cosw[:, t, :], sinw[:, t, :], H,
                           lambda ins: sig(ins, "qab_ready", NT * b + t + 1))
                dve.wait_ge(S["q_ready"], 1 + NT * (b + 1))
                for t in range(NT):
                    step(dve.tensor_scalar(XN[:, t, 0:CKV], CTX[:, t, :], sm[4][:, t:t + 1], None, ALU.mult))
                    rotary(XN[:, t, 0:CKV], QA[:, t, 0:CKV], QB[:, t, 0:CKV], cosk[:, t, :], sink[:, t, :], G, step)
                sig(dve.tensor_tensor(KR[:, :, :], QA[:, :, 0:CKV], QB[:, :, 0:CKV], ALU.add), "k_pre", b + 1)
                dve.wait_ge(S["kv_ps"], 1 + b + 1)
                sig(dve.tensor_tensor(KV[:, :, :], bank(2).rearrange("p (t d) -> p t d", t=NT),
                                      bk_row[:, :].unsqueeze(1).broadcast_to([P, NT, CKV]), ALU.add),
                    "kv_dve", b + 1)
                step(dve.memset(NM2[:, :], 0.0))
                alone(dve, "dve")
                with dve.Fori(0, G) as g:
                    gi = b * G + g
                    gstep.base, gstep.n = gi * DVE_G, 0
                    for i, (item, dst) in enumerate(((2, QST[1]), (4, QST[3]))):
                        dve.wait_ge(S["stack_T"], 1 + 5 * gi + item + 1)
                        sig(dve.tensor_copy(dst[:, :], bank(item)), "stack_sb_d", 2 * gi + i + 1)
                    for i, (t, lo) in enumerate(((3, 0), (2, 4), (1, 0), (0, 2))):
                        dve.wait_ge(S["s_ps"], 1 + NT * gi + i + 1)
                        n = (t + 1) * P
                        if t >= 2:
                            src = PS[:, lo * 512:(lo + 4) * 512].rearrange("p (n k) -> p n k", n=HPG)[:, :, 0:n]
                        else:
                            src = PS[:, lo * 512:lo * 512 + HPG * n].rearrange("p (n k) -> p n k", n=HPG)
                        sig(dve.tensor_reduce(NM[:, t * HPG:(t + 1) * HPG], src, AX, ALU.max, negate=True),
                            "s_max", NT * gi + i + 1)
                    dve.wait_ge(S["mt_ps"], 1 + gi)
                    gstep(dve.tensor_copy(NM2[:, 0:16].bitcast(F32R), NM[:, :]))
                    sig(dve.tensor_tensor(NM2[:, 32:48], NM[:, :], NM2[:, 0:16], ALU.subtract), "nm_ready", gi + 1)
                    dve.wait_ge(S["mt_ps"], 1 + gi + 1)
                    sig(dve.tensor_tensor(RM[:, :].rearrange("p (t q) -> p t q", t=NT),
                                          bank(3, 0, P).unsqueeze(1).broadcast_to([P, NT, P]), blockmask[:, :, :],
                                          ALU.mult), "rm_ready", gi + 1)
                    for i, bk in enumerate((7, 0)):
                        dve.wait_ge(S["pv_ps"], 1 + 2 * gi + i + 1)
                        ov = bank(bk, 0, 8 * (HD + 1)).rearrange("p (m d) -> p m d", m=8)
                        gstep(dve.reciprocal(RD[:, i, :], ov[:, :, HD]))
                        for u in range(2):
                            t = 2 * i + u
                            ins = dve.tensor_tensor(
                                O[:, t, bass.ds(g * P, P)].rearrange("p (n d) -> p n d", n=HPG),
                                ov[:, u * HPG:(u + 1) * HPG, 0:HD],
                                RD[:, i, u * HPG:(u + 1) * HPG].unsqueeze(2).broadcast_to([P, HPG, HD]), ALU.mult)
                            if u == 0:
                                gstep(ins)
                            else:
                                sig(ins, "o_ready", 2 * gi + i + 1)
                gstep.end()
                for t in range(NT):
                    dve.wait_ge(S["oT_hi"], 1 + NT * b + t + 1)
                    sl = slice(t * P, (t + 1) * P)
                    sig(dve.tensor_tensor(OTL[:, :, sl], bank(t).rearrange("p (k q) -> p k q", k=KC),
                                          OTH[:, :, sl], ALU.subtract), "oT_lo", NT * b + t + 1)
                for t in range(NT):
                    dve.wait_ge(S["op_ps"], 1 + NT * b + t + 1)
                    sig(dve.tensor_tensor(X[:, t, :], bank(4 + t), XIN[:, t, :], ALU.add), "x1_ready", NT * b + t + 1)
                layer_norm(X, XN, EPS_LN, "xn_ready")
                for t in range(NT):
                    dve.wait_ge(S["xT_hi"], 1 + NT * b + t + 1)
                    sl = slice(t * P, (t + 1) * P)
                    sig(dve.tensor_tensor(XTL[:, :, sl], bank(t).rearrange("p (k q) -> p k q", k=KC),
                                          XTH[:, :, sl], ALU.subtract), "xT_lo", NT * b + t + 1)
                for i in range(2):
                    dve.wait_ge(S["pj_ps"], 1 + 2 * b + i + 1)
                    ins = dve.tensor_copy(PA[:, 2 * i:2 * i + 2, :],
                                          bank(4 + i).rearrange("p (t c) -> p t c", t=2)[:, :, 0:PJ])
                    if i == 0:
                        step(ins)
                    else:
                        sig(ins, "pa_ready", b + 1)
                dve.wait_ge(S["sig_ready"], 1 + b + 1)
                step(dve.tensor_scalar(r8[1][:, :, :], r8[0][:, :, :], 1.0, None, ALU.add))
                step(dve.reciprocal(r8[0][:, :, :], r8[1][:, :, :]))
                step(dve.tensor_tensor(r8[1][:, :, :], r8[0][:, :, :],
                                       ebias[:, :].unsqueeze(1).broadcast_to([P, NT, E0]), ALU.add))
                for t in range(NT):
                    alone(dve, "dve")
                    step(dve.max(top2[:, t, :], r8[1][:, t, :]))
                    alone(dve, "dve")
                    step(dve.max_index(top2i[:, t, :], top2[:, t, :], r8[1][:, t, :]))
                step(dve.tensor_copy(top2f[:, :, :], top2i[:, :, :]))
                for t in range(NT):
                    step(dve.tensor_scalar(r8[2][:, t, :], iota8[:, :], top2f[:, t, 0:1], None, ALU.is_equal))
                    step(dve.scalar_tensor_tensor(out=r8[3][:, t, :], in0=iota8[:, :], scalar=top2f[:, t, 1:2],
                                                  in1=r8[2][:, t, :], op0=ALU.is_equal, op1=ALU.add))
                step(dve.tensor_tensor(r8[2][:, :, :], r8[3][:, :, :], r8[0][:, :, :], ALU.mult))
                step(dve.tensor_reduce(sm[2][:, :], r8[2][:, :, :], AX, ALU.add))
                step(dve.tensor_scalar(sm[3][:, :], sm[2][:, :], 1e-8, None, ALU.add))
                step(dve.reciprocal(sm[2][:, :], sm[3][:, :]))
                step(dve.tensor_scalar(sm[3][:, :], sm[2][:, :], 1.0 / R0, None, ALU.mult))
                step(dve.tensor_tensor(r8[3][:, :, :], r8[2][:, :, :],
                                       sm[3][:, :].unsqueeze(2).broadcast_to([P, NT, E0]), ALU.mult))
                step(dve.memset(WX[:, :, 0:R0], 1.0 / R0))
                for t in range(NT):
                    step(dve.tensor_copy(WX[:, t, R0:LR].rearrange("p (e r) -> p e r", e=E0),
                                         r8[3][:, t, :].unsqueeze(2).broadcast_to([P, E0, R0])))
                for t in range(NT):
                    ins = dve.tensor_tensor(LG[:, t, :, :], PA[:, t, E0:PJ].rearrange("p (h r) -> p h r", h=2),
                                            WX[:, t, :].unsqueeze(1).broadcast_to([P, 2, LR]), ALU.mult)
                    if t < NT - 1:
                        step(ins)
                    else:
                        sig(ins, "lg_ready", b + 1)

                def wlo(n, slot):
                    dve.wait_ge(S["w_hi"], 1 + b * NF + n + 1)
                    sig(dve.tensor_tensor(WLO[slot][:, :], WRAW[slot][:, :], WHI[slot][:, :], ALU.subtract),
                        "w_lo", b * NF + n + 1)

                def hid(n):
                    dve.wait_ge(S["sil_ready"], 1 + b * NF + n + 1)
                    dve.wait_ge(S["up_ps"], 1 + b * NF + n + 1)
                    dve.wait_ge(S["hl_ready"], 1 + b * NF + n)
                    sig(dve.tensor_tensor(HID[:, :], SIL[:, :], bank(1), ALU.mult), "hid_ready", b * NF + n + 1)
                wlo(0, 0)
                for h in range(2):
                    dve.wait_ge(S["lx_hi"], 1 + 2 * b + h + 1)
                    sig(dve.tensor_tensor(LXL[:, h, :], bank(6 + h, parts=LR), LXH[:, h, :], ALU.subtract),
                        "lx_lo", 2 * b + h + 1)
                wlo(1, 1)
                hid(0)
                alone(dve, "dve")
                with dve.Fori(0, NF // 2 - 1) as i:
                    for d in (1, 2):
                        wlo(2 * i + d + 1, (d + 1) % 2)
                        hid(2 * i + d)
                wlo(NF - 1, 0)
                hid(NF - 2)
                hid(NF - 1)
                dve.wait_ge(S["ha_ps"], 1 + b + 1)
                sig(dve.tensor_tensor(LG[:, :, 0, :], bank(2, 0, NT * LR).rearrange("p (t r) -> p t r", t=NT),
                                      WX[:, :, :], ALU.mult), "ld_ready", b + 1)
                dve.wait_ge(S["ld_hi"], 1 + b + 1)
                sig(dve.tensor_tensor(LDL[:, :], bank(3, parts=LR), LDH[:, :], ALU.subtract), "ld_lo", b + 1)
                for t in range(NT):
                    dve.wait_ge(S["ffn_ps"], 1 + NT * b + t + 1)
                    sig(dve.tensor_tensor(X[:, t, :], bank(4 + t), X[:, t, :], ALU.add), "x2_ready", NT * b + t + 1)
                layer_norm(X, XN, EPS_LN, "xn3_ready")
                for t in range(NT):
                    dve.wait_ge(S["sim_ps"], 1 + NT * b + t + 1)
                    step(dve.bn_stats(ST6[:, t, :], bank(t)))
                    alone(dve, "dve")
                    step(dve.bn_aggr(MV[:, t, :], ST6[:, t, :]))
                sig(dve.tensor_scalar(sm[0][:, :], MV[:, :, 1], EPS_SIM, None, ALU.add), "norm_in", 7 * b + norms[0] + 1)
                inverse_root()
                for t in range(NT):
                    step(dve.tensor_scalar(Y[:, t, :], bank(t), MV[:, t, 0:1], sm[1][:, t:t + 1],
                                           ALU.subtract, ALU.mult))
                    step(dve.tensor_tensor(Y[:, t, :], Y[:, t, :], gam[:, :], ALU.mult))
                    step(dve.tensor_tensor(Y[:, t, :], Y[:, t, :], bet[:, :], ALU.add))
                    sig(dve.tensor_reduce(nmx[:, t:t + 1], Y[:, t, :], AX, ALU.max, negate=True),
                        "y_ready", NT * b + t + 1)
                for t in range(NT):
                    dve.wait_ge(S["e_ready"], 1 + NT * b + t + 1)
                    step(dve.reciprocal(sm[2][:, t:t + 1], ssum[:, t:t + 1]))
                    sig(dve.scalar_tensor_tensor(out=X[:, t, :], in0=Y[:, t, :], scalar=sm[2][:, t:t + 1],
                                                 in1=X[:, t, :], op0=ALU.mult, op1=ALU.add),
                        "x3_ready", NT * b + t + 1)
                layer_norm(X, HN, EPS_LN, "xn4_ready")
                dve.wait_ge(S["lgt_ps"], 1 + b + 1)
                lg = bank(0, 0, NT * E1).rearrange("p (t e) -> p t e", t=NT)
                step(dve.tensor_reduce(sm[2][:, :], lg, AX, ALU.max))
                sig(dve.tensor_tensor(SC[:, :, :], lg, sm[2][:, :].unsqueeze(2).broadcast_to([P, NT, E1]),
                                      ALU.subtract), "lgt_max", b + 1)
                dve.wait_ge(S["lgt_exp"], 1 + b + 1)
                step(dve.tensor_reduce(sm[2][:, :], SC[:, :, :], AX, ALU.add))
                step(dve.reciprocal(sm[3][:, :], sm[2][:, :]))
                step(dve.tensor_tensor(SC[:, :, :], SC[:, :, :], sm[3][:, :].unsqueeze(2).broadcast_to([P, NT, E1]),
                                       ALU.mult))
                for t in range(NT):
                    alone(dve, "dve")
                    step(dve.max(t8[:, t, :], SC[:, t, :]))
                    alone(dve, "dve")
                    step(dve.match_replace(SR[:, t, :], t8[:, t, :], SC[:, t, :], -1.0))
                sig(dve.tensor_scalar(MK[:, :, :], SR[:, :, :], 0.0, None, ALU.is_lt), "mk_ready", b + 1)
                step(dve.tensor_tensor(SR[:, :, :], MK[:, :, :], SC[:, :, :], ALU.mult))
                step(dve.tensor_reduce(sm[2][:, :], SR[:, :, :], AX, ALU.add))
                step(dve.tensor_scalar(sm[3][:, :], sm[2][:, :], 1e-20, None, ALU.add))
                step(dve.reciprocal(sm[2][:, :], sm[3][:, :]))
                step(dve.tensor_tensor(HN[:, :, C:HROW], SR[:, :, :],
                                       sm[2][:, :].unsqueeze(2).broadcast_to([P, NT, E1]), ALU.mult))
                dve.wait_ge(S["mk_ps"], 1 + b + 1)
                sig(dve.tensor_tensor(KEY[:, bass.ds(b * T, T)], bank(1, parts=E1), revt[:, bass.ds(b * T, T)],
                                      ALU.mult), "key_ready", b + 1)
                dve.sem_inc(S["end_dve"], 1)
            step.end()

        @block.tensor
        def _(pe):
            def three(dst, a, b_, first, last, **kw):
                pe.matmul(dst, a[0], b_[0], start=first, stop=False, **kw)
                pe.matmul(dst, a[0], b_[1], start=False, stop=False, **kw)
                return pe.matmul(dst, a[1], b_[0], start=False, stop=last, **kw)

            with pe.Fori(0, B) as b:
                batch_start(pe, b)
                pe.wait_ge(S["ctx_loaded"], 16 * (b + 1))
                for t in range(NT):
                    mm = pe.transpose(bank(0, t * P, (t + 1) * P), CTX[:, t, :], ident[:, :])
                mm.then_inc(S["ctxT_ps"], 1)
                pe.wait_ge(S["ctxT_sb"], 1 + b + 1)
                ctxT = XN[:, 0, :]
                pe.matmul(bank(1), wk[:, :], ctxT, start=True, stop=True)
                for t in range(NT):
                    mm = pe.matmul(bank(2, t * P, (t + 1) * P), ctxT[:, t * P:(t + 1) * P], wk[:, :],
                                   start=True, stop=True)
                mm.then_inc(S["kv_ps"], 1)
                pe.wait_ge(S["kv_act"], 1 + b + 1)
                pe.wait_ge(S["kv_dve"], 1 + b + 1)
                alone(pe, "pe")
                with pe.Fori(0, G) as g:
                    gi = b * G + g
                    pe.wait_ge(S["o_ready"], 1 + 2 * gi)
                    for item, src in enumerate([KS] + QS):
                        pe.wait_ge(S["stack_ready"], 1 + 5 * gi + item + 1)
                        for t in range(NT):
                            mm = pe.transpose(bank(item, t * P, (t + 1) * P), src[:, t, :], ident[:, :])
                        mm.then_inc(S["stack_T"], 1)
                    pe.wait_ge(S["stack_sb_a"], 1 + 3 * gi + 3)
                    pe.wait_ge(S["stack_sb_d"], 1 + 2 * gi + 2)
                    for i, (t, lo) in enumerate(((3, 0), (2, 4), (1, 0), (0, 2))):
                        n_keys = (t + 1) * P
                        if t == 1:
                            pe.wait_ge(S["s_max"], 1 + NT * gi + 1)
                        for n in range(HPG):
                            at = (lo + n) * 512 if t >= 2 else lo * 512 + n * n_keys
                            pe.matmul(PS[:, at + t * P:at + n_keys], identb[:, :], mask_qk[:, :],
                                      start=True, stop=False, skip_group_check=True)
                            mm = pe.matmul(PS[:, at:at + n_keys], QST[n][:, t * P:(t + 1) * P], KST[:, 0:n_keys],
                                           start=False, stop=True, skip_group_check=True)
                        mm.then_inc(S["s_ps"], 1)
                    def shifted(j, lo, width, n, parts):
                        at = lo * 512 + n * width
                        n_q = (NT - j) * P
                        if "scores" in parts:
                            pe.matmul(PS[:, at:at + P], identb[:, :], mask_kq[:, :], start=True, stop=False,
                                      skip_group_check=True)
                            mm = pe.matmul(PS[:, at:at + n_q], KST[:, j * P:(j + 1) * P], QST[n][:, j * P:T],
                                           start=False, stop=False, skip_group_check=True)
                        if "maxima" in parts:
                            mm = pe.matmul(PS[:, at:at + n_q], sel[:, n, :], RM[:, j * P:T], start=False,
                                           stop=True, skip_group_check=True)
                        return mm
                    pe.wait_ge(S["s_max"], 1 + NT * gi + 2)
                    for n in range(HPG):
                        shifted(0, 4, 512, n, "scores")
                    pe.wait_ge(S["nm_ready"], 1 + gi + 1)
                    pe.transpose(bank(3, 0, P), NM2[:, :], ident[:, :]).then_inc(S["mt_ps"], 1)
                    pe.wait_ge(S["rm_ready"], 1 + gi + 1)
                    for n in range(HPG):
                        mm = shifted(0, 4, 512, n, "maxima")
                    mm.then_inc(S["st_ps"], 1)
                    for n in range(HPG):
                        mm = shifted(1, 0, 512, n, "scores maxima")
                    mm.then_inc(S["st_ps"], 1)
                    pe.wait_ge(S["pt_ready"], 1 + NT * gi + 1)
                    for j, lo, width in ((2, 4, 256), (3, 6, 128)):
                        for n in range(HPG):
                            mm = shifted(j, lo, width, n, "scores maxima")
                        mm.then_inc(S["st_ps"], 1)
                    pe.wait_ge(S["v_ready"], 1 + gi + 1)
                    for t in range(NT):
                        bk = 7 if t < 2 else 0
                        pe.wait_ge(S["pt_ready"], 1 + NT * gi + max(t, 1 if t >= 2 else 0) + 1)
                        for n in range(HPG):
                            at = ((t % 2) * HPG + n) * (HD + 1)
                            for j in range(t + 1):
                                mm = pe.matmul(bank(bk, at, at + HD + 1), PTj(j)[:, n, (t - j) * P:(t - j + 1) * P],
                                               V5[:, j, :], start=(j == 0), stop=(j == t))
                        if t % 2:
                            mm.then_inc(S["pv_ps"], 1)
                pe.wait_ge(S["o_ready"], 1 + 2 * G * (b + 1))
                for t in range(NT):
                    for k in range(KC):
                        mm = pe.transpose(bank(t, k * P, (k + 1) * P), O[:, t, k * P:(k + 1) * P], ident[:, :])
                    mm.then_inc(S["oT_ps"], 1)
                for t in range(NT):
                    pe.wait_ge(S["oT_lo"], 1 + NT * b + t + 1)
                    sl = slice(t * P, (t + 1) * P)
                    for k in range(KC):
                        mm = three(bank(4 + t), (OTH[:, k, sl], OTL[:, k, sl]), (woH[:, k, :], woL[:, k, :]),
                                   k == 0, k == KC - 1)
                    mm.then_inc(S["op_ps"], 1)
                for t in range(NT):
                    pe.wait_ge(S["xn_ready"], 1 + NT * b + t + 1)
                    for k in range(KC):
                        mm = pe.transpose(bank(t, k * P, (k + 1) * P), XN[:, t, k * P:(k + 1) * P], ident[:, :])
                    mm.then_inc(S["xT_ps"], 1)
                for t in range(NT):
                    pe.wait_ge(S["xT_lo"], 1 + NT * b + t + 1)
                    sl = slice(t * P, (t + 1) * P)
                    for k in range(KC):
                        mm = three(bank(4 + t // 2, (t % 2) * 256, (t % 2) * 256 + PJ),
                                   (XTH[:, k, sl], XTL[:, k, sl]), (acH[:, k, :], acL[:, k, :]), k == 0, k == KC - 1)
                    if t % 2:
                        mm.then_inc(S["pj_ps"], 1)

                def gate_up(f, slot):
                    hi, lo = WHI[slot], WLO[slot]
                    pe.wait_ge(S["w_lo"], 1 + b * NF + f + 1)
                    for h, (bk, free, done) in enumerate(((0, "sil_ready", "gate_ps"), (1, "hid_ready", "up_ps"))):
                        pe.wait_ge(S[free], 1 + b * NF + f)
                        for k in range(KC):
                            c0 = k * 2 * P + h * P
                            three(bank(bk), (hi[:, c0:c0 + P], lo[:, c0:c0 + P]), (XTH[:, k, :], XTL[:, k, :]),
                                  k == 0, False)
                        c0 = WBG + h * P
                        three(bank(bk), (hi[0:LR, c0:c0 + P], lo[0:LR, c0:c0 + P]), (LXH[:, h, :], LXL[:, h, :]),
                              False, True).then_inc(S[done], 1)

                def down(f, slot):
                    hi, lo = WHI[slot], WLO[slot]
                    pe.wait_ge(S["hl_ready"], 1 + b * NF + f + 1)
                    for t in range(NT):
                        sl = slice(t * P, (t + 1) * P)
                        three(bank(2, t * LR, (t + 1) * LR), (HH[slot][:, sl], HL[slot][:, sl]),
                              (hi[:, WAD:WAD + LR], lo[:, WAD:WAD + LR]), False, False, skip_group_check=True)
                        mm = three(bank(4 + t), (HH[slot][:, sl], HL[slot][:, sl]),
                                   (hi[:, WD:WD + C], lo[:, WD:WD + C]), False, False, skip_group_check=True)
                    mm.then_inc(S["dn_ps"], 1)

                pe.wait_ge(S["lg_ready"], 1 + b + 1)
                for h in range(2):
                    for t in range(NT):
                        mm = pe.transpose(bank(6 + h, t * P, (t + 1) * P, parts=LR), LG[:, t, h, :], ident[:, :])
                    mm.then_inc(S["lx_ps"], 1)
                pe.wait_ge(S["lx_lo"], 1 + 2 * (b + 1))
                gate_up(0, 0)
                for bk in (2, 4, 5, 6, 7):
                    n = NT * LR if bk == 2 else 512
                    pe.matmul(bank(bk, 0, n), zrow[:, 0:P], zrow[:, 0:n], start=True, stop=False, skip_group_check=True)
                alone(pe, "pe")
                with pe.Fori(0, NF // 2) as i:
                    for d in (1, 2):
                        gate_up(2 * i + d, d % 2)
                        down(2 * i + d - 1, (d + 1) % 2)
                slot = (NF - 1) % 2
                hi, lo = WHI[slot], WLO[slot]
                pe.wait_ge(S["hl_ready"], 1 + b * NF + NF)
                for t in range(NT):
                    sl = slice(t * P, (t + 1) * P)
                    mm = three(bank(2, t * LR, (t + 1) * LR), (HH[slot][:, sl], HL[slot][:, sl]),
                               (hi[:, WAD:WAD + LR], lo[:, WAD:WAD + LR]), False, True, skip_group_check=True)
                mm.then_inc(S["ha_ps"], 1)
                for t in range(NT):
                    sl = slice(t * P, (t + 1) * P)
                    mm = three(bank(4 + t), (HH[slot][:, sl], HL[slot][:, sl]),
                               (hi[:, WD:WD + C], lo[:, WD:WD + C]), False, False, skip_group_check=True)
                mm.then_inc(S["dn_ps"], 1)
                pe.wait_ge(S["ld_ready"], 1 + b + 1)
                for t in range(NT):
                    mm = pe.transpose(bank(3, t * P, (t + 1) * P, parts=LR), LG[:, t, 0, :], ident[:, :])
                mm.then_inc(S["ld_ps"], 1)
                pe.wait_ge(S["ld_lo"], 1 + b + 1)
                for t in range(NT):
                    sl = slice(t * P, (t + 1) * P)
                    three(bank(4 + t), (LDH[:, sl], LDL[:, sl]), (bdH[:, :], bdL[:, :]), False, True,
                          skip_group_check=True).then_inc(S["ffn_ps"], 1)
                for t in range(NT):
                    pe.wait_ge(S["xn3_ready"], 1 + NT * b + t + 1)
                    for k in range(KC):
                        mm = pe.transpose(bank(t, k * P, (k + 1) * P), XN[:, t, k * P:(k + 1) * P], ident[:, :])
                    mm.then_inc(S["xT3_ps"], 1)
                pe.wait_ge(S["xT3_sb"], 1 + NT * (b + 1))
                for k in range(KC):
                    mm = pe.matmul(bank(4), KV[:, k, :], XTF[:, k, :], start=(k == 0), stop=(k == KC - 1))
                mm.then_inc(S["o1_ps"], 1)
                pe.wait_ge(S["o1_sb"], 1 + b + 1)
                for t in range(NT):
                    pe.matmul(bank(t), OT1[:, t * P:(t + 1) * P], KVT[:, :], start=True,
                              stop=True).then_inc(S["sim_ps"], 1)
                for t in range(NT):
                    pe.wait_ge(S["xn4_ready"], 1 + NT * b + t + 1)
                    for k in range(KC):
                        mm = pe.transpose(bank(4 + t, k * P, (k + 1) * P), HN[:, t, k * P:(k + 1) * P], ident[:, :])
                    mm.then_inc(S["xT4_ps"], 1)
                for t in range(NT):
                    pe.wait_ge(S["xT4_sb"], 1 + NT * b + t + 1)
                    for k in range(KC):
                        mm = pe.matmul(bank(0, t * E1, (t + 1) * E1), XTF[:, k, t * P:(t + 1) * P], rw[:, k, :],
                                       start=(k == 0), stop=(k == KC - 1))
                mm.then_inc(S["lgt_ps"], 1)
                pe.wait_ge(S["mk_ready"], 1 + b + 1)
                alone(pe, "pe")
                for t in range(NT):
                    mm = pe.transpose(bank(1, t * P, (t + 1) * P, parts=E1), MK[:, t, :], ident[:, :])
                mm.then_inc(S["mk_ps"], 1)
                pe.wait_ge(S["key_ready"], 1 + b + 1)
                pe.sem_inc(S["end_pe"], 1)

    place["at"] = part3_base
    LST = sb("LST", [E1, CAP])
    KEY2 = sb("KEY2", [E1, NTOK])
    next8 = [sb(f"next8_{h}", [E1, 8]) for h in range(2)]
    LT = sb("LT", [P, E1])
    lv = sb("lv", [P, E1])
    list_step, list_ready, list_ps = sem("list_step"), sem("list_ready"), sem("list_ps")
    W1 = [sb(f"W1_{s}", [P, KC, 2 * F1]) for s in range(4)]
    W2 = [sb(f"W2_{s}", [FH, 2, C]) for s in range(4)]
    with nc.Block() as block:
        @block.vector
        def _(dve):
            with dve.Fori(0, CAP // 16) as i:
                step = Chain(dve, list_step, 6, i * 6)
                for h, (src, dst) in enumerate(((KEY, KEY2), (KEY2, KEY))):
                    step(dve.max(next8[h][:, :], src[:, :]))
                    alone(dve, "dve")
                    step(dve.match_replace(dst[:, :], next8[h][:, :], src[:, :], -1.0))
                    step(dve.tensor_copy(LST[:, bass.ds(i * 16 + 8 * h, 8)], next8[h][:, :]))
                    alone(dve, "dve")
                step.end()
            done = CAP // 16 * 6
            dve.memset(lv[:, :], 0.0).then_inc(list_ready, 1)
            dve.wait_ge(list_ps, 1)
            dve.wait_ge(list_ready, 1)
            step = Chain(dve, list_step, 5, done)
            lt = bank(0, 0, E1)
            step(dve.tensor_scalar(lv[:, :], lt, 0.0, None, ALU.is_gt))
            step(dve.tensor_scalar(LT[:, :], lt, -1.0, float(2 * NTOK), ALU.mult, ALU.add))
            step(dve.tensor_scalar(LT[:, :], LT[:, :], dummy[:, 0:1], None, ALU.subtract))
            step(dve.tensor_tensor(LT[:, :], LT[:, :], lv[:, :], ALU.mult))
            step(dve.tensor_scalar(IDX[:, :], LT[:, :], dummy[:, 0:1], None, ALU.add))

        @block.tensor
        def _(pe):
            pe.wait_ge(list_ready, 1)
            pe.transpose(bank(0, 0, E1), LST[:, :], ident[0:E1, 0:E1]).then_inc(list_ps, 1)

    IDX1 = [sb(f"IDX1_{s}", [P, 1], U32) for s in range(4)]
    XG = [sb(f"XG{s}", [P, HROW]) for s in range(4)]
    XGT = [sb(f"XGT{s}", [P, KC, P]) for s in range(2)]
    WC = [sb(f"WC{s}", [P, 1]) for s in range(2)]
    SL = [sb(f"SL{s}", [P, F1]) for s in range(2)]
    HM = [sb(f"HM{s}", [P, F1]) for s in range(2)]
    HMT = [sb(f"HMT{s}", [FH, 2, P]) for s in range(2)]
    YE = [sb(f"YE{s}", [P, C]) for s in range(2)]
    w1_loaded = [sem(f"w1_loaded{s}") for s in range(4)]
    w2_loaded = [sem(f"w2_loaded{s}") for s in range(4)]
    gathered = [sem(f"gathered{s}") for s in range(4)]
    NW = 4
    with nc.Block() as block:
        @block.sync
        def _(sp):
            def load(e, s):
                sp.dma_start(W1[s][:, :, :], w["w1"][bass.ds(e * P, P), :].rearrange(
                    "p (k f) -> p k f", k=KC)).then_inc(w1_loaded[s], 16)
                sp.dma_start(W2[s][:, :, :], w["w2"][bass.ds(e * FH, FH), :].rearrange(
                    "p (h c) -> p h c", h=2)).then_inc(w2_loaded[s], 16)
            for s in range(NW):
                load(s, s)
            with sp.Fori(1, E1 // NW) as i:
                for s in range(NW):
                    sp.wait_ge(M["y_ps"], 1 + i * NW + s + 1 - NW)
                    alone(sp, "sp")
                    sp.wait_ge(w1_loaded[s], 16 * i)
                    sp.wait_ge(w2_loaded[s], 16 * i)
                    alone(sp, "sp")
                    load(i * NW + s, s)

        @block.gpsimd
        def _(pool):
            def gather(e, s, ahead):
                alone(pool, "pool")
                pool.tensor_copy(IDX1[s][:, :], IDX[:, bass.ds(e, 1)]).then_inc(M["idx"], 1)

            def start_gather(n, s):
                pool.wait_ge(M["idx"], 1 + n)
                alone(pool, "pool")
                pool.indirect_dma_start(out=XG[s][:, :], out_offset=None, in_=hx,
                                        in_offset=bass.IndirectOffsetOnAxis(ap=IDX1[s][:, 0:1], axis=0),
                                        ).then_inc(gathered[s], 16)

            def scatter(e, s, first=False):
                if not first:
                    pool.wait_ge(scattered, 16 * e)
                    alone(pool, "pool")
                pool.sem_inc(M["added"], 1)
                pool.wait_ge(M["y_sb"], 1 + e + 1)
                alone(pool, "pool")
                pool.indirect_dma_start(out=out, out_offset=bass.IndirectOffsetOnAxis(ap=IDX1[s][:, 0:1], axis=0),
                                        in_=YE[s % 2][:, :], in_offset=None, compute_op=ALU.add,
                                        ).then_inc(scattered, 16)

            def expert(e, s, first=False, last=False):
                if not last:
                    ahead = (s + 2) % NW
                    pool.wait_ge(M["hm"], 1 + e)
                    if not first:
                        pool.wait_ge(scattered, 16 * e)
                    gather(e + 2, ahead, None)
                    start_gather(e + 3, ahead)
                scatter(e, s, first)
            for s in range(2):
                gather(s, s, 0)
                start_gather(s + 1, s)
            for s in range(NW):
                expert(s, s, first=(s == 0))
            alone(pool, "pool")
            with pool.Fori(1, E1 // NW - 1) as i:
                for s in range(NW):
                    expert(i * NW + s, s)
            for s in range(NW):
                expert(E1 - NW + s, s, last=(s >= 2))
            pool.wait_ge(scattered, 16 * E1)

        @block.tensor
        def _(pe):
            with pe.Fori(0, E1 // NW) as i:
                for s in range(NW):
                    e = i * NW + s
                    u = s % 2
                    pe.wait_ge(gathered[s], 16 * (i + 1))
                    pe.wait_ge(M["xgt_sb"], 1 + e)
                    for k in range(KC):
                        mm = pe.transpose(bank(u, k * P, (k + 1) * P), XG[s][:, k * P:(k + 1) * P], ident[:, :])
                    mm.then_inc(M["xgt_ps"], 1)
                    pe.wait_ge(w1_loaded[s], 16 * (i + 1))
                    pe.wait_ge(M["xgt_sb"], 1 + e + 1)
                    pe.wait_ge(M["hm"], 1 + e)
                    for k in range(KC):
                        mm = pe.matmul(bank(2 + u, 0, 2 * F1), XGT[u][:, k, :], W1[s][:, k, :], start=(k == 0),
                                       stop=(k == KC - 1))
                    mm.then_inc(M["gu_ps"], 1)
                    pe.wait_ge(M["hm"], 1 + e + 1)
                    for h in range(2):
                        mm = pe.transpose(bank(4 + u, h * P, (h + 1) * P, parts=FH), HM[u][:, h * FH:(h + 1) * FH],
                                          ident[:, :])
                    mm.then_inc(M["hmt_ps"], 1)
                    pe.wait_ge(w2_loaded[s], 16 * (i + 1))
                    pe.wait_ge(M["hmt_sb"], 1 + e + 1)
                    pe.wait_ge(M["y_sb"], 1 + e)
                    for h in range(2):
                        mm = pe.matmul(bank(6 + u), HMT[u][:, h, :], W2[s][:, h, :], start=(h == 0), stop=(h == 1))
                    mm.then_inc(M["y_ps"], 1)

        @block.scalar
        def _(act):
            with act.Fori(0, E1 // NW) as i:
                for s in range(NW):
                    e = i * NW + s
                    u = s % 2
                    act.wait_ge(M["xgt_ps"], 1 + e + 1)
                    act.wait_ge(M["gu_ps"], 1 + e)
                    act.activation(XGT[u][:, :, :], bank(u).rearrange("p (k q) -> p k q", k=KC),
                                   ACT.Copy).then_inc(M["xgt_sb"], 1)
                    act.wait_ge(M["gu_ps"], 1 + e + 1)
                    act.wait_ge(M["hm"], 1 + e)
                    act.activation(SL[u][:, :], bank(2 + u, 0, F1), ACT.Silu).then_inc(M["sil"], 1)
                    act.wait_ge(M["y_ps"], 1 + e + 1)
                    act.wait_ge(M["added"], 1 + e)
                    act.activation(YE[u][:, :], bank(6 + u), ACT.Copy).then_inc(M["y_sb"], 1)

        @block.vector
        def _(dve):
            with dve.Fori(0, E1 // NW) as i:
                for s in range(NW):
                    e = i * NW + s
                    u = s % 2
                    dve.wait_ge(gathered[s], 16 * (i + 1))
                    dve.wait_ge(M["hmt_ps"], 1 + e)
                    dve.tensor_copy(WC[u][:, :], XG[s][:, bass.ds(C + e, 1)]).then_inc(M["wc"], 1)
                    dve.wait_ge(M["wc"], 1 + e + 1)
                    dve.wait_ge(M["sil"], 1 + e + 1)
                    dve.scalar_tensor_tensor(out=HM[u][:, :], in0=SL[u][:, :], scalar=WC[u][:, 0:1],
                                             in1=bank(2 + u, F1, 2 * F1), op0=ALU.mult,
                                             op1=ALU.mult).then_inc(M["hm"], 1)
                    dve.wait_ge(M["hmt_ps"], 1 + e + 1)
                    dve.wait_ge(M["y_ps"], 1 + e)
                    dve.tensor_copy(HMT[u][:, :, :], bank(4 + u, 0, 2 * P, parts=FH).rearrange(
                        "p (h q) -> p h q", h=2)).then_inc(M["hmt_sb"], 1)


BY_DMA = {"x_loaded", "ctx_loaded", "hx_stored", "out_stored", "dve_step", "g_dve", "g_pool"}
KSTEPS = {"dve": 152, "pool": 0, "act": 0, "g_dve": 5, "g_pool": 6}


def shape_constants():
    import numpy as np
    p = np.arange(P)
    c = {}
    c["ident"] = np.eye(P, dtype=np.float32)
    bf = mybir.dt.np(BF16)
    c["identb"] = np.eye(P).astype(bf)
    later = p[None, :] > p[:, None]
    c["mask_qk"] = np.where(later, -1e30, 0.0).astype(bf)
    c["mask_kq"] = np.where(later.T, -1e30, 0.0).astype(bf)
    c["iota8"] = np.tile(np.arange(E0, dtype=np.float32), (P, 1))
    c["dummy"] = (NTOK + p).astype(np.float32)[:, None]
    c["revt"] = np.tile(2 * NTOK - np.arange(NTOK, dtype=np.float32), (E1, 1))
    r = p % 32
    live = (r < NT * HPG) & (p < 64)
    c["blockmask"] = ((r[:, None] // HPG == np.arange(NT)) & live[:, None]).astype(np.float32)[:, :, None] * np.ones(
        (1, 1, P), np.float32)
    c["sel"] = ((r[:, None] % HPG == np.arange(HPG)) & live[:, None]).astype(np.float32)[:, :, None] * np.ones(
        (1, 1, P), np.float32)
    inv = (np.float32(1.0) / np.float32(10000.0) ** (np.arange(0, HD, 2, dtype=np.float32) / np.float32(HD)))
    fr = np.outer(np.arange(T, dtype=np.float32), inv.astype(np.float32)).astype(np.float32)
    emb = np.concatenate([fr, fr], -1)
    cos, sin = np.cos(emb.astype(np.float64)), np.sin(emb.astype(np.float64))
    sin = sin * np.where(np.arange(HD) < ROT, -1.0, 1.0)
    tiled = lambda a: np.ascontiguousarray(a.astype(np.float32).reshape(NT, P, HD).transpose(1, 0, 2))
    scale = float(HD) ** -0.5
    c["cos_q"], c["sin_q"], c["cos_k"], c["sin_k"] = tiled(cos * scale), tiled(sin * scale), tiled(cos), tiled(sin)
    return c


def lay_out(i):
    import numpy as np
    a = {k: np.asarray(v) for k, v in i.items()}
    kp = lambda m: np.ascontiguousarray(m.reshape(KC, P, -1).transpose(1, 0, 2))
    o = {}
    o["wo"] = kp(a["L0_xattn_w_out"].T)
    ex = lambda m: m.transpose(1, 0, 2).reshape(m.shape[1], -1)
    o["acat"] = kp(np.concatenate([a["L0_ffn_W_router"], a["L0_ffn_sA_gate"], ex(a["L0_ffn_A_gate"]),
                                   a["L0_ffn_sA_up"], ex(a["L0_ffn_A_up"])], 1))
    rowsb = lambda s, m: np.concatenate([s, m.reshape(E0 * R0, -1)], 0)
    o["bdown"] = np.ascontiguousarray(rowsb(a["L0_ffn_sB_down"], a["L0_ffn_B_down"]))
    st = np.zeros((NF, P, WCOLS), np.float32)
    bg, bu = rowsb(a["L0_ffn_sB_gate"], a["L0_ffn_B_gate"]), rowsb(a["L0_ffn_sB_up"], a["L0_ffn_B_up"])
    ad = np.concatenate([a["L0_ffn_sA_down"], ex(a["L0_ffn_A_down"])], 1)
    for f in range(NF):
        f0, f1 = f * P, min((f + 1) * P, DFF)
        n = f1 - f0
        for h, m in enumerate((a["L0_ffn_W_gate"], a["L0_ffn_W_up"])):
            for k in range(KC):
                st[f, :, k * 2 * P + h * P:k * 2 * P + h * P + n] = m[k * P:(k + 1) * P, f0:f1]
        st[f, 0:n, WD:WD + C] = a["L0_ffn_W_down"][f0:f1]
        st[f, 0:LR, WBG:WBG + n] = bg[:, f0:f1]
        st[f, 0:LR, WBU:WBU + n] = bu[:, f0:f1]
        st[f, 0:n, WAD:WAD + LR] = ad[f0:f1]
    o["ffn"] = st.reshape(NF * P, WCOLS)
    o["wk"] = np.ascontiguousarray(a["L1_xattn_W_k"].T)
    o["rw"] = kp(a["L1_ffn_router_w"].T)
    o["bk"], o["gamma"], o["beta"] = a["L1_xattn_b_k"], a["L1_xattn_ln_gamma"], a["L1_xattn_ln_beta"]
    o["ebias"], o["wq"], o["wkn"] = a["L0_ffn_expert_bias"], a["L0_xattn_q_norm_w"], a["L0_xattn_k_norm_w"]
    gu = np.concatenate([a["L1_ffn_w_gate"], a["L1_ffn_w_up"]], 2)
    o["w1"] = np.ascontiguousarray(gu.reshape(E1, KC, P, 2 * F1).transpose(0, 2, 1, 3)).reshape(E1 * P, -1)
    o["w2"] = np.ascontiguousarray(a["L1_ffn_w_down"].reshape(E1, 2, FH, C).transpose(0, 2, 1, 3)).reshape(
        E1 * FH, -1)
    o["x"] = a["x"].reshape(NTOK, C)
    o["ctx"] = a["ctx_512"].reshape(NTOK, CKV)
    return o


def kernel(**inputs):
    import numpy as np
    import concourse.bacc as bacc
    from concourse.bass_utils import run_bass_kernel_spmd as run

    nc = bacc.Bacc("TRN2", target_bir_lowering=False, num_devices=1)
    arrays = {"in_" + k: np.ascontiguousarray(v) for k, v in {**lay_out(inputs), **shape_constants()}.items()}
    ap = {k[3:]: nc.dram_tensor(k, v.shape, mybir.dt.from_np(v.dtype), kind="ExternalInput").ap()
          for k, v in arrays.items()}
    out = nc.dram_tensor("out", (ROWS, C), F32, kind="ExternalOutput").ap()
    hx = nc.dram_tensor("hx", (ROWS, HROW), F32, kind="Internal").ap()
    build(nc, ap["x"], ap["ctx"], ap, out, hx)
    r = run(nc, [arrays], core_ids=[0])
    return r.results[0]["out"][0:NTOK].reshape(B, T, C)
```

```python
import concourse.bass as bass
from concourse import mybir

F32 = mybir.dt.float32
F32R = mybir.dt.float32r
BF16 = mybir.dt.bfloat16
U32 = mybir.dt.uint32
ALU = mybir.AluOpType
ACT = mybir.ActivationFunctionType
AX = mybir.AxisListType.X

P = 128
B, T, C = 4, 512, 512
NT = T // P
KC = C // P
H, G = 16, 4
HPG = H // G
HD = C // H
CKV = G * HD
ROT = HD // 2
E0, R0 = 8, 8
LR = R0 * (E0 + 1)
DFF = 1376
NF = -(-DFF // P)
PJ = E0 + 2 * LR
WBG = KC * 2 * P
WBU, WD = WBG + P, WBG + 2 * P
WAD = WD + C
WCOLS = WAD + LR
E1, K1, F1, CAP = 64, 8, 192, 128
FH = F1 // 2
NTOK = B * T
ROWS = NTOK + P
HROW = C + E1
EPS_LN, EPS_RMS, EPS_SIM = 1e-5, 1e-5, 1e-6


class Chain:

    def __init__(self, engine, sem, per, base=0):
        self.engine, self.sem, self.per, self.base, self.n = engine, sem, per, base, 0

    def __call__(self, instruction):
        self.n += 1
        instruction.then_inc(self.sem, 1)
        self.engine.wait_ge(self.sem, self.base + self.n)

    def end(self):
        assert self.n == self.per, (self.sem, self.n, self.per)


def build(nc, x, ctx_in, w, out, hx):
    place = {"at": 16896}

    def sb(name, shape, dt=F32):
        size = 1
        for s in shape[1:]:
            size *= s
        size = -(-size * mybir.dt.size(dt) // 32) * 32
        t = nc.alloc_sbuf_tensor_at(name, shape, dt, offset=place["at"])
        place["at"] += size
        assert place["at"] <= 229344, (name, place["at"])
        return t

    def sem(name):
        return nc.alloc_semaphore(name)

    PS = nc.alloc_psum_tensor("PS", [P, 8 * 512], F32)

    def bank(i, a=0, b=512, parts=P):
        return PS[0:parts, i * 512 + a:i * 512 + b]

    ident = sb("ident", [P, P])
    identb = sb("identb", [P, P], BF16)
    mask_qk = sb("mask_qk", [P, P], BF16)
    mask_kq = sb("mask_kq", [P, P], BF16)
    zrow = sb("zrow", [1, 512], BF16)
    iota8 = sb("iota8", [P, E0])
    dummy = sb("dummy", [P, 1])
    revt = sb("revt", [E1, T])
    KEYS = [sb(f"KEYS{i}", [E1, CAP + T]) for i in range(2)]
    LST = sb("LST", [E1, CAP])
    next8 = sb("next8", [E1, 8])
    mhalf = sb("mhalf", [P, 8])
    IDX = sb("IDX", [P, E1], U32)
    part3_base = place["at"]
    blockmask = sb("blockmask", [P, NT, P])
    sel = sb("sel", [P, HPG, P], F32R)
    cosw = sb("cosw", [P, NT, C])
    sinw = sb("sinw", [P, NT, C])
    cosk = sb("cosk", [P, NT, CKV])
    sink = sb("sink", [P, NT, CKV])
    woH = sb("woH", [P, KC, C], F32R)
    woL = sb("woL", [P, KC, C], F32R)
    acH = sb("acH", [P, KC, PJ], F32R)
    acL = sb("acL", [P, KC, PJ], F32R)
    bdH = sb("bdH", [LR, C], F32R)
    bdL = sb("bdL", [LR, C], F32R)
    wk = sb("wk", [CKV, CKV])
    bk_col = sb("bk_col", [P, 1])
    bk_row = sb("bk_row", [P, CKV])
    gam = sb("gam", [P, T])
    bet = sb("bet", [P, T])
    ebias = sb("ebias", [P, E0])
    rw = sb("rw", [P, KC, E1])
    X = sb("X", [P, NT, C])
    XIN = sb("XIN", [P, NT, C])
    CTX = sb("CTX", [P, NT, CKV])
    KVT = sb("KVT", [P, T])
    KV = sb("KV", [P, NT, CKV])
    V8 = sb("V8", [P, NT, HPG * (P + HD)])
    ST6 = sb("ST6", [P, NT, 6])
    MV = sb("MV", [P, NT, 2])
    sm = [sb(f"sm{i}", [P, NT]) for i in range(6)]
    XN = sb("XN", [P, NT, C])
    QR = sb("QR", [P, NT, C])
    KR = sb("KR", [P, NT, CKV])
    FST6 = sb("FST6", [P, 2 * NT, 6])
    FMV = sb("FMV", [P, 2 * NT, 2])
    fvar, finv = sb("fvar", [P, 2 * NT]), sb("finv", [P, 2 * NT])
    fvar2, fscale, fms = sb("fvar2", [P, NT]), sb("fscale", [P, NT]), sb("fms", [P, NT])
    XW, QA, QB = XN[:, 0, :], XN[:, 1, :], XN[:, 2, :]
    region = place["at"]
    OTH = sb("OTH", [P, KC, T], F32R)
    OTL = sb("OTL", [P, KC, T], F32R)
    KS = sb("KS", [P, NT, P])
    QS = [sb(f"QS{n}", [P, NT, P]) for n in range(HPG)]
    KST = sb("KST", [P, T], F32R)
    QST = [sb(f"QST{n}", [P, T], F32R) for n in range(HPG)]
    NM = sb("NM", [P, NT * HPG])
    NM2 = sb("NM2", [P, P])
    RM = sb("RM", [P, T], F32R)
    SUMS = sb("SUMS", [P, T])
    UN = sb("UN", [P, T])
    RD = sb("RD", [P, NT * HPG])
    RDB = sb("RDB", [P, NT * HPG, HD])
    PT = sb("PT", [P, 10, P * HPG])
    OT = sb("OT", [P, G, T])
    pt_at = [0, 4, 7, 9]

    def PTj(j):
        return PT[:, pt_at[j]:pt_at[j] + NT - j, :].rearrange("p a b -> p (a b)").rearrange(
            "p (n q) -> p n q", n=HPG)

    place["at"] = region
    XTH = sb("XTH", [P, KC, T], F32R)
    XTL = sb("XTL", [P, KC, T], F32R)
    WRAW = [sb(f"WRAW{s}", [P, WCOLS]) for s in range(2)]
    WHI = [sb(f"WHI{s}", [P, WCOLS], F32R) for s in range(2)]
    WLO = [sb(f"WLO{s}", [P, WCOLS], F32R) for s in range(2)]
    SIL = sb("SIL", [P, T])
    HID = sb("HID", [P, T])
    HH = [sb(f"HH{s}", [P, T], F32R) for s in range(2)]
    HL = [sb(f"HL{s}", [P, T], F32R) for s in range(2)]
    PA = sb("PA", [P, NT, PJ])
    LG = sb("LG", [P, NT, 2, LR])
    LXH = sb("LXH", [LR, 2, T], F32R)
    LXL = sb("LXL", [LR, 2, T], F32R)
    LDH = sb("LDH", [LR, T], F32R)
    LDL = sb("LDL", [LR, T], F32R)
    r8 = [sb(f"r8_{i}", [P, NT, E0]) for i in range(4)]
    top2 = sb("top2", [P, NT, 8])
    top2i = sb("top2i", [P, NT, 8], U32)
    top2f = sb("top2f", [P, NT, 8])
    WX = sb("WX", [P, NT, LR])
    place["at"] = region + 2 * KC * T * 4
    XTF = sb("XTF", [P, KC, T])
    OT1 = sb("OT1", [P, T])
    Y = sb("Y", [P, NT, T])
    HN = sb("HN", [P, NT, HROW])
    SC = sb("SC", [P, NT, E1])
    SR = sb("SR", [P, NT, E1])
    MK = sb("MK", [P, NT, E1])
    t8 = sb("t8", [P, NT, 8])
    nmx = sb("nmx", [P, NT])
    ssum = sb("ssum", [P, NT])
    place["at"] = region
    wq_bc = sb("wq_bc", [P, C])
    wkn_bc = sb("wkn_bc", [P, CKV])
    cq = sb("cq", [P, NT, HD])
    sq = sb("sq", [P, NT, HD])
    ck = sb("ck", [P, NT, HD])
    sk = sb("sk", [P, NT, HD])
    wo_raw = sb("wo_raw", [P, KC, C])
    ac_raw = sb("ac_raw", [P, KC, PJ])
    bd_raw = sb("bd_raw", [LR, C])
    sel_raw = sb("sel_raw", [P, HPG, P])
    ZR = sb("ZR", [P, HROW])

    def cols(g, width, at=0, n=None):
        n = width if n is None else n
        return slice(g * width + at, g * width + at + n) if isinstance(g, int) else bass.ds(g * width + at, n)

    def row(g):
        return slice(g, g + 1) if isinstance(g, int) else bass.ds(g, 1)

    def rows(ap, n):
        return ap.rearrange("(t p) c -> p t c", p=P)

    def bcast(ap, n):
        return ap.rearrange("(a n) -> a n", a=1).broadcast_to([P, n])

    names = ("x_loaded ctx_loaded rev_loaded f_in f_out f_dve end_sp end_pool end_act end_dve end_pe alone_dve alone_pool alone_pe alone_sp "
             "qab_ready q_ready k_ready norm_in norm_out ctxT_ps ctxT_sb kv_ps kv_act kv_dve "
             "stack_ready stack_T stack_sb_a stack_sb_d v_ready s_ps s_max nm_ready mt_ps rm_ready "
             "st_ps pt_ready pv_ps sums_sb out_sb sums_T sums_inv inv_ps o_ready "
             "oT_ps oT_hi oT_lo op_ps x1_ready "
             "xn_ready xT_ps xT_hi xT_lo pj_ps pa_ready sig_ready lg_ready lx_ps lx_hi lx_lo "
             "wg_hi wg_lo wd_hi wd_lo gate_ps up_ps sil_ready hid_ready hh_ready hl_ready dn_ps ha_ps "
             "ld_ready ld_ps ld_hi ld_lo ffn_ps x2_ready "
             "xn3_ready xT3_ps xT3_sb o1_ps o1_sb sim_ps y_ready e_ready x3_ready "
             "xn4_ready xT4_ps xT4_sb lgt_ps lgt_max lgt_exp mk_ready mk_ps key_ready "
             "hx_stored out_stored dve_step pool_step g_dve g_pool list_dve").split()
    S = {n: sem(n) for n in names}
    w_loaded = [sem("w_loaded0"), sem("w_loaded1")]
    M = {n: sem("m_" + n) for n in ("idx xgt_ps xgt_sb gu_ps sil wc hm hmt_ps hmt_sb y_ps y_sb added".split())}
    scattered = sem("scattered")
    setup_loaded, setup_dve, setup_act, dummy_rows = (sem(n) for n in (
        "setup_loaded", "setup_dve", "setup_act", "dummy_rows"))
    n_loads = [0]
    with nc.Block() as block:
        @block.sync
        def _(sp):
            loads = [(ident, w["ident"]), (identb, w["identb"]), (mask_qk, w["mask_qk"]),
                     (mask_kq, w["mask_kq"]), (iota8, w["iota8"]), (dummy, w["dummy"]),
                     (blockmask, w["blockmask"]), (sel_raw, w["sel"]),
                     (cq, w["cos_q"]), (sq, w["sin_q"]), (ck, w["cos_k"]), (sk, w["sin_k"]),
                     (wo_raw, w["wo"]), (ac_raw, w["acat"]), (bd_raw, w["bdown"]),
                     (wk, w["wk"]), (rw, w["rw"])]
            for dst, src in loads:
                n = len(src.shape)
                sp.dma_start(dst[(slice(None),) * n], src).then_inc(setup_loaded, 16)
            sp.dma_start(bk_col[:, :], w["bk"].rearrange("(p a) -> p a", a=1)).then_inc(setup_loaded, 16)
            for dst, src, n in ((bk_row, w["bk"], CKV), (gam, w["gamma"], T), (bet, w["beta"], T),
                                (ebias, w["ebias"], E0), (wq_bc, w["wq"], C), (wkn_bc, w["wkn"], CKV)):
                sp.dma_start(dst[:, :], bcast(src, n)).then_inc(setup_loaded, 16)
            n_loads[0] = len(loads) + 7
            sp.wait_ge(setup_dve, 3)
            sp.dma_start(hx[NTOK:ROWS, :], ZR[:, :]).then_inc(dummy_rows, 16)
            sp.dma_start(out[NTOK:ROWS, :], ZR[:, 0:C]).then_inc(dummy_rows, 16)
            sp.wait_ge(dummy_rows, 32)

        @block.vector
        def _(dve):
            step = Chain(dve, setup_dve, None)
            step(dve.memset(ZR[:, :], 0.0))
            step(dve.memset(zrow[:, :], 0.0))
            step(dve.memset(mhalf[:, :], -0.5))
            step(dve.memset(V8[:, :, :], 0.0))
            for n in range(HPG):
                c0 = n * P + (n * HD + P // 2) % P
                step(dve.memset(V8[:, :, c0:c0 + HD], 1.0))
            step(dve.memset(LST[:, :], 0.0))
            step(dve.memset(KEYS[0][:, CAP:CAP + T], 0.0))
            dve.wait_ge(setup_loaded, 16 * n_loads[0])
            for t in range(NT):
                for tab_c, tab_s, wt, c_, s_, nh in ((cosw, sinw, wq_bc, cq, sq, H),
                                                     (cosk, sink, wkn_bc, ck, sk, G)):
                    def heads(ap, a, b):
                        return ap.rearrange("p (h d) -> p h d", h=nh)[:, :, a:b]

                    def table(ap, a, b):
                        return ap[:, t, a:b].unsqueeze(1).broadcast_to([P, nh, b - a])
                    step(dve.tensor_tensor(heads(tab_c[:, t, :], 0, HD), heads(wt[:, :], 0, HD),
                                           table(c_, 0, HD), ALU.mult))
                    step(dve.tensor_tensor(heads(tab_s[:, t, :], 0, ROT), heads(wt[:, :], ROT, HD),
                                           table(s_, 0, ROT), ALU.mult))
                    step(dve.tensor_tensor(heads(tab_s[:, t, :], ROT, HD), heads(wt[:, :], 0, ROT),
                                           table(s_, ROT, HD), ALU.mult))
            dve.wait_ge(setup_act, 4)
            step(dve.tensor_tensor(woL[:, :, :], wo_raw[:, :, :], woH[:, :, :], ALU.subtract))
            step(dve.tensor_tensor(acL[:, :, :], ac_raw[:, :, :], acH[:, :, :], ALU.subtract))
            step(dve.tensor_tensor(bdL[:, :], bd_raw[:, :], bdH[:, :], ALU.subtract))

        @block.gpsimd
        def _(pool):
            for name in S:
                if name not in BY_DMA:
                    pool.sem_inc(S[name], 1)
            for name in M:
                pool.sem_inc(M[name], 1)

        @block.scalar
        def _(act):
            act.wait_ge(setup_loaded, 16 * n_loads[0])
            for dst, src in ((woH, wo_raw), (acH, ac_raw), (sel, sel_raw)):
                act.activation(dst[:, :, :], src[:, :, :], ACT.Copy).then_inc(setup_act, 1)
            act.activation(bdH[:, :], bd_raw[:, :], ACT.Copy).then_inc(setup_act, 1)

    DVE_B, POOL_B, ACT_B, DVE_G, POOL_G = KSTEPS["dve"], KSTEPS["pool"], KSTEPS["act"], KSTEPS["g_dve"], KSTEPS["g_pool"]

    def batch_start(engine, b):
        for name in ("end_sp", "end_pool", "end_act", "end_dve", "end_pe"):
            engine.wait_ge(S[name], 1 + b)

    def alone(engine, name):
        engine.sem_inc(S["alone_" + name], 1)

    def list_round(dve, n, c):
        step = Chain(dve, S["list_dve"], 6, n * 6)
        for h in range(2):
            src, dst = KEYS[h], KEYS[1 - h]
            alone(dve, "dve")
            step(dve.max(next8[:, :], src[:, :]))
            alone(dve, "dve")
            step(dve.match_replace(dst[:, :], next8[:, :], src[:, :], -1.0))
            step(dve.tensor_copy(LST[:, bass.ds(16 * c + 8 * h, 8)], next8[:, :]))
        step.end()

    MAX_UNITS = [(3, 0, 2, 0, 512), (3, 2, 2, 1024, 512), (2, 0, 2, 0, 512), (2, 2, 2, 1024, 512),
                 (1, 0, 4, 0, 256), (0, 0, 4, 1024, 128)]
    PROB_UNITS = [(0, n, 1) for n in range(HPG)] + [(1, n, 1) for n in range(HPG)] + [(2, 0, 2), (2, 2, 2), (3, 0, 4)]
    MU, PU = len(MAX_UNITS), len(PROB_UNITS)

    with nc.Block() as block:
        @block.sync
        def _(sp):
            def load_batch(b):
                ctx_rows, x_rows = ((ap[b * T:(b + 1) * T, :] if isinstance(b, int) else ap[bass.ds(b * T, T), :])
                                    for ap in (ctx_in, x))
                sp.dma_start(CTX[:, :, :], rows(ctx_rows, NT)).then_inc(S["ctx_loaded"], 16)
                sp.dma_start(XIN[:, :, :], rows(x_rows, NT)).then_inc(S["x_loaded"], 16)
            load_batch(0)
            with sp.Fori(0, B) as b:
                batch_start(sp, b)
                alone(sp, "sp")
                sp.wait_ge(S["v_ready"], 1 + G * (b + 1))
                alone(sp, "sp")
                sp.wait_ge(S["kv_ps"], 1 + b + 1)
                alone(sp, "sp")
                sp.wait_ge(S["x1_ready"], 1 + NT * (b + 1))
                alone(sp, "sp")
                sp.dma_start(WRAW[0][:, :], w["ffn"][0:P, :]).then_inc(w_loaded[0], 16)
                sp.dma_start(WRAW[1][:, :], w["ffn"][P:2 * P, :]).then_inc(w_loaded[1], 16)
                load_batch(b + 1)
                sp.dma_start(revt[:, :], w["revt"][:, bass.ds(b * T, T)]).then_inc(S["rev_loaded"], 16)

                def load_w(f, slot):
                    sp.wait_ge(S["wg_hi"], 1 + b * NF + f - 1)
                    sp.wait_ge(S["wg_lo"], 1 + b * NF + f - 1)
                    sp.wait_ge(S["wd_hi"], 1 + b * NF + f - 1)
                    sp.wait_ge(S["wd_lo"], 1 + b * NF + f - 1)
                    alone(sp, "sp")
                    sp.dma_start(WRAW[slot][:, :], w["ffn"][bass.ds(f * P, P), :]).then_inc(w_loaded[slot], 16)
                with sp.Fori(1, NF // 2) as i:
                    load_w(2 * i, 0)
                    load_w(2 * i + 1, 1)
                load_w(NF - 1, 0)
                sp.wait_ge(S["key_ready"], 1 + b + 1)
                alone(sp, "sp")
                sp.dma_start(rows(hx[bass.ds(b * T, T), :], NT), HN[:, :, :]).then_inc(S["hx_stored"], 16)
                sp.dma_start(rows(out[bass.ds(b * T, T), :], NT), X[:, :, :]).then_inc(S["out_stored"], 16)
                sp.wait_ge(S["hx_stored"], 16 * (b + 1))
                sp.wait_ge(S["out_stored"], 16 * (b + 1))
                sp.sem_inc(S["end_sp"], 1)

        @block.gpsimd
        def _(pool):
            step = Chain(pool, S["pool_step"], POOL_B)

            def front_power(fb, n):
                pool.wait_ge(S["f_in"], 1 + 2 * fb + n)
                if n == 1:
                    ins = pool.tensor_tensor(finv[:, :], fvar[:, :], mhalf[:, :], ALU.pow)
                else:
                    ins = pool.tensor_tensor(fms[:, :], fvar2[:, :], mhalf[:, 0:NT], ALU.pow)
                ins.then_inc(S["f_out"], 1)

            def front_q(fb, t):
                pool.wait_ge(S["qab_ready"], 1 + NT * fb + t + 1)
                if not isinstance(t, int):
                    alone(pool, "pool")
                pool.tensor_tensor(QR[:, row(t), :], QA.unsqueeze(1), QB.unsqueeze(1), ALU.add).then_inc(S["q_ready"], 1)
            front_power(0, 1)
            front_power(0, 2)
            for t in range(NT):
                front_q(0, t)
            with pool.Fori(0, B) as b:
                step.base, step.n = b * POOL_B, 0
                batch_start(pool, b)

                def power(n):
                    pool.wait_ge(S["norm_in"], 1 + 4 * b + n)
                    pool.tensor_tensor(sm[1][:, :], sm[0][:, :], mhalf[:, 0:NT], ALU.pow).then_inc(S["norm_out"], 1)
                gstep = Chain(pool, S["g_pool"], POOL_G)

                def stacks(gi, g):
                    gstep.base, gstep.n = gi * POOL_G, 0
                    pool.wait_ge(S["stack_T"], 1 + 5 * gi)
                    kin = KR[:, :, cols(g, HD)].unsqueeze(2).broadcast_to([P, NT, 2, HD])
                    ks = KS[:, :, :].rearrange("p t (r s d) -> p t r s d", r=2, s=2)
                    alone(pool, "pool")
                    gstep(pool.tensor_copy(ks[:, :, :, 0, :].bitcast(F32R), kin))
                    alone(pool, "pool")
                    pool.tensor_tensor(ks[:, :, :, 1, :], kin, ks[:, :, :, 0, :], ALU.subtract).then_inc(S["stack_ready"], 1)
                    for n in range(HPG):
                        qin = QR[:, :, cols(g, P, n * HD, HD)].unsqueeze(2).broadcast_to([P, NT, 2, HD])
                        qs = QS[n][:, :, :].rearrange("p t (s r d) -> p t s r d", r=2, s=2)
                        gstep(pool.tensor_copy(qs[:, :, 0, :, :].bitcast(F32R), qin))
                        alone(pool, "pool")
                        pool.tensor_tensor(qs[:, :, 1, :, :], qin, qs[:, :, 0, :, :], ALU.subtract).then_inc(S["stack_ready"], 1)
                    gstep.end()

                def values(gi, g):
                    pool.wait_ge(S["pv_ps"], 1 + gi)
                    alone(pool, "pool")
                    diagonal = V8[:, :, :].rearrange("p t (n c) -> p t n c", c=P + HD)[:, :, :, 0:HD]
                    pool.tensor_copy(diagonal, CTX[:, :, cols(g, HD)].unsqueeze(2).broadcast_to(
                        [P, NT, HPG, HD])).then_inc(S["v_ready"], 1)

                def split_output(gi, g):
                    pool.wait_ge(S["o_ready"], 1 + gi + 1)
                    alone(pool, "pool")
                    pool.tensor_copy(OTH[:, row(g), :], OT[:, row(g), :]).then_inc(S["oT_hi"], 1)
                    pool.wait_ge(S["oT_hi"], 1 + gi + 1)
                    alone(pool, "pool")
                    pool.tensor_tensor(OTL[:, row(g), :], OT[:, row(g), :], OTH[:, row(g), :],
                                       ALU.subtract).then_inc(S["oT_lo"], 1)
                pool.wait_ge(S["q_ready"], 1 + NT * (b + 1))
                pool.wait_ge(S["k_ready"], 1 + b + 1)
                stacks(b * G, 0)
                values(b * G, 0)
                stacks(b * G + 1, 1)
                alone(pool, "pool")
                with pool.Fori(0, G - 2) as g:
                    stacks(b * G + g + 2, g + 2)
                    values(b * G + g + 1, g + 1)
                    split_output(b * G + g, g)
                values(b * G + G - 1, G - 1)
                split_output(b * G + G - 2, G - 2)
                split_output(b * G + G - 1, G - 1)
                pool.wait_ge(S["oT_lo"], 1 + G * (b + 1))
                power(1)
                def hidden(f, slot):
                    pool.wait_ge(S["hid_ready"], 1 + b * NF + f + 1)
                    pool.wait_ge(S["dn_ps"], 1 + b * NF + f - 1)
                    hid_split(slot)

                def hid_split(slot):
                    alone(pool, "pool")
                    pool.tensor_copy(HH[slot][:, :], HID[:, :]).then_inc(S["hh_ready"], 1)

                def hidden_tail(f, slot):
                    pool.wait_ge(S["hh_ready"], 1 + b * NF + f + 1)
                    pool.tensor_tensor(HL[slot][:, :], HID[:, :], HH[slot][:, :], ALU.subtract).then_inc(S["hl_ready"], 1)
                pool.wait_ge(S["hid_ready"], 1 + b * NF + 1)
                pool.wait_ge(S["dn_ps"], 1 + b * NF)
                hid_split(0)
                hidden_tail(0, 0)
                front_power(b + 1, 1)
                front_power(b + 1, 2)
                alone(pool, "pool")
                with pool.Fori(0, NF // 2 - 1) as i:
                    for d in (1, 2):
                        hidden(2 * i + d, d % 2)
                        hidden_tail(2 * i + d, d % 2)
                        if d == 1:
                            front_q(b + 1, i)
                for f in (NF - 2, NF - 1):
                    hidden(f, f % 2)
                    hidden_tail(f, f % 2)
                power(2)
                power(3)
                power(4)
                pool.wait_ge(S["norm_out"], 1 + 4 * (b + 1))
                pool.sem_inc(S["end_pool"], 1)

        @block.scalar
        def _(act):
            with act.Fori(0, B) as b:
                batch_start(act, b)
                act.wait_ge(S["ctxT_ps"], 1 + b + 1)
                act.activation(XN[:, 3, :], bank(0), ACT.Copy).then_inc(S["ctxT_sb"], 1)
                act.wait_ge(S["kv_ps"], 1 + b + 1)
                act.activation(KVT[:, :], bank(1), ACT.Identity, bias=bk_col[:, 0:1]).then_inc(S["kv_act"], 1)
                def stacks(gi):
                    for item, dst in ((0, KST), (1, QST[0]), (3, QST[2])):
                        act.wait_ge(S["stack_T"], 1 + 5 * gi + item + 1)
                        act.activation(dst[:, :], bank(item), ACT.Copy).then_inc(S["stack_sb_a"], 1)

                def probabilities(gi):
                    for u, (j, n0, nh) in enumerate(PROB_UNITS):
                        act.wait_ge(S["st_ps"], 1 + PU * gi + u + 1)
                        act.activation(PTj(j)[:, n0:n0 + nh, :], bank(4 + u % 2, 0, nh * (NT - j) * P).rearrange(
                            "p (n q) -> p n q", n=nh), ACT.Exp).then_inc(S["pt_ready"], 1)
                def unload(gi):
                    act.wait_ge(S["pv_ps"], 1 + gi + 1)
                    lo, hi = slice(0, P // 2), slice(P // 2, P)
                    act.wait_ge(S["sums_T"], 1 + gi)
                    act.activation(SUMS[hi, :], PS[hi, 6 * 512:7 * 512], ACT.Copy).then_inc(S["sums_sb"], 1)
                    act.activation(SUMS[lo, :], PS[lo, 7 * 512:8 * 512], ACT.Copy).then_inc(S["sums_sb"], 1)
                    act.wait_ge(S["o_ready"], 1 + gi)
                    act.activation(UN[lo, :], PS[lo, 6 * 512:7 * 512], ACT.Copy).then_inc(S["out_sb"], 1)
                    act.activation(UN[hi, :], PS[hi, 7 * 512:8 * 512], ACT.Copy).then_inc(S["out_sb"], 1)
                stacks(b * G)
                with act.Fori(0, G - 1) as g:
                    probabilities(b * G + g)
                    stacks(b * G + g + 1)
                    unload(b * G + g)
                probabilities(b * G + G - 1)
                unload(b * G + G - 1)
                act.wait_ge(S["op_ps"], 1 + NT * (b + 1))
                for t in range(NT):
                    act.wait_ge(S["xT_ps"], 1 + NT * b + t + 1)
                    act.activation(XTH[:, :, t * P:(t + 1) * P], bank(4 + t).rearrange("p (k q) -> p k q", k=KC),
                                   ACT.Copy).then_inc(S["xT_hi"], 1)
                act.wait_ge(S["pa_ready"], 1 + b + 1)
                act.activation(r8[0][:, :, :], PA[:, :, 0:E0], ACT.Exp, scale=-1.0).then_inc(S["sig_ready"], 1)

                N0, N1 = NF // 2 + 1, NF // 2

                def wg_hi(f, slot, loads):
                    act.wait_ge(w_loaded[slot], 16 * loads)
                    act.activation(WHI[slot][:, 0:WD], WRAW[slot][:, 0:WD], ACT.Copy).then_inc(S["wg_hi"], 1)

                def wd_hi(slot):
                    act.activation(WHI[slot][:, WD:WCOLS], WRAW[slot][:, WD:WCOLS], ACT.Copy).then_inc(S["wd_hi"], 1)

                def silu(f):
                    act.wait_ge(S["gate_ps"], 1 + b * NF + f + 1)
                    act.wait_ge(S["hid_ready"], 1 + b * NF + f)
                    act.activation(SIL[:, :], bank(0), ACT.Silu).then_inc(S["sil_ready"], 1)

                def chunk(f, slot, next_loads):
                    if next_loads is not None:
                        act.wait_ge(S["up_ps"], 1 + b * NF + f)
                        wg_hi(f + 1, 1 - slot, next_loads)
                    if not (isinstance(f, int) and f < 2):
                        act.wait_ge(S["dn_ps"], 1 + b * NF + f - 1)
                    wd_hi(slot)
                    silu(f)
                wg_hi(0, 0, b * N0 + 1)
                for h in range(2):
                    act.wait_ge(S["lx_ps"], 1 + 2 * b + h + 1)
                    act.activation(LXH[:, h, :], bank(6 + h, parts=LR), ACT.Copy).then_inc(S["lx_hi"], 1)
                chunk(0, 0, b * N1 + 1)
                with act.Fori(0, NF // 2 - 1) as i:
                    for d in (1, 2):
                        chunk(2 * i + d, d % 2, (b * N0 + i + 2) if d == 1 else (b * N1 + i + 2))
                chunk(NF - 2, 1, (b + 1) * N0)
                chunk(NF - 1, 0, None)
                act.wait_ge(S["ld_ps"], 1 + b + 1)
                act.activation(LDH[:, :], bank(3, parts=LR), ACT.Copy).then_inc(S["ld_hi"], 1)
                for t in range(NT):
                    act.wait_ge(S["xT3_ps"], 1 + NT * b + t + 1)
                    act.activation(XTF[:, :, t * P:(t + 1) * P], bank(t).rearrange("p (k q) -> p k q", k=KC),
                                   ACT.Copy).then_inc(S["xT3_sb"], 1)
                act.wait_ge(S["o1_ps"], 1 + b + 1)
                act.activation(OT1[:, :], bank(4), ACT.Copy, scale=float(C) ** -0.5).then_inc(S["o1_sb"], 1)
                for t in range(NT):
                    act.wait_ge(S["y_ready"], 1 + NT * b + t + 1)
                    act.activation(Y[:, t, :], Y[:, t, :], ACT.Exp, bias=nmx[:, t:t + 1],
                                   accum_out=ssum[:, t:t + 1]).then_inc(S["e_ready"], 1)
                for t in range(NT):
                    act.wait_ge(S["xT4_ps"], 1 + NT * b + t + 1)
                    act.activation(XTF[:, :, t * P:(t + 1) * P], bank(4 + t).rearrange("p (k q) -> p k q", k=KC),
                                   ACT.Copy).then_inc(S["xT4_sb"], 1)
                act.wait_ge(S["lgt_max"], 1 + b + 1)
                act.activation(SC[:, :, :], SC[:, :, :], ACT.Exp).then_inc(S["lgt_exp"], 1)
                act.wait_ge(S["lgt_exp"], 1 + b + 1)
                act.sem_inc(S["end_act"], 1)

        @block.vector
        def _(dve):
            step = Chain(dve, S["dve_step"], DVE_B)
            gstep = Chain(dve, S["g_dve"], DVE_G)
            fstep = Chain(dve, S["f_dve"], KSTEPS["f_dve"])

            def sig(instruction, name, value):
                instruction.then_inc(S[name], 1)
                dve.wait_ge(S[name], 1 + value)

            def front_norms(fb):
                fstep.base, fstep.n = fb * KSTEPS["f_dve"], 0
                dve.wait_ge(S["ctx_loaded"], 16 * (fb + 1))
                dve.wait_ge(S["x_loaded"], 16 * (fb + 1))
                alone(dve, "dve")
                for i in range(2 * NT):
                    ins = dve.bn_stats(FST6[:, i, :], CTX[:, i, :] if i < NT else XIN[:, i - NT, :])
                    if i < 2 * NT - 1:
                        ins.then_inc(S["f_dve"], 1)
                        fstep.n += 1
                    else:
                        fstep(ins)
                for i in range(2 * NT):
                    alone(dve, "dve")
                    ins = dve.bn_aggr(FMV[:, i, :], FST6[:, i, :])
                    if i < 2 * NT - 1:
                        ins.then_inc(S["f_dve"], 1)
                        fstep.n += 1
                    else:
                        fstep(ins)
                fstep(dve.tensor_tensor(fscale[:, :], FMV[:, 0:NT, 0], FMV[:, 0:NT, 0], ALU.mult))
                fstep(dve.tensor_tensor(fscale[:, :], fscale[:, :], FMV[:, 0:NT, 1], ALU.add))
                fstep(dve.tensor_scalar(fvar[:, 0:NT], fscale[:, :], EPS_RMS, None, ALU.add))
                sig(dve.tensor_scalar(fvar[:, NT:2 * NT], FMV[:, NT:2 * NT, 1], EPS_LN, None, ALU.add),
                    "f_in", 2 * fb + 1)
                dve.wait_ge(S["f_out"], 1 + 2 * fb + 1)
                fstep(dve.tensor_tensor(fscale[:, :], finv[:, NT:2 * NT], finv[:, NT:2 * NT], ALU.mult))
                fstep(dve.tensor_tensor(fscale[:, :], fscale[:, :], FMV[:, NT:2 * NT, 1], ALU.mult))
                sig(dve.tensor_scalar(fvar2[:, :], fscale[:, :], EPS_RMS, None, ALU.add), "f_in", 2 * fb + 2)
                dve.wait_ge(S["f_out"], 1 + 2 * fb + 2)
                fstep(dve.tensor_tensor(fscale[:, :], finv[:, NT:2 * NT], fms[:, :], ALU.mult))

            def rotary(xm, qa, qb, tab_c, tab_s, last):
                hv = lambda ap, a, z: ap.rearrange("p (h d) -> p h d", d=HD)[:, :, a:z]
                fstep(dve.tensor_tensor(qa, xm, tab_c, ALU.mult))
                fstep(dve.tensor_tensor(hv(qb, 0, ROT), hv(xm, ROT, HD), hv(tab_s, 0, ROT), ALU.mult))
                last(dve.tensor_tensor(hv(qb, ROT, HD), hv(xm, 0, ROT), hv(tab_s, ROT, HD), ALU.mult))

            def front_q(fb, t):
                if isinstance(t, int):
                    xt, sc, mn, tc, ts = XIN[:, t, :], fscale[:, t:t + 1], FMV[:, NT + t, 0:1], cosw[:, t, :], sinw[:, t, :]
                else:
                    xt, sc, mn = (XIN[:, bass.ds(t, 1), :].rearrange("p t c -> p (t c)"), fscale[:, bass.ds(t, 1)],
                                  FMV[:, bass.ds(NT + t, 1), 0])
                    tc, ts = (tab[:, bass.ds(t, 1), :].rearrange("p t c -> p (t c)") for tab in (cosw, sinw))
                dve.wait_ge(S["q_ready"], 1 + NT * fb + t)
                fstep(dve.tensor_scalar(XW, xt, mn, sc, ALU.subtract, ALU.mult))
                rotary(XW, QA, QB, tc, ts, lambda ins: sig(ins, "qab_ready", NT * fb + t + 1))

            def front_k(fb):
                dve.wait_ge(S["q_ready"], 1 + NT * (fb + 1))
                flat = lambda ap: ap.rearrange("p t c -> p (t c)")
                fstep(dve.tensor_tensor(XW.rearrange("p (t c) -> p t c", t=NT), CTX[:, :, :],
                                        finv[:, 0:NT].unsqueeze(2).broadcast_to([P, NT, CKV]), ALU.mult))
                rotary(XW, QA, QB, flat(cosk[:, :, :]), flat(sink[:, :, :]), fstep)
                sig(dve.tensor_tensor(flat(KR[:, :, :]), QA, QB, ALU.add), "k_ready", fb + 1)
            front_norms(0)
            for t in range(NT):
                front_q(0, t)
            front_k(0)
            fstep.end()
            with dve.Fori(0, B) as b:
                step.base, step.n = b * DVE_B, 0
                batch_start(dve, b)
                norms = [0]

                def inverse_root():
                    norms[0] += 1
                    dve.wait_ge(S["norm_out"], 1 + 4 * b + norms[0])

                def stats(src, s6, mv):
                    for t in range(NT):
                        step(dve.bn_stats(s6[:, t, :], src[:, t, :]))
                        alone(dve, "dve")
                        step(dve.bn_aggr(mv[:, t, :], s6[:, t, :]))

                def layer_norm(src, dst, eps, ready):
                    stats(src, ST6, MV)
                    sig(dve.tensor_scalar(sm[0][:, :], MV[:, :, 1], eps, None, ALU.add), "norm_in", 4 * b + norms[0] + 1)
                    inverse_root()
                    for t in range(NT):
                        sig(dve.tensor_scalar(dst[:, t, 0:C], src[:, t, :], MV[:, t, 0:1], sm[1][:, t:t + 1],
                                              ALU.subtract, ALU.mult), ready, NT * b + t + 1)

                dve.wait_ge(S["kv_ps"], 1 + b + 1)
                sig(dve.tensor_tensor(KV[:, :, :], bank(2).rearrange("p (t d) -> p t d", t=NT),
                                      bk_row[:, :].unsqueeze(1).broadcast_to([P, NT, CKV]), ALU.add),
                    "kv_dve", b + 1)
                step(dve.memset(NM2[:, :], 0.0))
                alone(dve, "dve")
                def maxima(gi):
                    for i, (item, bk, dst) in enumerate(((2, 2, QST[1]), (4, 5, QST[3]))):
                        dve.wait_ge(S["stack_T"], 1 + 5 * gi + item + 1)
                        sig(dve.tensor_copy(dst[:, :], bank(bk)), "stack_sb_d", 2 * gi + i + 1)
                    for i, (t, n0, nh, at, width) in enumerate(MAX_UNITS):
                        dve.wait_ge(S["s_ps"], 1 + MU * gi + i + 1)
                        src = PS[:, at:at + nh * width].rearrange("p (n k) -> p n k", n=nh)[:, :, 0:(t + 1) * P]
                        sig(dve.tensor_reduce(NM[:, t * HPG + n0:t * HPG + n0 + nh], src, AX, ALU.max, negate=True),
                            "s_max", MU * gi + i + 1)
                    dve.wait_ge(S["mt_ps"], 1 + gi)
                    gstep(dve.tensor_copy(NM2[:, 0:16].bitcast(F32R), NM[:, :]))
                    sig(dve.tensor_tensor(NM2[:, 32:48], NM[:, :], NM2[:, 0:16], ALU.subtract), "nm_ready", gi + 1)
                    dve.wait_ge(S["mt_ps"], 1 + gi + 1)
                    sig(dve.tensor_tensor(RM[:, :].rearrange("p (t q) -> p t q", t=NT),
                                          bank(3, 0, P).unsqueeze(1).broadcast_to([P, NT, P]), blockmask[:, :, :],
                                          ALU.mult), "rm_ready", gi + 1)

                def normalise(gi, g):
                    dve.wait_ge(S["sums_T"], 1 + gi + 1)
                    dve.wait_ge(S["inv_ps"], 1 + gi)
                    ones = bank(0).rearrange("p (t n d) -> p t n d", t=NT, n=HPG)
                    rd = RD[:, :].rearrange("p (t n) -> p t n", t=NT)
                    gstep(dve.reciprocal(rd[:, :, 0:2], ones[:, :, 2:4, 0]))
                    gstep(dve.reciprocal(rd[:, :, 2:4], ones[:, :, 0:2, 0]))
                    sig(dve.tensor_copy(RDB[:, :, :], RD[:, :].unsqueeze(2).broadcast_to([P, NT * HPG, HD])),
                        "sums_inv", gi + 1)
                    dve.wait_ge(S["oT_lo"], 1 + gi)
                    dve.wait_ge(S["inv_ps"], 1 + gi + 1)
                    dve.wait_ge(S["out_sb"], 1 + 2 * (gi + 1))
                    sig(dve.tensor_tensor(OT[:, row(g), :], bank(1).unsqueeze(1), UN[:, :].unsqueeze(1), ALU.mult),
                        "o_ready", gi + 1)
                gstep.base, gstep.n = b * G * DVE_G, 0
                maxima(b * G)
                alone(dve, "dve")
                with dve.Fori(0, G - 1) as g:
                    gi = b * G + g
                    gstep.base, gstep.n = gi * DVE_G + 1, 0
                    dve.wait_ge(S["st_ps"], 1 + PU * (gi + 1))
                    maxima(gi + 1)
                    normalise(gi, g)
                gstep.end()
                gstep.base, gstep.n = (b * G + G - 1) * DVE_G + 1, 0
                normalise(b * G + G - 1, G - 1)
                for t in range(NT):
                    dve.wait_ge(S["op_ps"], 1 + NT * b + t + 1)
                    sig(dve.tensor_tensor(X[:, t, :], bank(2 + t), XIN[:, t, :], ALU.add), "x1_ready", NT * b + t + 1)
                layer_norm(X, XN, EPS_LN, "xn_ready")
                for t in range(NT):
                    dve.wait_ge(S["xT_hi"], 1 + NT * b + t + 1)
                    sl = slice(t * P, (t + 1) * P)
                    sig(dve.tensor_tensor(XTL[:, :, sl], bank(4 + t).rearrange("p (k q) -> p k q", k=KC),
                                          XTH[:, :, sl], ALU.subtract), "xT_lo", NT * b + t + 1)
                for i in range(2):
                    dve.wait_ge(S["pj_ps"], 1 + 2 * b + i + 1)
                    ins = dve.tensor_copy(PA[:, 2 * i:2 * i + 2, :],
                                          bank(i).rearrange("p (t c) -> p t c", t=2)[:, :, 0:PJ])
                    if i == 0:
                        step(ins)
                    else:
                        sig(ins, "pa_ready", b + 1)
                dve.wait_ge(S["sig_ready"], 1 + b + 1)
                step(dve.tensor_scalar(r8[1][:, :, :], r8[0][:, :, :], 1.0, None, ALU.add))
                step(dve.reciprocal(r8[0][:, :, :], r8[1][:, :, :]))
                step(dve.tensor_tensor(r8[1][:, :, :], r8[0][:, :, :],
                                       ebias[:, :].unsqueeze(1).broadcast_to([P, NT, E0]), ALU.add))
                for t in range(NT):
                    alone(dve, "dve")
                    step(dve.max(top2[:, t, :], r8[1][:, t, :]))
                    alone(dve, "dve")
                    step(dve.max_index(top2i[:, t, :], top2[:, t, :], r8[1][:, t, :]))
                step(dve.tensor_copy(top2f[:, :, :], top2i[:, :, :]))
                for t in range(NT):
                    step(dve.tensor_scalar(r8[2][:, t, :], iota8[:, :], top2f[:, t, 0:1], None, ALU.is_equal))
                    step(dve.scalar_tensor_tensor(out=r8[3][:, t, :], in0=iota8[:, :], scalar=top2f[:, t, 1:2],
                                                  in1=r8[2][:, t, :], op0=ALU.is_equal, op1=ALU.add))
                step(dve.tensor_tensor(r8[2][:, :, :], r8[3][:, :, :], r8[0][:, :, :], ALU.mult))
                step(dve.tensor_reduce(sm[2][:, :], r8[2][:, :, :], AX, ALU.add))
                step(dve.tensor_scalar(sm[3][:, :], sm[2][:, :], 1e-8, None, ALU.add))
                step(dve.reciprocal(sm[2][:, :], sm[3][:, :]))
                step(dve.tensor_scalar(sm[3][:, :], sm[2][:, :], 1.0 / R0, None, ALU.mult))
                step(dve.tensor_tensor(r8[3][:, :, :], r8[2][:, :, :],
                                       sm[3][:, :].unsqueeze(2).broadcast_to([P, NT, E0]), ALU.mult))
                step(dve.memset(WX[:, :, 0:R0], 1.0 / R0))
                for t in range(NT):
                    step(dve.tensor_copy(WX[:, t, R0:LR].rearrange("p (e r) -> p e r", e=E0),
                                         r8[3][:, t, :].unsqueeze(2).broadcast_to([P, E0, R0])))
                for t in range(NT):
                    ins = dve.tensor_tensor(LG[:, t, :, :], PA[:, t, E0:PJ].rearrange("p (h r) -> p h r", h=2),
                                            WX[:, t, :].unsqueeze(1).broadcast_to([P, 2, LR]), ALU.mult)
                    if t < NT - 1:
                        step(ins)
                    else:
                        sig(ins, "lg_ready", b + 1)

                def w_rest(n, slot, a, z, hi, lo):
                    dve.wait_ge(S[hi], 1 + b * NF + n + 1)
                    sig(dve.tensor_tensor(WLO[slot][:, a:z], WRAW[slot][:, a:z], WHI[slot][:, a:z], ALU.subtract),
                        lo, b * NF + n + 1)

                def chunk(f, slot, last=False):
                    if not last:
                        w_rest(f + 1, 1 - slot, 0, WD, "wg_hi", "wg_lo")
                    w_rest(f, slot, WD, WCOLS, "wd_hi", "wd_lo")
                    dve.wait_ge(S["sil_ready"], 1 + b * NF + f + 1)
                    dve.wait_ge(S["up_ps"], 1 + b * NF + f + 1)
                    dve.wait_ge(S["hl_ready"], 1 + b * NF + f)
                    sig(dve.tensor_tensor(HID[:, :], SIL[:, :], bank(1), ALU.mult), "hid_ready", b * NF + f + 1)
                w_rest(0, 0, 0, WD, "wg_hi", "wg_lo")
                for h in range(2):
                    dve.wait_ge(S["lx_hi"], 1 + 2 * b + h + 1)
                    sig(dve.tensor_tensor(LXL[:, h, :], bank(6 + h, parts=LR), LXH[:, h, :], ALU.subtract),
                        "lx_lo", 2 * b + h + 1)
                step(dve.tensor_copy(KEYS[0][:, 0:CAP], LST[:, :]))
                chunk(0, 0)
                front_norms(b + 1)
                fdone = fstep.n
                alone(dve, "dve")
                with dve.Fori(0, NF // 2 - 1) as i:
                    for d in (1, 2):
                        chunk(2 * i + d, d % 2)
                        list_round(dve, (NF // 2 - 1) * 2 * b + 2 * i + d - 1, 2 * i + d - 1)
                        if d == 1:
                            fstep.base, fstep.n = (b + 1) * KSTEPS["f_dve"] + fdone + i * 3, 0
                            front_q(b + 1, i)
                chunk(NF - 2, 1)
                fstep.base, fstep.n = (b + 1) * KSTEPS["f_dve"], fdone + 3 * NT
                front_k(b + 1)
                fstep.end()
                chunk(NF - 1, 0, last=True)
                dve.wait_ge(S["ha_ps"], 1 + b + 1)
                sig(dve.tensor_tensor(LG[:, :, 0, :], bank(2, 0, NT * LR).rearrange("p (t r) -> p t r", t=NT),
                                      WX[:, :, :], ALU.mult), "ld_ready", b + 1)
                dve.wait_ge(S["ld_hi"], 1 + b + 1)
                sig(dve.tensor_tensor(LDL[:, :], bank(3, parts=LR), LDH[:, :], ALU.subtract), "ld_lo", b + 1)
                for t in range(NT):
                    dve.wait_ge(S["ffn_ps"], 1 + NT * b + t + 1)
                    sig(dve.tensor_tensor(X[:, t, :], bank(4 + t), X[:, t, :], ALU.add), "x2_ready", NT * b + t + 1)
                layer_norm(X, XN, EPS_LN, "xn3_ready")
                for t in range(NT):
                    dve.wait_ge(S["sim_ps"], 1 + NT * b + t + 1)
                    step(dve.bn_stats(ST6[:, t, :], bank(t)))
                    alone(dve, "dve")
                    step(dve.bn_aggr(MV[:, t, :], ST6[:, t, :]))
                sig(dve.tensor_scalar(sm[0][:, :], MV[:, :, 1], EPS_SIM, None, ALU.add), "norm_in", 4 * b + norms[0] + 1)
                inverse_root()
                for t in range(NT):
                    step(dve.tensor_scalar(Y[:, t, :], bank(t), MV[:, t, 0:1], sm[1][:, t:t + 1],
                                           ALU.subtract, ALU.mult))
                    step(dve.tensor_tensor(Y[:, t, :], Y[:, t, :], gam[:, :], ALU.mult))
                    step(dve.tensor_tensor(Y[:, t, :], Y[:, t, :], bet[:, :], ALU.add))
                    sig(dve.tensor_reduce(nmx[:, t:t + 1], Y[:, t, :], AX, ALU.max, negate=True),
                        "y_ready", NT * b + t + 1)
                for t in range(NT):
                    dve.wait_ge(S["e_ready"], 1 + NT * b + t + 1)
                    step(dve.reciprocal(sm[2][:, t:t + 1], ssum[:, t:t + 1]))
                    sig(dve.scalar_tensor_tensor(out=X[:, t, :], in0=Y[:, t, :], scalar=sm[2][:, t:t + 1],
                                                 in1=X[:, t, :], op0=ALU.mult, op1=ALU.add),
                        "x3_ready", NT * b + t + 1)
                layer_norm(X, HN, EPS_LN, "xn4_ready")
                dve.wait_ge(S["lgt_ps"], 1 + b + 1)
                lg = bank(0, 0, NT * E1).rearrange("p (t e) -> p t e", t=NT)
                step(dve.tensor_reduce(sm[2][:, :], lg, AX, ALU.max))
                sig(dve.tensor_tensor(SC[:, :, :], lg, sm[2][:, :].unsqueeze(2).broadcast_to([P, NT, E1]),
                                      ALU.subtract), "lgt_max", b + 1)
                dve.wait_ge(S["lgt_exp"], 1 + b + 1)
                step(dve.tensor_reduce(sm[2][:, :], SC[:, :, :], AX, ALU.add))
                step(dve.reciprocal(sm[3][:, :], sm[2][:, :]))
                step(dve.tensor_tensor(SC[:, :, :], SC[:, :, :], sm[3][:, :].unsqueeze(2).broadcast_to([P, NT, E1]),
                                       ALU.mult))
                for t in range(NT):
                    alone(dve, "dve")
                    step(dve.max(t8[:, t, :], SC[:, t, :]))
                    alone(dve, "dve")
                    step(dve.match_replace(SR[:, t, :], t8[:, t, :], SC[:, t, :], -1.0))
                sig(dve.tensor_scalar(MK[:, :, :], SR[:, :, :], 0.0, None, ALU.is_lt), "mk_ready", b + 1)
                step(dve.tensor_tensor(SR[:, :, :], MK[:, :, :], SC[:, :, :], ALU.mult))
                step(dve.tensor_reduce(sm[2][:, :], SR[:, :, :], AX, ALU.add))
                step(dve.tensor_scalar(sm[3][:, :], sm[2][:, :], 1e-20, None, ALU.add))
                step(dve.reciprocal(sm[2][:, :], sm[3][:, :]))
                step(dve.tensor_tensor(HN[:, :, C:HROW], SR[:, :, :],
                                       sm[2][:, :].unsqueeze(2).broadcast_to([P, NT, E1]), ALU.mult))
                dve.wait_ge(S["rev_loaded"], 16 * (b + 1))
                dve.wait_ge(S["mk_ps"], 1 + b + 1)
                sig(dve.tensor_tensor(KEYS[0][:, CAP:CAP + T], bank(1, parts=E1), revt[:, :],
                                      ALU.mult), "key_ready", b + 1)
                dve.sem_inc(S["end_dve"], 1)
            step.end()

        @block.tensor
        def _(pe):
            def three(dst, a, b_, first, last, **kw):
                pe.matmul(dst, a[0], b_[0], start=first, stop=False, **kw)
                pe.matmul(dst, a[0], b_[1], start=False, stop=False, **kw)
                return pe.matmul(dst, a[1], b_[0], start=False, stop=last, **kw)

            with pe.Fori(0, B) as b:
                batch_start(pe, b)
                pe.wait_ge(S["ctx_loaded"], 16 * (b + 1))
                for t in range(NT):
                    mm = pe.transpose(bank(0, t * P, (t + 1) * P), CTX[:, t, :], ident[:, :])
                mm.then_inc(S["ctxT_ps"], 1)
                pe.wait_ge(S["ctxT_sb"], 1 + b + 1)
                ctxT = XN[:, 3, :]
                pe.matmul(bank(1), wk[:, :], ctxT, start=True, stop=True)
                for t in range(NT):
                    mm = pe.matmul(bank(2, t * P, (t + 1) * P), ctxT[:, t * P:(t + 1) * P], wk[:, :],
                                   start=True, stop=True)
                mm.then_inc(S["kv_ps"], 1)
                pe.wait_ge(S["kv_act"], 1 + b + 1)
                pe.wait_ge(S["kv_dve"], 1 + b + 1)
                def stack_T(gi, items):
                    for item in items:
                        pe.wait_ge(S["stack_ready"], 1 + 5 * gi + item + 1)
                        src, bk = ([KS] + QS)[item], (0, 1, 2, 3, 5)[item]
                        for t in range(NT):
                            mm = pe.transpose(bank(bk, t * P, (t + 1) * P), src[:, t, :], ident[:, :])
                        mm.then_inc(S["stack_T"], 1)

                def max_unit(gi, i):
                    t, n0, nh, at, width = MAX_UNITS[i]
                    n_keys = (t + 1) * P
                    if i >= 2:
                        pe.wait_ge(S["s_max"], 1 + MU * gi + i - 1)
                    for n in range(nh):
                        a = at + n * width
                        pe.matmul(PS[:, a + t * P:a + n_keys], identb[:, :], mask_qk[:, :],
                                  start=True, stop=False, skip_group_check=True)
                        mm = pe.matmul(PS[:, a:a + n_keys], QST[n0 + n][:, t * P:(t + 1) * P], KST[:, 0:n_keys],
                                       start=False, stop=True, skip_group_check=True)
                    mm.then_inc(S["s_ps"], 1)

                def prob_unit(gi, u, parts="scores maxima"):
                    j, n0, nh = PROB_UNITS[u]
                    n_q = (NT - j) * P
                    if "scores" in parts:
                        pe.wait_ge(S["pt_ready"], 1 + PU * gi + max(u - 1, 0))
                    for n in range(nh):
                        at = (4 + u % 2) * 512 + n * n_q
                        if "scores" in parts:
                            pe.matmul(PS[:, at:at + P], identb[:, :], mask_kq[:, :], start=True, stop=False,
                                      skip_group_check=True)
                            pe.matmul(PS[:, at:at + n_q], KST[:, j * P:(j + 1) * P], QST[n0 + n][:, j * P:T],
                                      start=False, stop=False, skip_group_check=True)
                        if "maxima" in parts:
                            mm = pe.matmul(PS[:, at:at + n_q], sel[:, n0 + n, :], RM[:, j * P:T], start=False,
                                           stop=True, skip_group_check=True)
                    if "maxima" in parts:
                        mm.then_inc(S["st_ps"], 1)

                def times_v(gi, *units):
                    for u in units:
                        j, n0, nh = PROB_UNITS[u]
                        if u == 0:
                            pe.wait_ge(S["v_ready"], 1 + gi + 1)
                        if u == 0:
                            pe.wait_ge(S["out_sb"], 1 + 2 * gi)
                            pe.wait_ge(S["sums_sb"], 1 + 2 * gi)
                        pe.wait_ge(S["pt_ready"], 1 + PU * gi + u + 1)
                        for n in range(n0, n0 + nh):
                            mm = pe.matmul(bank(6 + n // 2, j * P, T), V8[:, j, n * P:(n + 1) * P], PTj(j)[:, n, :],
                                           start=(j == 0 and n % 2 == 0), stop=(j == NT - 1), skip_group_check=True)
                        if u == PU - 1:
                            mm.then_inc(S["pv_ps"], 1)

                def divisors(gi, part):
                    if part == "sums":
                        pe.wait_ge(S["sums_sb"], 1 + 2 * (gi + 1))
                        for t in range(NT):
                            mm = pe.transpose(bank(0, t * P, (t + 1) * P), SUMS[:, t * P:(t + 1) * P], ident[:, :])
                        mm.then_inc(S["sums_T"], 1)
                    else:
                        pe.wait_ge(S["sums_inv"], 1 + gi + 1)
                        for t in range(NT):
                            mm = pe.matmul(bank(1, t * P, (t + 1) * P), RDB[:, t * HPG:(t + 1) * HPG, :].rearrange(
                                "p n d -> p (n d)"), ident[:, :], start=True, stop=True)
                        mm.then_inc(S["inv_ps"], 1)

                def open_group(gi):
                    prob_unit(gi, 0, "scores")
                    prob_unit(gi, 1, "scores")
                    pe.wait_ge(S["rm_ready"], 1 + gi + 1)
                    prob_unit(gi, 0, "maxima")
                    prob_unit(gi, 1, "maxima")

                def group(gi, following):
                    prob_unit(gi, 2)
                    times_v(gi, 0)
                    prob_unit(gi, 3)
                    prob_unit(gi, 4)
                    times_v(gi, 1)
                    prob_unit(gi, 5)
                    prob_unit(gi, 6)
                    times_v(gi, 2)
                    if following:
                        pe.wait_ge(S["o_ready"], 1 + gi)
                    for u in (7, 8, 9, 10):
                        prob_unit(gi, u)
                        if following and u > 7:
                            stack_T(gi + 1, (u - 8,))
                    if following:
                        stack_T(gi + 1, (3,))
                    times_v(gi, 3)
                    if following:
                        pe.wait_ge(S["pt_ready"], 1 + PU * gi + 10)
                        stack_T(gi + 1, (4,))
                    times_v(gi, 4)
                    if following:
                        pe.wait_ge(S["stack_sb_a"], 1 + 3 * (gi + 1) + 3)
                        pe.wait_ge(S["stack_sb_d"], 1 + 2 * (gi + 1) + 2)
                        max_unit(gi + 1, 0)
                        max_unit(gi + 1, 1)
                        times_v(gi, 5)
                        max_unit(gi + 1, 2)
                        times_v(gi, 6)
                        max_unit(gi + 1, 3)
                        times_v(gi, 7)
                        max_unit(gi + 1, 4)
                        times_v(gi, 8)
                        max_unit(gi + 1, 5)
                        times_v(gi, 9, 10)
                        rows_of_maxima(gi + 1)
                        open_group(gi + 1)
                    else:
                        times_v(gi, 5, 6, 7, 8, 9, 10)
                    divisors(gi, "sums")
                    if following:
                        divisors(gi, "inverses")

                def rows_of_maxima(gi):
                    pe.wait_ge(S["nm_ready"], 1 + gi + 1)
                    pe.transpose(bank(3, 0, P), NM2[:, :], ident[:, :]).then_inc(S["mt_ps"], 1)
                stack_T(b * G, range(5))
                pe.wait_ge(S["stack_sb_a"], 1 + 3 * b * G + 3)
                pe.wait_ge(S["stack_sb_d"], 1 + 2 * b * G + 2)
                for i in range(MU):
                    max_unit(b * G, i)
                rows_of_maxima(b * G)
                open_group(b * G)
                alone(pe, "pe")
                with pe.Fori(0, G - 1) as g:
                    group(b * G + g, True)
                group(b * G + G - 1, False)
                for k0, k1 in ((0, KC - 1), (KC - 1, KC)):
                    if k1 == KC:
                        divisors(b * G + G - 1, "inverses")
                    pe.wait_ge(S["oT_lo"], 1 + G * b + k1)
                    for t in range(NT):
                        sl = slice(t * P, (t + 1) * P)
                        for k in range(k0, k1):
                            mm = three(bank(2 + t), (OTH[:, k, sl], OTL[:, k, sl]), (woH[:, k, :], woL[:, k, :]),
                                       k == 0, k == KC - 1)
                        if k1 == KC:
                            mm.then_inc(S["op_ps"], 1)
                for t in range(NT):
                    pe.wait_ge(S["xn_ready"], 1 + NT * b + t + 1)
                    for k in range(KC):
                        mm = pe.transpose(bank(4 + t, k * P, (k + 1) * P), XN[:, t, k * P:(k + 1) * P], ident[:, :])
                    mm.then_inc(S["xT_ps"], 1)
                for t in range(NT):
                    pe.wait_ge(S["xT_lo"], 1 + NT * b + t + 1)
                    sl = slice(t * P, (t + 1) * P)
                    for k in range(KC):
                        mm = three(bank(t // 2, (t % 2) * 256, (t % 2) * 256 + PJ),
                                   (XTH[:, k, sl], XTL[:, k, sl]), (acH[:, k, :], acL[:, k, :]), k == 0, k == KC - 1)
                    if t % 2:
                        mm.then_inc(S["pj_ps"], 1)

                def gate_up(f, slot):
                    hi, lo = WHI[slot], WLO[slot]
                    pe.wait_ge(S["wg_lo"], 1 + b * NF + f + 1)
                    for h, (bk, free, done) in enumerate(((0, "sil_ready", "gate_ps"), (1, "hid_ready", "up_ps"))):
                        pe.wait_ge(S[free], 1 + b * NF + f)
                        for k in range(KC):
                            c0 = k * 2 * P + h * P
                            three(bank(bk), (hi[:, c0:c0 + P], lo[:, c0:c0 + P]), (XTH[:, k, :], XTL[:, k, :]),
                                  k == 0, False)
                        c0 = WBG + h * P
                        three(bank(bk), (hi[0:LR, c0:c0 + P], lo[0:LR, c0:c0 + P]), (LXH[:, h, :], LXL[:, h, :]),
                              False, True).then_inc(S[done], 1)

                def down(f, slot):
                    hi, lo = WHI[slot], WLO[slot]
                    pe.wait_ge(S["wd_lo"], 1 + b * NF + f + 1)
                    pe.wait_ge(S["hl_ready"], 1 + b * NF + f + 1)
                    for t in range(NT):
                        sl = slice(t * P, (t + 1) * P)
                        three(bank(2, t * LR, (t + 1) * LR), (HH[slot][:, sl], HL[slot][:, sl]),
                              (hi[:, WAD:WAD + LR], lo[:, WAD:WAD + LR]), False, False, skip_group_check=True)
                        mm = three(bank(4 + t), (HH[slot][:, sl], HL[slot][:, sl]),
                                   (hi[:, WD:WD + C], lo[:, WD:WD + C]), False, False, skip_group_check=True)
                    mm.then_inc(S["dn_ps"], 1)

                pe.wait_ge(S["lg_ready"], 1 + b + 1)
                for h in range(2):
                    for t in range(NT):
                        mm = pe.transpose(bank(6 + h, t * P, (t + 1) * P, parts=LR), LG[:, t, h, :], ident[:, :])
                    mm.then_inc(S["lx_ps"], 1)
                pe.wait_ge(S["lx_lo"], 1 + 2 * (b + 1))
                gate_up(0, 0)
                for bk in (2, 4, 5, 6, 7):
                    n = NT * LR if bk == 2 else 512
                    pe.matmul(bank(bk, 0, n), zrow[:, 0:P], zrow[:, 0:n], start=True, stop=False, skip_group_check=True)
                alone(pe, "pe")
                with pe.Fori(0, NF // 2) as i:
                    for d in (1, 2):
                        gate_up(2 * i + d, d % 2)
                        down(2 * i + d - 1, (d + 1) % 2)
                slot = (NF - 1) % 2
                hi, lo = WHI[slot], WLO[slot]
                pe.wait_ge(S["wd_lo"], 1 + b * NF + NF)
                pe.wait_ge(S["hl_ready"], 1 + b * NF + NF)
                for t in range(NT):
                    sl = slice(t * P, (t + 1) * P)
                    mm = three(bank(2, t * LR, (t + 1) * LR), (HH[slot][:, sl], HL[slot][:, sl]),
                               (hi[:, WAD:WAD + LR], lo[:, WAD:WAD + LR]), False, True, skip_group_check=True)
                mm.then_inc(S["ha_ps"], 1)
                for t in range(NT):
                    sl = slice(t * P, (t + 1) * P)
                    mm = three(bank(4 + t), (HH[slot][:, sl], HL[slot][:, sl]),
                               (hi[:, WD:WD + C], lo[:, WD:WD + C]), False, False, skip_group_check=True)
                mm.then_inc(S["dn_ps"], 1)
                pe.wait_ge(S["ld_ready"], 1 + b + 1)
                for t in range(NT):
                    mm = pe.transpose(bank(3, t * P, (t + 1) * P, parts=LR), LG[:, t, 0, :], ident[:, :])
                mm.then_inc(S["ld_ps"], 1)
                pe.wait_ge(S["ld_lo"], 1 + b + 1)
                for t in range(NT):
                    sl = slice(t * P, (t + 1) * P)
                    three(bank(4 + t), (LDH[:, sl], LDL[:, sl]), (bdH[:, :], bdL[:, :]), False, True,
                          skip_group_check=True).then_inc(S["ffn_ps"], 1)
                for t in range(NT):
                    pe.wait_ge(S["xn3_ready"], 1 + NT * b + t + 1)
                    for k in range(KC):
                        mm = pe.transpose(bank(t, k * P, (k + 1) * P), XN[:, t, k * P:(k + 1) * P], ident[:, :])
                    mm.then_inc(S["xT3_ps"], 1)
                pe.wait_ge(S["xT3_sb"], 1 + NT * (b + 1))
                for k in range(KC):
                    mm = pe.matmul(bank(4), KV[:, k, :], XTF[:, k, :], start=(k == 0), stop=(k == KC - 1))
                mm.then_inc(S["o1_ps"], 1)
                pe.wait_ge(S["o1_sb"], 1 + b + 1)
                for t in range(NT):
                    pe.matmul(bank(t), OT1[:, t * P:(t + 1) * P], KVT[:, :], start=True,
                              stop=True).then_inc(S["sim_ps"], 1)
                for t in range(NT):
                    pe.wait_ge(S["xn4_ready"], 1 + NT * b + t + 1)
                    for k in range(KC):
                        mm = pe.transpose(bank(4 + t, k * P, (k + 1) * P), HN[:, t, k * P:(k + 1) * P], ident[:, :])
                    mm.then_inc(S["xT4_ps"], 1)
                for t in range(NT):
                    pe.wait_ge(S["xT4_sb"], 1 + NT * b + t + 1)
                    for k in range(KC):
                        mm = pe.matmul(bank(0, t * E1, (t + 1) * E1), XTF[:, k, t * P:(t + 1) * P], rw[:, k, :],
                                       start=(k == 0), stop=(k == KC - 1))
                mm.then_inc(S["lgt_ps"], 1)
                pe.wait_ge(S["mk_ready"], 1 + b + 1)
                alone(pe, "pe")
                for t in range(NT):
                    mm = pe.transpose(bank(1, t * P, (t + 1) * P, parts=E1), MK[:, t, :], ident[:, :])
                mm.then_inc(S["mk_ps"], 1)
                pe.wait_ge(S["key_ready"], 1 + b + 1)
                pe.sem_inc(S["end_pe"], 1)

    place["at"] = part3_base
    LT = sb("LT", [P, E1])
    lv = sb("lv", [P, E1])
    NW, NX = 8, 8
    W1 = [sb(f"W1_{s}", [P, KC, 2 * F1]) for s in range(NW)]
    W2 = [sb(f"W2_{s}", [FH, 2, C]) for s in range(NW)]
    IDX1 = [sb(f"IDX1_{s}", [P, 1], U32) for s in range(NX)]
    XG = [sb(f"XG{s}", [P, HROW]) for s in range(NX)]
    XGT = [sb(f"XGT{s}", [P, KC, P]) for s in range(2)]
    WC = [sb(f"WC{s}", [P, 1]) for s in range(2)]
    SL = [sb(f"SL{s}", [P, F1]) for s in range(2)]
    HM = [sb(f"HM{s}", [P, F1]) for s in range(2)]
    HMT = [sb(f"HMT{s}", [FH, 2, P]) for s in range(2)]
    YE = [sb(f"YE{s}", [P, C]) for s in range(4)]
    lst_ready, lst_ps, idx_ready = sem("lst_ready"), sem("lst_ps"), sem("idx_ready")
    w1_loaded = [sem(f"w1_loaded{s}") for s in range(NW)]
    w2_loaded = [sem(f"w2_loaded{s}") for s in range(NW)]
    gathered = [sem(f"gathered{s}") for s in range(NX)]
    AHEAD = 4

    def experts(engine, body, start, stop):
        rounds = (stop - start) // NW

        def call(i, d):
            body((i * NW + start + d), (start + d) % NW, i + (start + d) // NW)
        with engine.Fori(0, rounds) as i:
            for d in range(NW):
                call(i, d)
        for e in range(start + rounds * NW, stop):
            body(e, e % NW, e // NW)

    with nc.Block() as block:
        @block.sync
        def _(sp):
            def load(e, s):
                sp.dma_start(W1[s][:, :, :], w["w1"][bass.ds(e * P, P), :].rearrange(
                    "p (k f) -> p k f", k=KC)).then_inc(w1_loaded[s], 16)
                sp.dma_start(W2[s][:, :, :], w["w2"][bass.ds(e * FH, FH), :].rearrange(
                    "p (h c) -> p h c", h=2)).then_inc(w2_loaded[s], 16)
            for s in range(NW):
                load(s, s)
            with sp.Fori(1, E1 // NW) as i:
                for s in range(NW):
                    sp.wait_ge(M["y_ps"], 1 + i * NW + s + 1 - NW)
                    alone(sp, "sp")
                    sp.wait_ge(w1_loaded[s], 16 * i)
                    sp.wait_ge(w2_loaded[s], 16 * i)
                    alone(sp, "sp")
                    load(i * NW + s, s)

        @block.gpsimd
        def _(pool):
            def gather(e, s):
                alone(pool, "pool")
                pool.tensor_copy(IDX1[s][:, :], IDX[:, bass.ds(e, 1)]).then_inc(M["idx"], 1)
                pool.wait_ge(M["idx"], 1 + e + 1)
                alone(pool, "pool")
                pool.indirect_dma_start(out=XG[s][:, :], out_offset=None, in_=hx,
                                        in_offset=bass.IndirectOffsetOnAxis(ap=IDX1[s][:, 0:1], axis=0),
                                        ).then_inc(gathered[s], 16)

            def scatter(e, s, first=False):
                if not first:
                    pool.wait_ge(scattered, 16 * e)
                    alone(pool, "pool")
                pool.sem_inc(M["added"], 1)
                pool.wait_ge(M["y_sb"], 1 + e + 1)
                alone(pool, "pool")
                pool.indirect_dma_start(out=out, out_offset=bass.IndirectOffsetOnAxis(ap=IDX1[s][:, 0:1], axis=0),
                                        in_=YE[s % 4][:, :], in_offset=None, compute_op=ALU.add,
                                        ).then_inc(scattered, 16)

            def expert(e, s, r):
                scatter(e, s)
                pool.wait_ge(M["hm"], 1 + e + AHEAD - NX + 1)
                gather(e + AHEAD, (s + AHEAD) % NX)
            pool.wait_ge(idx_ready, 1)
            for e in range(AHEAD):
                gather(e, e)
            for e in range(AHEAD):
                scatter(e, e, first=(e == 0))
                gather(e + AHEAD, e + AHEAD)
            alone(pool, "pool")
            experts(pool, expert, AHEAD, E1 - AHEAD)
            for e in range(E1 - AHEAD, E1):
                scatter(e, e % NX)
            pool.wait_ge(scattered, 16 * E1)

        @block.tensor
        def _(pe):
            def rows_T(e, s, r):
                pe.wait_ge(gathered[s], 16 * (r + 1))
                pe.wait_ge(M["xgt_sb"], 1 + e - 1 if not isinstance(e, int) or e > 1 else 1)
                for k in range(KC):
                    mm = pe.transpose(bank(s % 2, k * P, (k + 1) * P), XG[s][:, k * P:(k + 1) * P], ident[:, :])
                mm.then_inc(M["xgt_ps"], 1)

            def gate_up(e, s, r):
                pe.wait_ge(w1_loaded[s], 16 * (r + 1))
                pe.wait_ge(M["xgt_sb"], 1 + e + 1)
                pe.wait_ge(M["hm"], 1 + e - 1 if not isinstance(e, int) or e > 1 else 1)
                for k in range(KC):
                    mm = pe.matmul(bank(2 + s % 2, 0, 2 * F1), XGT[s % 2][:, k, :], W1[s][:, k, :], start=(k == 0),
                                   stop=(k == KC - 1))
                mm.then_inc(M["gu_ps"], 1)

            def hidden_T(e, s):
                pe.wait_ge(M["hm"], 1 + e + 1)
                pe.wait_ge(M["hmt_sb"], 1 + e)
                for h in range(2):
                    mm = pe.transpose(bank(4 + s % 2, h * P, (h + 1) * P, parts=FH), HM[s % 2][:, h * FH:(h + 1) * FH],
                                      ident[:, :])
                mm.then_inc(M["hmt_ps"], 1)

            def down(e, s, r):
                pe.wait_ge(w2_loaded[s], 16 * (r + 1))
                pe.wait_ge(M["hmt_sb"], 1 + e + 1)
                pe.wait_ge(M["y_sb"], 1 + e)
                for h in range(2):
                    mm = pe.matmul(bank(6 + s % 2), HMT[s % 2][:, h, :], W2[s][:, h, :], start=(h == 0), stop=(h == 1))
                mm.then_inc(M["y_ps"], 1)

            pe.wait_ge(lst_ready, 2)
            pe.transpose(bank(0, 0, E1), LST[:, :], ident[0:E1, 0:E1]).then_inc(lst_ps, 1)
            pe.wait_ge(idx_ready, 1)
            rows_T(0, 0, 0)
            gate_up(0, 0, 0)
            rows_T(1, 1, 0)

            def expert(e, s, r):
                last = isinstance(e, int) and e == E1 - 1
                gate_up(e, s, r)
                hidden_T(e - 1, (s - 1) % NW)
                if not last:
                    rows_T(e + 1, (s + 1) % NW, r + (s + 1) // NW)
                down(e - 1, (s - 1) % NW, r if s else r - 1)
            experts(pe, expert, 1, E1)
            hidden_T(E1 - 1, NW - 1)
            down(E1 - 1, NW - 1, E1 // NW - 1)

        @block.scalar
        def _(act):
            def rows_T(e, u):
                act.wait_ge(M["xgt_ps"], 1 + e + 1)
                act.wait_ge(M["gu_ps"], 1 + e - 1 if not isinstance(e, int) or e > 1 else 1)
                act.activation(XGT[u][:, :, :], bank(u).rearrange("p (k q) -> p k q", k=KC),
                               ACT.Copy).then_inc(M["xgt_sb"], 1)

            def silu(e, u):
                act.wait_ge(M["gu_ps"], 1 + e + 1)
                act.wait_ge(M["hm"], 1 + e - 1 if not isinstance(e, int) or e > 1 else 1)
                act.activation(SL[u][:, :], bank(2 + u, 0, F1), ACT.Silu).then_inc(M["sil"], 1)

            def down(e, s):
                act.wait_ge(M["y_ps"], 1 + e + 1)
                if not isinstance(e, int) or e > 3:
                    act.wait_ge(M["added"], 1 + e - 3)
                act.activation(YE[s % 4][:, :], bank(6 + s % 2), ACT.Copy).then_inc(M["y_sb"], 1)

            rows_T(0, 0)
            silu(0, 0)
            rows_T(1, 1)

            def expert(e, s, r):
                silu(e, s % 2)
                if not (isinstance(e, int) and e == E1 - 1):
                    rows_T(e + 1, (s + 1) % 2)
                down(e - 1, (s - 1) % NW)
            for e in range(1, 5):
                expert(e, e, 0)
            experts(act, expert, 5, E1)
            down(E1 - 1, NW - 1)

        @block.vector
        def _(dve):
            dve.tensor_copy(KEYS[0][:, 0:CAP], LST[:, :]).then_inc(lst_ready, 1)
            dve.wait_ge(lst_ready, 1)
            done = B * (NF // 2 - 1) * 2
            alone(dve, "dve")
            with dve.Fori(0, CAP // 16) as i:
                list_round(dve, done + i, i)
            dve.wait_ge(S["list_dve"], 6 * (done + CAP // 16))
            dve.memset(lv[:, :], 0.0).then_inc(lst_ready, 1)
            dve.wait_ge(lst_ps, 1)
            dve.wait_ge(lst_ready, 2)
            step = Chain(dve, S["list_dve"], 4, 6 * (done + CAP // 16))
            lt = bank(0, 0, E1)
            step(dve.tensor_scalar(lv[:, :], lt, 0.0, None, ALU.is_gt))
            step(dve.tensor_scalar(LT[:, :], lt, -1.0, float(2 * NTOK), ALU.mult, ALU.add))
            step(dve.tensor_scalar(LT[:, :], LT[:, :], dummy[:, 0:1], None, ALU.subtract))
            step(dve.tensor_tensor(LT[:, :], LT[:, :], lv[:, :], ALU.mult))
            dve.tensor_scalar(IDX[:, :], LT[:, :], dummy[:, 0:1], None, ALU.add).then_inc(idx_ready, 1)

            def gated(e, s, r):
                u = s % 2
                dve.wait_ge(M["hm"], 1 + e - 1 if not isinstance(e, int) or e > 1 else 1)
                dve.tensor_copy(WC[u][:, :], XG[s][:, bass.ds(C + e, 1)]).then_inc(M["wc"], 1)
                dve.wait_ge(M["wc"], 1 + e + 1)
                dve.wait_ge(M["sil"], 1 + e + 1)
                dve.scalar_tensor_tensor(out=HM[u][:, :], in0=SL[u][:, :], scalar=WC[u][:, 0:1],
                                         in1=bank(2 + u, F1, 2 * F1), op0=ALU.mult,
                                         op1=ALU.mult).then_inc(M["hm"], 1)

            def hidden_T(e, u):
                dve.wait_ge(M["hmt_ps"], 1 + e + 1)
                dve.wait_ge(M["y_ps"], 1 + e - 1 if not isinstance(e, int) or e > 1 else 1)
                dve.tensor_copy(HMT[u][:, :, :], bank(4 + u, 0, 2 * P, parts=FH).rearrange(
                    "p (h q) -> p h q", h=2)).then_inc(M["hmt_sb"], 1)
            dve.wait_ge(gathered[0], 16)
            gated(0, 0, 0)

            def expert(e, s, r):
                hidden_T(e - 1, (s - 1) % 2)
                dve.wait_ge(gathered[s], 16 * (r + 1))
                gated(e, s, r)
            experts(dve, expert, 1, E1)
            hidden_T(E1 - 1, 1)


BY_DMA = {"x_loaded", "ctx_loaded", "hx_stored", "out_stored", "dve_step", "g_dve", "g_pool", "list_dve", "f_dve", "rev_loaded"}
KSTEPS = {"f_dve": 38, "dve": 102, "pool": 0, "act": 0, "g_dve": 3, "g_pool": 5}


def shape_constants():
    import numpy as np
    p = np.arange(P)
    c = {}
    c["ident"] = np.eye(P, dtype=np.float32)
    bf = mybir.dt.np(BF16)
    c["identb"] = np.eye(P).astype(bf)
    later = p[None, :] > p[:, None]
    c["mask_qk"] = np.where(later, -1e30, 0.0).astype(bf)
    c["mask_kq"] = np.where(later.T, -1e30, 0.0).astype(bf)
    c["iota8"] = np.tile(np.arange(E0, dtype=np.float32), (P, 1))
    c["dummy"] = (NTOK + p).astype(np.float32)[:, None]
    c["revt"] = np.tile(2 * NTOK - np.arange(NTOK, dtype=np.float32), (E1, 1))
    r = p % 32
    live = (r < NT * HPG) & (p < 64)
    c["blockmask"] = ((r[:, None] // HPG == np.arange(NT)) & live[:, None]).astype(np.float32)[:, :, None] * np.ones(
        (1, 1, P), np.float32)
    c["sel"] = ((r[:, None] % HPG == np.arange(HPG)) & live[:, None]).astype(np.float32)[:, :, None] * np.ones(
        (1, 1, P), np.float32)
    inv = (np.float32(1.0) / np.float32(10000.0) ** (np.arange(0, HD, 2, dtype=np.float32) / np.float32(HD)))
    fr = np.outer(np.arange(T, dtype=np.float32), inv.astype(np.float32)).astype(np.float32)
    emb = np.concatenate([fr, fr], -1)
    cos, sin = np.cos(emb.astype(np.float64)), np.sin(emb.astype(np.float64))
    sin = sin * np.where(np.arange(HD) < ROT, -1.0, 1.0)
    tiled = lambda a: np.ascontiguousarray(a.astype(np.float32).reshape(NT, P, HD).transpose(1, 0, 2))
    scale = float(HD) ** -0.5
    c["cos_q"], c["sin_q"], c["cos_k"], c["sin_k"] = tiled(cos * scale), tiled(sin * scale), tiled(cos), tiled(sin)
    return c


def lay_out(i):
    import numpy as np
    a = {k: np.asarray(v) for k, v in i.items()}
    kp = lambda m: np.ascontiguousarray(m.reshape(KC, P, -1).transpose(1, 0, 2))
    o = {}
    o["wo"] = kp(a["L0_xattn_w_out"].T)
    ex = lambda m: m.transpose(1, 0, 2).reshape(m.shape[1], -1)
    o["acat"] = kp(np.concatenate([a["L0_ffn_W_router"], a["L0_ffn_sA_gate"], ex(a["L0_ffn_A_gate"]),
                                   a["L0_ffn_sA_up"], ex(a["L0_ffn_A_up"])], 1))
    rowsb = lambda s, m: np.concatenate([s, m.reshape(E0 * R0, -1)], 0)
    o["bdown"] = np.ascontiguousarray(rowsb(a["L0_ffn_sB_down"], a["L0_ffn_B_down"]))
    st = np.zeros((NF, P, WCOLS), np.float32)
    bg, bu = rowsb(a["L0_ffn_sB_gate"], a["L0_ffn_B_gate"]), rowsb(a["L0_ffn_sB_up"], a["L0_ffn_B_up"])
    ad = np.concatenate([a["L0_ffn_sA_down"], ex(a["L0_ffn_A_down"])], 1)
    for f in range(NF):
        f0, f1 = f * P, min((f + 1) * P, DFF)
        n = f1 - f0
        for h, m in enumerate((a["L0_ffn_W_gate"], a["L0_ffn_W_up"])):
            for k in range(KC):
                st[f, :, k * 2 * P + h * P:k * 2 * P + h * P + n] = m[k * P:(k + 1) * P, f0:f1]
        st[f, 0:n, WD:WD + C] = a["L0_ffn_W_down"][f0:f1]
        st[f, 0:LR, WBG:WBG + n] = bg[:, f0:f1]
        st[f, 0:LR, WBU:WBU + n] = bu[:, f0:f1]
        st[f, 0:n, WAD:WAD + LR] = ad[f0:f1]
    o["ffn"] = st.reshape(NF * P, WCOLS)
    o["wk"] = np.ascontiguousarray(a["L1_xattn_W_k"].T)
    o["rw"] = kp(a["L1_ffn_router_w"].T)
    o["bk"], o["gamma"], o["beta"] = a["L1_xattn_b_k"], a["L1_xattn_ln_gamma"], a["L1_xattn_ln_beta"]
    o["ebias"], o["wq"], o["wkn"] = a["L0_ffn_expert_bias"], a["L0_xattn_q_norm_w"], a["L0_xattn_k_norm_w"]
    gu = np.concatenate([a["L1_ffn_w_gate"], a["L1_ffn_w_up"]], 2)
    o["w1"] = np.ascontiguousarray(gu.reshape(E1, KC, P, 2 * F1).transpose(0, 2, 1, 3)).reshape(E1 * P, -1)
    o["w2"] = np.ascontiguousarray(a["L1_ffn_w_down"].reshape(E1, 2, FH, C).transpose(0, 2, 1, 3)).reshape(
        E1 * FH, -1)
    o["x"] = np.concatenate([a["x"].reshape(NTOK, C), np.zeros((T, C), np.float32)], 0)
    o["ctx"] = np.concatenate([a["ctx_512"].reshape(NTOK, CKV), np.zeros((T, CKV), np.float32)], 0)
    return o


def kernel(**inputs):
    import numpy as np
    import concourse.bacc as bacc
    from concourse.bass_utils import run_bass_kernel_spmd as run

    nc = bacc.Bacc("TRN2", target_bir_lowering=False, num_devices=1)
    arrays = {"in_" + k: np.ascontiguousarray(v) for k, v in {**lay_out(inputs), **shape_constants()}.items()}
    ap = {k[3:]: nc.dram_tensor(k, v.shape, mybir.dt.from_np(v.dtype), kind="ExternalInput").ap()
          for k, v in arrays.items()}
    out = nc.dram_tensor("out", (ROWS, C), F32, kind="ExternalOutput").ap()
    hx = nc.dram_tensor("hx", (ROWS, HROW), F32, kind="Internal").ap()
    build(nc, ap["x"], ap["ctx"], ap, out, hx)
    r = run(nc, [arrays], core_ids=[0])
    return r.results[0]["out"][0:NTOK].reshape(B, T, C)
```

```python
import concourse.bass as bass
from concourse import mybir

F32 = mybir.dt.float32
F32R = mybir.dt.float32r
BF16 = mybir.dt.bfloat16
U32 = mybir.dt.uint32
ALU = mybir.AluOpType
ACT = mybir.ActivationFunctionType
AX = mybir.AxisListType.X

P = 128
B, T, C = 4, 512, 512
NT = T // P
KC = C // P
H, G = 16, 4
HPG = H // G
HD = C // H
CKV = G * HD
ROT = HD // 2
E0, R0 = 8, 8
LR = R0 * (E0 + 1)
DFF = 1376
NF = -(-DFF // P)
PJ = E0 + 2 * LR
WBG = KC * 2 * P
WBU, WD = WBG + P, WBG + 2 * P
WAD = WD + C
WCOLS = WAD + LR
E1, K1, F1, CAP = 64, 8, 192, 128
FH = F1 // 2
NTOK = B * T
ROWS = NTOK + P
HROW = C + E1
ABSENT = -3.0e38
EPS_LN, EPS_RMS, EPS_SIM = 1e-5, 1e-5, 1e-6


class Chain:

    def __init__(self, engine, sem, per, base=0):
        self.engine, self.sem, self.per, self.base, self.n = engine, sem, per, base, 0

    def __call__(self, instruction):
        self.n += 1
        instruction.then_inc(self.sem, 1)
        self.engine.wait_ge(self.sem, self.base + self.n)

    def post(self, instruction):
        self.n += 1
        instruction.then_inc(self.sem, 1)
        return self.n

    def need(self, n):
        self.engine.wait_ge(self.sem, self.base + n)

    def end(self):
        assert self.n == self.per, (self.sem, self.n, self.per)


def build(nc, x, ctx_in, w, out, hx):
    place = {"at": 16896}

    def sb(name, shape, dt=F32):
        size = 1
        for s in shape[1:]:
            size *= s
        size = -(-size * mybir.dt.size(dt) // 32) * 32
        t = nc.alloc_sbuf_tensor_at(name, shape, dt, offset=place["at"])
        place["at"] += size
        assert place["at"] <= 229344, (name, place["at"])
        return t

    def sem(name):
        return nc.alloc_semaphore(name)

    PS = nc.alloc_psum_tensor("PS", [P, 8 * 512], F32)

    def bank(i, a=0, b=512, parts=P):
        return PS[0:parts, i * 512 + a:i * 512 + b]

    projected = PS[:, 2 * 512:4 * 512].rearrange("p (t c) -> p t c", t=NT)[:, :, 0:PJ]

    ident = sb("ident", [P, P])
    identb = sb("identb", [P, P], BF16)
    mask_qk = sb("mask_qk", [P, P], BF16)
    mask_kq = sb("mask_kq", [P, P], BF16)
    zrow = sb("zrow", [1, 512], BF16)
    dummy = sb("dummy", [P, 1])
    revt = sb("revt", [E1, T])
    KEYS = [sb(f"KEYS{i}", [E1, CAP + T]) for i in range(2)]
    LST = sb("LST", [E1, CAP])
    next8 = sb("next8", [E1, 8])
    mhalf = sb("mhalf", [P, 8])
    IDX = sb("IDX", [P, E1], U32)
    part3_base = place["at"]
    blockmask = sb("blockmask", [P, NT, P])
    sel = sb("sel", [P, HPG, P], F32R)
    cosw = sb("cosw", [P, NT, C])
    sinw = sb("sinw", [P, NT, C])
    cosk = sb("cosk", [P, NT, CKV])
    sink = sb("sink", [P, NT, CKV])
    woH = sb("woH", [P, KC, C], F32R)
    woL = sb("woL", [P, KC, C], F32R)
    acH = sb("acH", [P, KC, PJ], F32R)
    acL = sb("acL", [P, KC, PJ], F32R)
    bdH = sb("bdH", [LR, C], F32R)
    bdL = sb("bdL", [LR, C], F32R)
    wk = sb("wk", [CKV, CKV])
    bk_col = sb("bk_col", [P, 1])
    gam = sb("gam", [P, T])
    bet = sb("bet", [P, T])
    ebias = sb("ebias", [P, E0])
    rw = sb("rw", [P, KC, E1])
    X = sb("X", [P, NT, C])
    XIN = sb("XIN", [P, NT, C])
    CTX = sb("CTX", [P, NT, CKV])
    KVT = sb("KVT", [P, T])
    KV = sb("KV", [P, NT, CKV])
    V8 = sb("V8", [P, NT, HPG * (P + HD)])
    ST6 = sb("ST6", [P, NT, 6])
    MV = sb("MV", [P, NT, 2])
    sm = [sb(f"sm{i}", [P, NT]) for i in range(6)]
    XN = sb("XN", [P, NT, C])
    QR = sb("QR", [P, NT, C])
    KR = sb("KR", [P, NT, CKV])
    FST6 = sb("FST6", [P, 2 * NT, 6])
    FMV = sb("FMV", [P, 2 * NT, 2])
    fvar, finv = sb("fvar", [P, 2 * NT]), sb("finv", [P, 2 * NT])
    fvar2, fscale, fms = sb("fvar2", [P, NT]), sb("fscale", [P, NT]), sb("fms", [P, NT])
    XW, QA, QB = XN[:, 0, :], XN[:, 1, :], XN[:, 2, :]
    FIRST_QAB = ((QA, QB), (X[:, 0, :], X[:, 1, :]))
    region = place["at"]
    OTH = sb("OTH", [P, KC, T], F32R)
    OTL = sb("OTL", [P, KC, T], F32R)
    Y = sb("Y", [P, NT, T])
    HN = sb("HN", [P, NT, HROW])
    KS = sb("KS", [P, NT, P])
    QS = [sb(f"QS{n}", [P, NT, P]) for n in range(HPG)]
    KST = sb("KST", [P, T], F32R)
    QST = [sb(f"QST{n}", [P, T], F32R) for n in range(HPG)]
    NM = sb("NM", [P, NT * HPG])
    NM2 = sb("NM2", [P, P])
    RM = sb("RM", [P, T], F32R)
    SUMS = sb("SUMS", [P, T])
    UN = sb("UN", [P, T])
    RD = sb("RD", [P, NT * HPG])
    RDB = sb("RDB", [P, NT * HPG, HD])
    PT = sb("PT", [P, 10, P * HPG])
    OT = sb("OT", [P, G, T])
    pt_at = [0, 4, 7, 9]

    def PTj(j):
        return PT[:, pt_at[j]:pt_at[j] + NT - j, :].rearrange("p a b -> p (a b)").rearrange(
            "p (n q) -> p n q", n=HPG)

    place["at"] = region
    XTH = sb("XTH", [P, KC, T], F32R)
    XTL = sb("XTL", [P, KC, T], F32R)
    WRAW = [sb(f"WRAW{s}", [P, WCOLS]) for s in range(2)]
    WHI = [sb(f"WHI{s}", [P, WCOLS], F32R) for s in range(2)]
    WLO = [sb(f"WLO{s}", [P, WCOLS], F32R) for s in range(2)]
    SIL = sb("SIL", [P, T])
    HID = sb("HID", [P, T])
    HH = [sb(f"HH{s}", [P, T], F32R) for s in range(2)]
    HL = [sb(f"HL{s}", [P, T], F32R) for s in range(2)]
    LG = sb("LG", [P, NT, 2, LR])
    LXH = sb("LXH", [LR, 2, T], F32R)
    LXL = sb("LXL", [LR, 2, T], F32R)
    LDH = sb("LDH", [LR, T], F32R)
    LDL = sb("LDL", [LR, T], F32R)
    r8 = [sb(f"r8_{i}", [P, NT, E0]) for i in range(4)]
    top2 = sb("top2", [P, NT, 8])
    WX = sb("WX", [P, NT, LR])
    WXT = sb("WXT", [LR, T])
    LD = sb("LD", [LR, T])
    place["at"] = region
    XTF = sb("XTF", [P, KC, T])
    OT1 = sb("OT1", [P, T])
    SC = sb("SC", [P, NT, E1])
    SR = sb("SR", [P, NT, E1])
    MK = sb("MK", [P, NT, E1])
    t8 = sb("t8", [P, NT, 8])
    nmx = sb("nmx", [P, NT])
    ssum = sb("ssum", [P, NT])
    assert place["at"] <= region + 2 * KC * T * 4
    place["at"] = region
    wq_bc = sb("wq_bc", [P, C])
    wkn_bc = sb("wkn_bc", [P, CKV])
    cq = sb("cq", [P, NT, HD])
    sq = sb("sq", [P, NT, HD])
    ck = sb("ck", [P, NT, HD])
    sk = sb("sk", [P, NT, HD])
    wo_raw = sb("wo_raw", [P, KC, C])
    ac_raw = sb("ac_raw", [P, KC, PJ])
    bd_raw = sb("bd_raw", [LR, C])
    sel_raw = sb("sel_raw", [P, HPG, P])
    ZR = sb("ZR", [P, HROW])
    assert place["at"] <= region + 2 * KC * T * 4 + (T + HROW) * NT * 4

    def cols(g, width, at=0, n=None):
        n = width if n is None else n
        return slice(g * width + at, g * width + at + n) if isinstance(g, int) else bass.ds(g * width + at, n)

    def span(e, n):
        return slice(e * n, (e + 1) * n) if isinstance(e, int) else bass.ds(e * n, n)

    def row(g):
        return slice(g, g + 1) if isinstance(g, int) else bass.ds(g, 1)

    def rows(ap, n):
        return ap.rearrange("(t p) c -> p t c", p=P)

    def bcast(ap, n):
        return ap.rearrange("(a n) -> a n", a=1).broadcast_to([P, n])

    names = ("x_loaded ctx_loaded rev_loaded f_in f_out f_dve alone_dve alone_pool alone_pe alone_sp "
             "qab_ready q_ready k_ready norm_in norm_out ctxT_ps ctxT_sb kvT_ps kv_ps kv_act kv_row "
             "stack_ready stack_T stack_sb_a stack_sb_d v_ready s_ps s_max nm_ready mt_ps rm_ready "
             "st_ps pt_ready pv_ps sums_sb out_sb sums_T sums_inv inv_ps o_ready "
             "oT_hi oT_lo oT_last_hi oT_last_lo op_ps x1_ready "
             "xn_ready xT_ps xT_hi xT_lo pj_ps sig_ready lg_ready lx_ps lx_hi lx_lo wxT_ps wxT_sb "
             "wg_hi wg_lo wd_hi wd_lo gate_ps up_ps sil_ready hid_ready hh_ready hl_ready dn_ps ha_ps "
             "ld_ready ld_hi ld_lo ffn_ps x2_ready "
             "xn3_ready xT3_ps xT3_sb o1_ps o1_sb sim_ps y_ready e_ready x3_ready "
             "xn4_ready xT4_ps xT4_sb lgt_ps lgt_max lgt_exp mk_ready mk_ps key_ready "
             "hx_stored out_stored dve_step  g_dve g_pool list_dve").split()
    S = {n: sem(n) for n in names}
    w_loaded = [sem("w_loaded0"), sem("w_loaded1")]
    M = {n: sem("m_" + n) for n in ("idx xgt_ps xgt_sb gu_ps sil wc hm hmt_ps hmt_sb y_ps y_sb added".split())}
    scattered = sem("scattered")
    tables_loaded, setup_loaded, setup_dve, setup_act, tables_made = (sem(n) for n in (
        "tables_loaded", "setup_loaded", "setup_dve", "setup_act", "tables_made"))
    CONSTANTS = [(ident, w["ident"]), (identb, w["identb"]), (mask_qk, w["mask_qk"]), (mask_kq, w["mask_kq"]),
                 (dummy, w["dummy"]), (blockmask, w["blockmask"]), (sel_raw, w["sel"]), (wk, w["wk"]),
                 (rw, w["rw"]), (wo_raw, w["wo"]), (ac_raw, w["acat"]), (bd_raw, w["bdown"])]
    SETUP_LOADED = 16 * (len(CONSTANTS) + 4)
    DVE_B, DVE_G, POOL_G = KSTEPS["dve"], KSTEPS["g_dve"], KSTEPS["g_pool"]

    POOL_TABLES = 2

    def rotary_table(engine, kind, t):
        tab_c, tab_s, wt, c_, s_, nh = {"q": (cosw, sinw, wq_bc, cq, sq, H), "k": (cosk, sink, wkn_bc, ck, sk, G)}[kind]

        def heads(ap, a, b):
            return ap.rearrange("p (h d) -> p h d", h=nh)[:, :, a:b]

        def table(ap, a, b):
            return ap[:, t, a:b].unsqueeze(1).broadcast_to([P, nh, b - a])
        yield engine.tensor_tensor(heads(tab_c[:, t, :], 0, HD), heads(wt[:, :], 0, HD), table(c_, 0, HD), ALU.mult)
        yield engine.tensor_tensor(heads(tab_s[:, t, :], 0, ROT), heads(wt[:, :], ROT, HD), table(s_, 0, ROT), ALU.mult)
        yield engine.tensor_tensor(heads(tab_s[:, t, :], ROT, HD), heads(wt[:, :], 0, ROT), table(s_, ROT, HD), ALU.mult)

    def alone(engine, name):
        engine.sem_inc(S["alone_" + name], 1)

    def list_round(dve, n, c):
        step = Chain(dve, S["list_dve"], 6, n * 6)
        for h in range(2):
            src, dst = KEYS[h], KEYS[1 - h]
            alone(dve, "dve")
            step(dve.max(next8[:, :], src[:, :]))
            alone(dve, "dve")
            step(dve.match_replace(dst[:, :], next8[:, :], src[:, :], -1.0))
            step(dve.tensor_copy(LST[:, bass.ds(16 * c + 8 * h, 8)], next8[:, :]))
        step.end()

    MAX_UNITS = [(3, 0, 2, 0, 512), (3, 2, 2, 1024, 512), (2, 0, 2, 0, 512), (2, 2, 2, 1024, 512),
                 (1, 0, 4, 0, 256), (0, 0, 4, 1024, 128)]
    PROB_UNITS = [(0, n, 1) for n in range(HPG)] + [(1, n, 1) for n in range(HPG)] + [(2, 0, 2), (2, 2, 2), (3, 0, 4)]
    FIRST_STACKS = ((0, 4), (1, 6), (2, 7), (3, 4), (4, 6))
    ACT_STACKS, DVE_STACKS = 5 + 3 * (G - 1), 2 * (G - 1)
    MU, PU = len(MAX_UNITS), len(PROB_UNITS)

    with nc.Block() as block:
        @block.sync
        def _(sp):
            def load_batch(b):
                ctx_rows, x_rows = ((ap[b * T:(b + 1) * T, :] if isinstance(b, int) else ap[bass.ds(b * T, T), :])
                                    for ap in (ctx_in, x))
                sp.dma_start(CTX[:, :, :], rows(ctx_rows, NT)).then_inc(S["ctx_loaded"], 16)
                sp.dma_start(XIN[:, :, :], rows(x_rows, NT)).then_inc(S["x_loaded"], 16)
            load_batch(0)
            for dst, src in ((cq, w["cos_q"]), (sq, w["sin_q"]), (ck, w["cos_k"]), (sk, w["sin_k"])):
                sp.dma_start(dst[:, :, :], src).then_inc(tables_loaded, 16)
            for dst, src, n in ((wq_bc, w["wq"], C), (wkn_bc, w["wkn"], CKV)):
                sp.dma_start(dst[:, :], bcast(src, n)).then_inc(tables_loaded, 16)
            for dst, src in CONSTANTS:
                sp.dma_start(dst[(slice(None),) * len(src.shape)], src).then_inc(setup_loaded, 16)
            sp.dma_start(bk_col[:, :], w["bk"].rearrange("(p a) -> p a", a=1)).then_inc(setup_loaded, 16)
            for dst, src, n in ((gam, w["gamma"], T), (bet, w["beta"], T), (ebias, w["ebias"], E0)):
                sp.dma_start(dst[:, :], bcast(src, n)).then_inc(setup_loaded, 16)
            sp.wait_ge(setup_dve, 1)
            sp.dma_start(hx[NTOK:ROWS, :], ZR[:, :]).then_inc(S["hx_stored"], 16)
            sp.dma_start(out[NTOK:ROWS, :], ZR[:, 0:C]).then_inc(S["out_stored"], 16)
            with sp.Fori(0, B) as b:
                sp.wait_ge(S["v_ready"], 1 + G * (b + 1))
                alone(sp, "sp")
                sp.wait_ge(S["x1_ready"], 1 + NT * (b + 1))
                alone(sp, "sp")
                sp.dma_start(WRAW[0][:, :], w["ffn"][0:P, :]).then_inc(w_loaded[0], 16)
                sp.dma_start(WRAW[1][:, :], w["ffn"][P:2 * P, :]).then_inc(w_loaded[1], 16)
                load_batch(b + 1)
                sp.dma_start(revt[:, :], w["revt"][:, bass.ds(b * T, T)]).then_inc(S["rev_loaded"], 16)

                def load_w(f, slot):
                    sp.wait_ge(S["wg_hi"], 1 + b * NF + f - 1)
                    sp.wait_ge(S["wg_lo"], 1 + b * NF + f - 1)
                    sp.wait_ge(S["wd_hi"], 1 + b * NF + f - 1)
                    sp.wait_ge(S["wd_lo"], 1 + b * NF + f - 1)
                    alone(sp, "sp")
                    sp.dma_start(WRAW[slot][:, :], w["ffn"][bass.ds(f * P, P), :]).then_inc(w_loaded[slot], 16)
                with sp.Fori(1, NF // 2) as i:
                    load_w(2 * i, 0)
                    load_w(2 * i + 1, 1)
                load_w(NF - 1, 0)
                sp.wait_ge(S["key_ready"], 1 + b + 1)
                alone(sp, "sp")
                sp.dma_start(rows(hx[bass.ds(b * T, T), :], NT), HN[:, :, :]).then_inc(S["hx_stored"], 16)
                sp.dma_start(rows(out[bass.ds(b * T, T), :], NT), X[:, :, :]).then_inc(S["out_stored"], 16)
            sp.wait_ge(S["hx_stored"], 16 * (B + 1))
            sp.wait_ge(S["out_stored"], 16 * (B + 1))

        @block.gpsimd
        def _(pool):
            for name in S:
                if name not in BY_DMA:
                    pool.sem_inc(S[name], 1)
            for name in M:
                pool.sem_inc(M[name], 1)

            def front_power(fb, n):
                pool.wait_ge(S["f_in"], 1 + 2 * fb + n)
                if n == 1:
                    ins = pool.tensor_tensor(finv[:, :], fvar[:, :], mhalf[:, :], ALU.pow)
                else:
                    ins = pool.tensor_tensor(fms[:, :], fvar2[:, :], mhalf[:, 0:NT], ALU.pow)
                ins.then_inc(S["f_out"], 1)

            def front_q(fb, t, qab=(QA, QB)):
                pool.wait_ge(S["qab_ready"], 1 + NT * fb + t + 1)
                if not isinstance(t, int):
                    alone(pool, "pool")
                pool.tensor_tensor(QR[:, row(t), :], qab[0].unsqueeze(1), qab[1].unsqueeze(1), ALU.add).then_inc(S["q_ready"], 1)
            gstep = Chain(pool, S["g_pool"], POOL_G)

            def stacks(gi, g):
                gstep.base, gstep.n = gi * POOL_G, 0
                pool.wait_ge(S["stack_T"], 1 + 5 * gi)
                kin = KR[:, :, cols(g, HD)].unsqueeze(2).broadcast_to([P, NT, 2, HD])
                ks = KS[:, :, :].rearrange("p t (r s d) -> p t r s d", r=2, s=2)
                alone(pool, "pool")
                gstep(pool.tensor_copy(ks[:, :, :, 0, :].bitcast(F32R), kin))
                alone(pool, "pool")
                pool.tensor_tensor(ks[:, :, :, 1, :], kin, ks[:, :, :, 0, :], ALU.subtract).then_inc(S["stack_ready"], 1)
                for n in range(HPG):
                    qin = QR[:, :, cols(g, P, n * HD, HD)].unsqueeze(2).broadcast_to([P, NT, 2, HD])
                    qs = QS[n][:, :, :].rearrange("p t (s r d) -> p t s r d", r=2, s=2)
                    gstep(pool.tensor_copy(qs[:, :, 0, :, :].bitcast(F32R), qin))
                    alone(pool, "pool")
                    pool.tensor_tensor(qs[:, :, 1, :, :], qin, qs[:, :, 0, :, :], ALU.subtract).then_inc(S["stack_ready"], 1)
                gstep.end()

            def values(gi, g):
                pool.wait_ge(S["pv_ps"], 1 + gi)
                alone(pool, "pool")
                diagonal = V8[:, :, :].rearrange("p t (n c) -> p t n c", c=P + HD)[:, :, :, 0:HD]
                pool.tensor_copy(diagonal, CTX[:, :, cols(g, HD)].unsqueeze(2).broadcast_to(
                    [P, NT, HPG, HD])).then_inc(S["v_ready"], 1)

            def first_group(fb):
                pool.wait_ge(S["q_ready"], 1 + NT * (fb + 1))
                pool.wait_ge(S["k_ready"], 1 + fb + 1)
                stacks(fb * G, 0)
                values(fb * G, 0)
            front_power(0, 1)
            front_power(0, 2)
            pool.wait_ge(tables_loaded, 16 * 6)
            for t in range(NT - POOL_TABLES, NT):
                for operation in rotary_table(pool, "q", t):
                    operation.then_inc(tables_made, 1)
            for t in range(NT):
                front_q(0, t, FIRST_QAB[t % len(FIRST_QAB)])
            first_group(0)
            with pool.Fori(0, B) as b:

                def power(n):
                    pool.wait_ge(S["norm_in"], 1 + 4 * b + n)
                    pool.tensor_tensor(sm[1][:, :], sm[0][:, :], mhalf[:, 0:NT], ALU.pow).then_inc(S["norm_out"], 1)
                def split_output(gi, g):
                    pool.wait_ge(S["o_ready"], 1 + gi + 1)
                    alone(pool, "pool")
                    pool.tensor_copy(OTH[:, row(g), :], OT[:, row(g), :]).then_inc(S["oT_hi"], 1)
                    pool.wait_ge(S["oT_hi"], 1 + (G - 1) * b + g + 1)
                    alone(pool, "pool")
                    pool.tensor_tensor(OTL[:, row(g), :], OT[:, row(g), :], OTH[:, row(g), :],
                                       ALU.subtract).then_inc(S["oT_lo"], 1)
                stacks(b * G + 1, 1)
                alone(pool, "pool")
                with pool.Fori(0, G - 2) as g:
                    stacks(b * G + g + 2, g + 2)
                    values(b * G + g + 1, g + 1)
                    split_output(b * G + g, g)
                values(b * G + G - 1, G - 1)
                split_output(b * G + G - 2, G - 2)
                pool.wait_ge(S["oT_lo"], 1 + (G - 1) * (b + 1))
                power(1)
                def hidden(f, slot):
                    pool.wait_ge(S["hid_ready"], 1 + b * NF + f + 1)
                    pool.wait_ge(S["dn_ps"], 1 + b * NF + f - 1)
                    hid_split(slot)

                def hid_split(slot):
                    alone(pool, "pool")
                    pool.tensor_copy(HH[slot][:, :], HID[:, :]).then_inc(S["hh_ready"], 1)

                def hidden_tail(f, slot):
                    pool.wait_ge(S["hh_ready"], 1 + b * NF + f + 1)
                    pool.tensor_tensor(HL[slot][:, :], HID[:, :], HH[slot][:, :], ALU.subtract).then_inc(S["hl_ready"], 1)
                pool.wait_ge(S["hid_ready"], 1 + b * NF + 1)
                pool.wait_ge(S["dn_ps"], 1 + b * NF)
                hid_split(0)
                hidden_tail(0, 0)
                front_power(b + 1, 1)

                def two_chunks(i):
                    for d in (1, 2):
                        hidden(2 * i + d, d % 2)
                        hidden_tail(2 * i + d, d % 2)
                        if d == 1 and isinstance(i, int):
                            front_power(b + 1, 2)
                    front_q(b + 1, i)
                two_chunks(0)
                alone(pool, "pool")
                with pool.Fori(1, NF // 2 - 1) as i:
                    two_chunks(i)
                for f in (NF - 2, NF - 1):
                    hidden(f, f % 2)
                    hidden_tail(f, f % 2)
                power(2)
                first_group(b + 1)
                power(3)
                power(4)
                pool.wait_ge(S["norm_out"], 1 + 4 * (b + 1))

        @block.scalar
        def _(act):
            act.wait_ge(setup_loaded, SETUP_LOADED)
            for dst, src in ((woH, wo_raw), (acH, ac_raw), (sel, sel_raw)):
                act.activation(dst[:, :, :], src[:, :, :], ACT.Copy).then_inc(setup_act, 1)
            act.activation(bdH[:, :], bd_raw[:, :], ACT.Copy).then_inc(setup_act, 1)

            def first_group(fb):
                act.wait_ge(S["ctxT_ps"], 1 + fb + 1)
                act.activation(XN[:, 3, :], bank(5), ACT.Copy).then_inc(S["ctxT_sb"], 1)
                for item, bk in FIRST_STACKS:
                    if item == 3:
                        act.wait_ge(S["kvT_ps"], 1 + fb + 1)
                        act.activation(KVT[:, :], bank(5), ACT.Identity, bias=bk_col[:, 0:1]).then_inc(S["kv_act"], 1)
                    act.wait_ge(S["stack_T"], 1 + 5 * G * fb + item + 1)
                    act.activation(([KST] + QST)[item][:, :], bank(bk), ACT.Copy).then_inc(S["stack_sb_a"], 1)
                act.wait_ge(S["kv_ps"], 1 + fb + 1)
                act.activation(KV[:, :, :], bank(7).rearrange("p (t d) -> p t d", t=NT),
                               ACT.Copy).then_inc(S["kv_row"], 1)
            first_group(0)
            with act.Fori(0, B) as b:
                def stacks(gi):
                    for item, dst in ((0, KST), (1, QST[0]), (3, QST[2])):
                        act.wait_ge(S["stack_T"], 1 + 5 * gi + item + 1)
                        act.activation(dst[:, :], bank(item), ACT.Copy).then_inc(S["stack_sb_a"], 1)

                def probabilities(gi):
                    for u, (j, n0, nh) in enumerate(PROB_UNITS):
                        act.wait_ge(S["st_ps"], 1 + PU * gi + u + 1)
                        act.activation(PTj(j)[:, n0:n0 + nh, :], bank(4 + u % 2, 0, nh * (NT - j) * P).rearrange(
                            "p (n q) -> p n q", n=nh), ACT.Exp).then_inc(S["pt_ready"], 1)
                def unload(gi):
                    act.wait_ge(S["pv_ps"], 1 + gi + 1)
                    lo, hi = slice(0, P // 2), slice(P // 2, P)
                    act.wait_ge(S["sums_T"], 1 + gi)
                    act.activation(SUMS[lo, :], PS[hi, 6 * 512:7 * 512], ACT.Copy).then_inc(S["sums_sb"], 1)
                    act.activation(SUMS[hi, :], PS[lo, 7 * 512:8 * 512], ACT.Copy).then_inc(S["sums_sb"], 1)
                    act.wait_ge(S["o_ready"], 1 + gi)
                    act.activation(UN[lo, :], PS[lo, 6 * 512:7 * 512], ACT.Copy).then_inc(S["out_sb"], 1)
                    act.activation(UN[hi, :], PS[hi, 7 * 512:8 * 512], ACT.Copy).then_inc(S["out_sb"], 1)
                with act.Fori(0, G - 1) as g:
                    probabilities(b * G + g)
                    stacks(b * G + g + 1)
                    unload(b * G + g)
                probabilities(b * G + G - 1)
                unload(b * G + G - 1)
                act.wait_ge(S["o_ready"], 1 + G * (b + 1))
                act.activation(OTH[:, G - 1, :], OT[:, G - 1, :], ACT.Copy).then_inc(S["oT_last_hi"], 1)
                act.wait_ge(S["op_ps"], 1 + NT * (b + 1))
                for t in range(NT):
                    act.wait_ge(S["xT_ps"], 1 + NT * b + t + 1)
                    act.activation(XTH[:, :, t * P:(t + 1) * P], bank(4 + t).rearrange("p (k q) -> p k q", k=KC),
                                   ACT.Copy).then_inc(S["xT_hi"], 1)
                N0, N1 = NF // 2 + 1, NF // 2

                def wg_hi(f, slot, loads):
                    act.wait_ge(w_loaded[slot], 16 * loads)
                    act.activation(WHI[slot][:, 0:WD], WRAW[slot][:, 0:WD], ACT.Copy).then_inc(S["wg_hi"], 1)

                wg_hi(0, 0, b * N0 + 1)
                act.wait_ge(S["pj_ps"], 1 + 2 * (b + 1))
                act.activation(r8[0][:, :, :], projected[:, :, 0:E0], ACT.Exp, scale=-1.0).then_inc(S["sig_ready"], 1)

                def wd_hi(slot):
                    act.activation(WHI[slot][:, WD:WCOLS], WRAW[slot][:, WD:WCOLS], ACT.Copy).then_inc(S["wd_hi"], 1)

                def silu(f):
                    act.wait_ge(S["gate_ps"], 1 + b * NF + f + 1)
                    act.wait_ge(S["hid_ready"], 1 + b * NF + f)
                    act.activation(SIL[:, :], bank(0), ACT.Silu).then_inc(S["sil_ready"], 1)

                def chunk(f, slot, next_loads):
                    if next_loads is not None:
                        act.wait_ge(S["up_ps"], 1 + b * NF + f)
                        wg_hi(f + 1, 1 - slot, next_loads)
                    if not (isinstance(f, int) and f < 2):
                        act.wait_ge(S["dn_ps"], 1 + b * NF + f - 1)
                    wd_hi(slot)
                    silu(f)
                for h in range(2):
                    act.wait_ge(S["lx_ps"], 1 + 2 * b + h + 1)
                    act.activation(LXH[:, h, :], bank(6 + h, parts=LR), ACT.Copy).then_inc(S["lx_hi"], 1)
                act.wait_ge(S["wxT_ps"], 1 + b + 1)
                act.activation(WXT[:, :], bank(3, parts=LR), ACT.Copy).then_inc(S["wxT_sb"], 1)
                chunk(0, 0, b * N1 + 1)
                with act.Fori(0, NF // 2 - 1) as i:
                    for d in (1, 2):
                        chunk(2 * i + d, d % 2, (b * N0 + i + 2) if d == 1 else (b * N1 + i + 2))
                chunk(NF - 2, 1, (b + 1) * N0)
                chunk(NF - 1, 0, None)
                act.wait_ge(S["ld_ready"], 1 + b + 1)
                act.activation(LDH[:, :], LD[:, :], ACT.Copy).then_inc(S["ld_hi"], 1)
                for t in range(NT):
                    act.wait_ge(S["xT3_ps"], 1 + NT * b + t + 1)
                    act.activation(XTF[:, :, t * P:(t + 1) * P], bank(t).rearrange("p (k q) -> p k q", k=KC),
                                   ACT.Copy).then_inc(S["xT3_sb"], 1)
                act.wait_ge(S["o1_ps"], 1 + b + 1)
                act.activation(OT1[:, :], bank(4), ACT.Copy, scale=float(C) ** -0.5).then_inc(S["o1_sb"], 1)
                first_group(b + 1)
                for t in range(NT):
                    act.wait_ge(S["y_ready"], 1 + NT * b + t + 1)
                    act.activation(Y[:, t, :], Y[:, t, :], ACT.Exp, bias=nmx[:, t:t + 1],
                                   accum_out=ssum[:, t:t + 1]).then_inc(S["e_ready"], 1)
                for t in range(NT):
                    act.wait_ge(S["xT4_ps"], 1 + NT * b + t + 1)
                    act.activation(XTF[:, :, t * P:(t + 1) * P], bank(4 + t).rearrange("p (k q) -> p k q", k=KC),
                                   ACT.Copy).then_inc(S["xT4_sb"], 1)
                act.wait_ge(S["lgt_max"], 1 + b + 1)
                act.activation(SC[:, :, :], SC[:, :, :], ACT.Exp).then_inc(S["lgt_exp"], 1)
                act.wait_ge(S["lgt_exp"], 1 + b + 1)

        @block.vector
        def _(dve):
            step = Chain(dve, S["dve_step"], DVE_B)
            gstep = Chain(dve, S["g_dve"], DVE_G)
            fstep = Chain(dve, S["f_dve"], KSTEPS["f_dve"])

            def sig(instruction, name, value):
                instruction.then_inc(S[name], 1)
                dve.wait_ge(S[name], 1 + value)

            def front_norms(fb):
                fstep.base, fstep.n = fb * KSTEPS["f_dve"], 0
                dve.wait_ge(S["ctx_loaded"], 16 * (fb + 1))
                dve.wait_ge(S["x_loaded"], 16 * (fb + 1))
                alone(dve, "dve")
                for i in range(2 * NT):
                    ins = dve.bn_stats(FST6[:, i, :], CTX[:, i, :] if i < NT else XIN[:, i - NT, :])
                    if i < 2 * NT - 1:
                        ins.then_inc(S["f_dve"], 1)
                        fstep.n += 1
                    else:
                        fstep(ins)
                for i in range(2 * NT):
                    alone(dve, "dve")
                    ins = dve.bn_aggr(FMV[:, i, :], FST6[:, i, :])
                    if i < 2 * NT - 1:
                        ins.then_inc(S["f_dve"], 1)
                        fstep.n += 1
                    else:
                        fstep(ins)
                fstep(dve.tensor_tensor(fscale[:, :], FMV[:, 0:NT, 0], FMV[:, 0:NT, 0], ALU.mult))
                fstep(dve.tensor_tensor(fscale[:, :], fscale[:, :], FMV[:, 0:NT, 1], ALU.add))
                fstep(dve.tensor_scalar(fvar[:, 0:NT], fscale[:, :], EPS_RMS, None, ALU.add))
                sig(dve.tensor_scalar(fvar[:, NT:2 * NT], FMV[:, NT:2 * NT, 1], EPS_LN, None, ALU.add),
                    "f_in", 2 * fb + 1)

            def front_scales(fb):
                dve.wait_ge(S["f_out"], 1 + 2 * fb + 1)
                fstep(dve.tensor_tensor(fscale[:, :], finv[:, NT:2 * NT], finv[:, NT:2 * NT], ALU.mult))
                fstep(dve.tensor_tensor(fscale[:, :], fscale[:, :], FMV[:, NT:2 * NT, 1], ALU.mult))
                sig(dve.tensor_scalar(fvar2[:, :], fscale[:, :], EPS_RMS, None, ALU.add), "f_in", 2 * fb + 2)
                dve.wait_ge(S["f_out"], 1 + 2 * fb + 2)
                fstep(dve.tensor_tensor(fscale[:, :], finv[:, NT:2 * NT], fms[:, :], ALU.mult))

            def rotary(xm, qa, qb, tab_c, tab_s, last):
                hv = lambda ap, a, z: ap.rearrange("p (h d) -> p h d", d=HD)[:, :, a:z]
                fstep(dve.tensor_tensor(qa, xm, tab_c, ALU.mult))
                fstep(dve.tensor_tensor(hv(qb, 0, ROT), hv(xm, ROT, HD), hv(tab_s, 0, ROT), ALU.mult))
                last(dve.tensor_tensor(hv(qb, ROT, HD), hv(xm, 0, ROT), hv(tab_s, ROT, HD), ALU.mult))

            def front_q(fb, t, qab=(QA, QB)):
                if isinstance(t, int):
                    xt, sc, mn, tc, ts = XIN[:, t, :], fscale[:, t:t + 1], FMV[:, NT + t, 0:1], cosw[:, t, :], sinw[:, t, :]
                else:
                    xt, sc, mn = (XIN[:, bass.ds(t, 1), :].rearrange("p t c -> p (t c)"), fscale[:, bass.ds(t, 1)],
                                  FMV[:, bass.ds(NT + t, 1), 0])
                    tc, ts = (tab[:, bass.ds(t, 1), :].rearrange("p t c -> p (t c)") for tab in (cosw, sinw))
                fstep(dve.tensor_scalar(XW, xt, mn, sc, ALU.subtract, ALU.mult))
                rotary(XW, *qab, tc, ts, lambda ins: sig(ins, "qab_ready", NT * fb + t + 1))

            def front_k(fb):
                flat = lambda ap: ap.rearrange("p t c -> p (t c)")
                fstep(dve.tensor_tensor(XW.rearrange("p (t c) -> p t c", t=NT), CTX[:, :, :],
                                        finv[:, 0:NT].unsqueeze(2).broadcast_to([P, NT, CKV]), ALU.mult))
                rotary(XW, QA, QB, flat(cosk[:, :, :]), flat(sink[:, :, :]), fstep)
                sig(dve.tensor_tensor(flat(KR[:, :, :]), QA, QB, ALU.add), "k_ready", fb + 1)
            setup = Chain(dve, setup_dve, None)
            setup(dve.memset(ZR[:, :], 0.0))
            setup(dve.memset(zrow[:, :], 0.0))
            setup(dve.memset(mhalf[:, :], -0.5))
            setup.post(dve.memset(LST[:, :], 0.0))
            setup.post(dve.memset(KEYS[0][:, CAP:CAP + T], 0.0))
            setup(dve.memset(V8[:, :, :], 0.0))
            for n in range(HPG):
                c0 = n * P + (n * HD + P // 2) % P
                setup.post(dve.memset(V8[:, :, c0:c0 + HD], 1.0))
            front_norms(0)
            dve.wait_ge(tables_loaded, 16 * 6)
            for t in range(NT):
                for kind in ("k", "q") if t < NT - POOL_TABLES else ("k",):
                    for operation in rotary_table(dve, kind, t):
                        setup.post(operation)
                if t == 0:
                    front_scales(0)
            setup.need(setup.n)
            for t in range(NT):
                if t == NT - POOL_TABLES:
                    dve.wait_ge(tables_made, 3 * POOL_TABLES)
                if t >= len(FIRST_QAB):
                    dve.wait_ge(S["q_ready"], 1 + t - len(FIRST_QAB) + 1)
                front_q(0, t, FIRST_QAB[t % len(FIRST_QAB)])
            dve.wait_ge(S["q_ready"], 1 + NT - 1)
            front_k(0)
            fstep.end()
            dve.wait_ge(setup_loaded, SETUP_LOADED)
            dve.wait_ge(setup_act, 4)
            setup(dve.tensor_tensor(woL[:, :, :], wo_raw[:, :, :], woH[:, :, :], ALU.subtract))
            setup(dve.tensor_tensor(acL[:, :, :], ac_raw[:, :, :], acH[:, :, :], ALU.subtract))
            setup(dve.tensor_tensor(bdL[:, :], bd_raw[:, :], bdH[:, :], ALU.subtract))
            with dve.Fori(0, B) as b:
                step.base, step.n = b * DVE_B, 0
                norms = [0]

                def inverse_root():
                    dve.wait_ge(S["norm_out"], 1 + 4 * b + norms[0])

                def stats(tile, make, name):
                    for t in range(NT + 1):
                        if t < NT:
                            make(t)
                        if t > 0:
                            dve.wait_ge(S[name], 1 + NT * b + t)
                            n = step.post(dve.bn_stats(ST6[:, t - 1, :], tile(t - 1)))
                    step.need(n)
                    alone(dve, "dve")
                    for t in range(NT):
                        n = step.post(dve.bn_aggr(MV[:, t, :], ST6[:, t, :]))
                    step.need(n)

                def variances(eps):
                    norms[0] += 1
                    sig(dve.tensor_scalar(sm[0][:, :], MV[:, :, 1], eps, None, ALU.add), "norm_in", 4 * b + norms[0])

                def layer_norm(make, name, dst, ready):
                    stats(lambda t: X[:, t, :], make, name)
                    variances(EPS_LN)
                    inverse_root()
                    for t in range(NT):
                        dve.tensor_scalar(dst[:, t, 0:C], X[:, t, :], MV[:, t, 0:1], sm[1][:, t:t + 1],
                                          ALU.subtract, ALU.mult).then_inc(S[ready], 1)
                    dve.wait_ge(S[ready], 1 + NT * (b + 1))

                step(dve.memset(NM2[:, :], 0.0))
                alone(dve, "dve")
                def maxima(gi):
                    for i, (t, n0, nh, at, width) in enumerate(MAX_UNITS):
                        dve.wait_ge(S["s_ps"], 1 + MU * gi + i + 1)
                        src = PS[:, at:at + nh * width].rearrange("p (n k) -> p n k", n=nh)[:, :, 0:(t + 1) * P]
                        dve.tensor_reduce(NM[:, t * HPG + n0:t * HPG + n0 + nh], src, AX, ALU.max,
                                          negate=True).then_inc(S["s_max"], 1)
                    dve.wait_ge(S["s_max"], 1 + MU * (gi + 1))
                    dve.wait_ge(S["mt_ps"], 1 + gi)
                    gstep(dve.tensor_copy(NM2[:, 0:16].bitcast(F32R), NM[:, :]))
                    sig(dve.tensor_tensor(NM2[:, 32:48], NM[:, :], NM2[:, 0:16], ALU.subtract), "nm_ready", gi + 1)
                    dve.wait_ge(S["mt_ps"], 1 + gi + 1)
                    sig(dve.tensor_tensor(RM[:, :].rearrange("p (t q) -> p t q", t=NT),
                                          bank(3, 0, P).unsqueeze(1).broadcast_to([P, NT, P]), blockmask[:, :, :],
                                          ALU.mult), "rm_ready", gi + 1)

                def normalise(gi, g):
                    dve.wait_ge(S["sums_T"], 1 + gi + 1)
                    dve.wait_ge(S["inv_ps"], 1 + gi)
                    ones = bank(0).rearrange("p (t n d) -> p t n d", t=NT, n=HPG)
                    gstep(dve.reciprocal(RD[:, :].rearrange("p (t n) -> p t n", t=NT), ones[:, :, :, 0]))
                    sig(dve.tensor_copy(RDB[:, :, :], RD[:, :].unsqueeze(2).broadcast_to([P, NT * HPG, HD])),
                        "sums_inv", gi + 1)
                    dve.wait_ge(S["oT_lo"], 1 + (G - 1) * b)
                    dve.wait_ge(S["oT_last_lo"], 1 + b)
                    dve.wait_ge(S["inv_ps"], 1 + gi + 1)
                    dve.wait_ge(S["out_sb"], 1 + 2 * (gi + 1))
                    sig(dve.tensor_tensor(OT[:, row(g), :], bank(1).unsqueeze(1), UN[:, :].unsqueeze(1), ALU.mult),
                        "o_ready", gi + 1)
                gstep.base, gstep.n = b * G * DVE_G, 0
                maxima(b * G)
                alone(dve, "dve")
                with dve.Fori(0, G - 1) as g:
                    gi = b * G + g
                    gstep.base, gstep.n = gi * DVE_G + 1, 0
                    dve.wait_ge(S["st_ps"], 1 + PU * (gi + 1))
                    for i, (item, bk, dst) in enumerate(((2, 2, QST[1]), (4, 5, QST[3]))):
                        dve.wait_ge(S["stack_T"], 1 + 5 * (gi + 1) + item + 1)
                        sig(dve.tensor_copy(dst[:, :], bank(bk)), "stack_sb_d", DVE_STACKS * b + 2 * g + i + 1)
                    maxima(gi + 1)
                    normalise(gi, g)
                gstep.end()
                gstep.base, gstep.n = (b * G + G - 1) * DVE_G + 1, 0
                normalise(b * G + G - 1, G - 1)
                dve.wait_ge(S["oT_last_hi"], 1 + b + 1)
                sig(dve.tensor_tensor(OTL[:, G - 1, :], OT[:, G - 1, :], OTH[:, G - 1, :], ALU.subtract),
                    "oT_last_lo", b + 1)
                dve.wait_ge(S["out_stored"], 16 * (b + 1))
                def x1(t):
                    dve.wait_ge(S["op_ps"], 1 + NT * b + t + 1)
                    dve.tensor_tensor(X[:, t, :], bank(2 + t), XIN[:, t, :], ALU.add).then_inc(S["x1_ready"], 1)
                layer_norm(x1, "x1_ready", XN, "xn_ready")
                for t in range(NT):
                    dve.wait_ge(S["xT_hi"], 1 + NT * b + t + 1)
                    sl = slice(t * P, (t + 1) * P)
                    sig(dve.tensor_tensor(XTL[:, :, sl], bank(4 + t).rearrange("p (k q) -> p k q", k=KC),
                                          XTH[:, :, sl], ALU.subtract), "xT_lo", NT * b + t + 1)
                def w_rest(n, slot, a, z, hi, lo):
                    dve.wait_ge(S[hi], 1 + b * NF + n + 1)
                    sig(dve.tensor_tensor(WLO[slot][:, a:z], WRAW[slot][:, a:z], WHI[slot][:, a:z], ALU.subtract),
                        lo, b * NF + n + 1)

                w_rest(0, 0, 0, WD, "wg_hi", "wg_lo")
                n = step.post(dve.memset(WX[:, :, 0:R0], 1.0 / R0))
                dve.wait_ge(S["sig_ready"], 1 + b + 1)
                step(dve.tensor_scalar(r8[1][:, :, :], r8[0][:, :, :], 1.0, None, ALU.add))
                step(dve.reciprocal(r8[0][:, :, :], r8[1][:, :, :]))
                step(dve.tensor_tensor(r8[1][:, :, :], r8[0][:, :, :],
                                       ebias[:, :].unsqueeze(1).broadcast_to([P, NT, E0]), ALU.add))
                alone(dve, "dve")
                for t in range(NT):
                    n = step.post(dve.max(top2[:, t, :], r8[1][:, t, :]))
                step.need(n)
                step(dve.memset(top2[:, :, 2:8], ABSENT))
                alone(dve, "dve")
                for t in range(NT):
                    n = step.post(dve.match_replace(r8[2][:, t, :], top2[:, t, :], r8[1][:, t, :], ABSENT))
                step.need(n)
                step(dve.tensor_tensor(r8[3][:, :, :], r8[2][:, :, :], r8[1][:, :, :], ALU.not_equal))
                step(dve.tensor_tensor(r8[2][:, :, :], r8[3][:, :, :], r8[0][:, :, :], ALU.mult))
                step(dve.tensor_reduce(sm[2][:, :], r8[2][:, :, :], AX, ALU.add))
                step(dve.tensor_scalar(sm[3][:, :], sm[2][:, :], 1e-8, float(R0), ALU.add, ALU.mult))
                step(dve.reciprocal(sm[2][:, :], sm[3][:, :]))
                step(dve.tensor_tensor(r8[3][:, :, :], r8[2][:, :, :],
                                       sm[2][:, :].unsqueeze(2).broadcast_to([P, NT, E0]), ALU.mult))
                step(dve.tensor_copy(WX[:, :, R0:LR].rearrange("p t (e r) -> p t e r", e=E0),
                                     r8[3][:, :, :].unsqueeze(3).broadcast_to([P, NT, E0, R0])))
                sig(dve.tensor_tensor(LG[:, :, :, :], projected[:, :, E0:PJ].rearrange("p t (h r) -> p t h r", h=2),
                                      WX[:, :, :].unsqueeze(2).broadcast_to([P, NT, 2, LR]), ALU.mult),
                    "lg_ready", b + 1)

                def chunk(f, slot, last=False, meanwhile=lambda: None):
                    if not last:
                        w_rest(f + 1, 1 - slot, 0, WD, "wg_hi", "wg_lo")
                    w_rest(f, slot, WD, WCOLS, "wd_hi", "wd_lo")
                    meanwhile()
                    dve.wait_ge(S["sil_ready"], 1 + b * NF + f + 1)
                    dve.wait_ge(S["up_ps"], 1 + b * NF + f + 1)
                    dve.wait_ge(S["hl_ready"], 1 + b * NF + f)
                    sig(dve.tensor_tensor(HID[:, :], SIL[:, :], bank(1), ALU.mult), "hid_ready", b * NF + f + 1)
                for h in range(2):
                    dve.wait_ge(S["lx_hi"], 1 + 2 * b + h + 1)
                    sig(dve.tensor_tensor(LXL[:, h, :], bank(6 + h, parts=LR), LXH[:, h, :], ALU.subtract),
                        "lx_lo", 2 * b + h + 1)
                step(dve.tensor_copy(KEYS[0][:, 0:CAP], LST[:, :]))
                chunk(0, 0)
                front_norms(b + 1)
                fdone = KSTEPS["f_dve"] - 3 * NT - 4

                def two_chunks(i):
                    for d in (1, 2):
                        chunk(2 * i + d, d % 2)
                        if d == 1 and isinstance(i, int):
                            front_scales(b + 1)
                        list_round(dve, (NF // 2 - 1) * 2 * b + 2 * i + d - 1, 2 * i + d - 1)
                        if d == 2:
                            fstep.base, fstep.n = (b + 1) * KSTEPS["f_dve"] + fdone + i * 3, 0
                            dve.wait_ge(S["q_ready"], 1 + NT * (b + 1) + i)
                            front_q(b + 1, i)
                two_chunks(0)
                alone(dve, "dve")
                with dve.Fori(1, NF // 2 - 1) as i:
                    two_chunks(i)
                chunk(NF - 2, 1)
                fstep.base, fstep.n = (b + 1) * KSTEPS["f_dve"], fdone + 3 * NT
                dve.wait_ge(S["q_ready"], 1 + NT * (b + 2))
                front_k(b + 1)
                fstep.end()
                chunk(NF - 1, 0, last=True)
                dve.wait_ge(S["ha_ps"], 1 + b + 1)
                dve.wait_ge(S["wxT_sb"], 1 + b + 1)
                sig(dve.tensor_tensor(LD[:, :], bank(2, parts=LR), WXT[:, :], ALU.mult), "ld_ready", b + 1)
                dve.wait_ge(S["ld_hi"], 1 + b + 1)
                sig(dve.tensor_tensor(LDL[:, :], LD[:, :], LDH[:, :], ALU.subtract), "ld_lo", b + 1)
                def x2(t):
                    dve.wait_ge(S["ffn_ps"], 1 + NT * b + t + 1)
                    dve.tensor_tensor(X[:, t, :], bank(4 + t), X[:, t, :], ALU.add).then_inc(S["x2_ready"], 1)
                layer_norm(x2, "x2_ready", XN, "xn3_ready")
                stats(bank, lambda t: None, "sim_ps")
                variances(EPS_SIM)
                scaled, shifted, peaks = [0] * NT, [0] * NT, 0
                for t in range(NT):
                    scaled[t] = step.post(dve.scalar_tensor_tensor(
                        out=Y[:, t, :], in0=bank(t), scalar=MV[:, t, 0:1], in1=gam[:, :],
                        op0=ALU.subtract, op1=ALU.mult))
                inverse_root()
                for t in range(NT + 1):
                    if t < NT:
                        step.need(scaled[t])
                        shifted[t] = step.post(dve.scalar_tensor_tensor(
                            out=Y[:, t, :], in0=Y[:, t, :], scalar=sm[1][:, t:t + 1], in1=bet[:, :],
                            op0=ALU.mult, op1=ALU.add))
                    if t > 0:
                        step.need(shifted[t - 1])
                        dve.tensor_reduce(nmx[:, t - 1:t], Y[:, t - 1, :], AX, ALU.max,
                                          negate=True).then_inc(S["y_ready"], 1)
                dve.wait_ge(S["e_ready"], 1 + NT * (b + 1) - 1)
                step(dve.reciprocal(sm[2][:, 0:NT - 1], ssum[:, 0:NT - 1]))

                def x3(t):
                    if t == NT - 1:
                        dve.wait_ge(S["e_ready"], 1 + NT * (b + 1))
                        step(dve.reciprocal(sm[2][:, t:NT], ssum[:, t:NT]))
                    dve.scalar_tensor_tensor(out=X[:, t, :], in0=Y[:, t, :], scalar=sm[2][:, t:t + 1],
                                             in1=X[:, t, :], op0=ALU.mult, op1=ALU.add).then_inc(S["x3_ready"], 1)
                dve.wait_ge(S["hx_stored"], 16 * (b + 1))
                layer_norm(x3, "x3_ready", HN, "xn4_ready")
                dve.wait_ge(S["lgt_ps"], 1 + b + 1)
                lg = bank(4, 0, NT * E1).rearrange("p (t e) -> p t e", t=NT)
                step(dve.tensor_reduce(sm[2][:, :], lg, AX, ALU.max))
                sig(dve.tensor_tensor(SC[:, :, :], lg, sm[2][:, :].unsqueeze(2).broadcast_to([P, NT, E1]),
                                      ALU.subtract), "lgt_max", b + 1)
                dve.wait_ge(S["lgt_exp"], 1 + b + 1)
                step(dve.tensor_reduce(sm[2][:, :], SC[:, :, :], AX, ALU.add))
                step(dve.reciprocal(sm[3][:, :], sm[2][:, :]))
                step(dve.tensor_tensor(SC[:, :, :], SC[:, :, :], sm[3][:, :].unsqueeze(2).broadcast_to([P, NT, E1]),
                                       ALU.mult))
                alone(dve, "dve")
                for t in range(NT):
                    n = step.post(dve.max(t8[:, t, :], SC[:, t, :]))
                step.need(n)
                alone(dve, "dve")
                for t in range(NT):
                    n = step.post(dve.match_replace(SR[:, t, :], t8[:, t, :], SC[:, t, :], -1.0))
                step.need(n)
                sig(dve.tensor_scalar(MK[:, :, :], SR[:, :, :], 0.0, None, ALU.is_lt), "mk_ready", b + 1)
                step(dve.tensor_tensor(SR[:, :, :], MK[:, :, :], SC[:, :, :], ALU.mult))
                step(dve.tensor_reduce(sm[2][:, :], SR[:, :, :], AX, ALU.add))
                step(dve.tensor_scalar(sm[3][:, :], sm[2][:, :], 1e-20, None, ALU.add))
                step(dve.reciprocal(sm[2][:, :], sm[3][:, :]))
                step(dve.tensor_tensor(HN[:, :, C:HROW], SR[:, :, :],
                                       sm[2][:, :].unsqueeze(2).broadcast_to([P, NT, E1]), ALU.mult))
                dve.wait_ge(S["rev_loaded"], 16 * (b + 1))
                dve.wait_ge(S["mk_ps"], 1 + b + 1)
                sig(dve.tensor_tensor(KEYS[0][:, CAP:CAP + T], bank(5, parts=E1), revt[:, :],
                                      ALU.mult), "key_ready", b + 1)
            step.end()

        @block.tensor
        def _(pe):
            def three(dst, a, b_, first, last, **kw):
                pe.matmul(dst, a[0], b_[0], start=first, stop=False, **kw)
                pe.matmul(dst, a[0], b_[1], start=False, stop=False, **kw)
                return pe.matmul(dst, a[1], b_[0], start=False, stop=last, **kw)

            def stack_T(gi, items):
                for item, bk in items:
                    pe.wait_ge(S["stack_ready"], 1 + 5 * gi + item + 1)
                    for t in range(NT):
                        mm = pe.transpose(bank(bk, t * P, (t + 1) * P), ([KS] + QS)[item][:, t, :], ident[:, :])
                    mm.then_inc(S["stack_T"], 1)

            def masks(at, nh, width, c, mask):
                per = min(nh, 512 // width)
                for n in range(0, nh, per):
                    blocks = PS[:, at + n * width:at + (n + per) * width].rearrange("p (n k) -> p n k", n=per)
                    pe.matmul(blocks[:, :, c:c + P], identb[:, :], mask[:, :].unsqueeze(1).broadcast_to(
                        [P, per, P]), start=True, stop=False, skip_group_check=True)

            def max_unit(gi, i):
                t, n0, nh, at, width = MAX_UNITS[i]
                n_keys = (t + 1) * P
                if i >= 2:
                    pe.wait_ge(S["s_max"], 1 + MU * gi + i - 1)
                masks(at, nh, width, t * P, mask_qk)
                for n in range(nh):
                    a = at + n * width
                    mm = pe.matmul(PS[:, a:a + n_keys], QST[n0 + n][:, t * P:(t + 1) * P], KST[:, 0:n_keys],
                                   start=False, stop=True, skip_group_check=True)
                mm.then_inc(S["s_ps"], 1)

            def first_group(fb, o1_read):
                pe.wait_ge(S["ctx_loaded"], 16 * (fb + 1))
                for t in range(NT):
                    mm = pe.transpose(bank(5, t * P, (t + 1) * P), CTX[:, t, :], ident[:, :])
                mm.then_inc(S["ctxT_ps"], 1)
                if o1_read is not None:
                    pe.wait_ge(S["o1_sb"], o1_read)
                stack_T(fb * G, FIRST_STACKS[0:3])
                pe.wait_ge(S["ctxT_sb"], 1 + fb + 1)
                ctxT = XN[:, 3, :]
                pe.matmul(bank(5), wk[:, :], ctxT, start=True, stop=True).then_inc(S["kvT_ps"], 1)
                for i in (3, 4):
                    pe.wait_ge(S["stack_sb_a"], 1 + ACT_STACKS * fb + i - 2)
                    stack_T(fb * G, FIRST_STACKS[i:i + 1])
                pe.wait_ge(S["stack_sb_a"], 1 + ACT_STACKS * fb + 3)
                pe.wait_ge(S["kv_act"], 1 + fb + 1)
                for t in range(NT):
                    mm = pe.transpose(bank(7, t * P, (t + 1) * P), KVT[:, t * P:(t + 1) * P], ident[:, :])
                mm.then_inc(S["kv_ps"], 1)

            pe.wait_ge(setup_loaded, SETUP_LOADED)
            first_group(0, None)
            pe.wait_ge(S["stack_sb_a"], 1 + 5)
            pe.wait_ge(S["kv_act"], 1 + 1)
            pe.wait_ge(S["kv_row"], 1 + 1)
            max_unit(0, 0)
            max_unit(0, 1)
            with pe.Fori(0, B) as b:
                def prob_unit(gi, u, parts="scores maxima"):
                    j, n0, nh = PROB_UNITS[u]
                    n_q = (NT - j) * P
                    if "scores" in parts:
                        pe.wait_ge(S["pt_ready"], 1 + PU * gi + max(u - 1, 0))
                        masks((4 + u % 2) * 512, nh, n_q, 0, mask_kq)
                    for n in range(nh):
                        at = (4 + u % 2) * 512 + n * n_q
                        if "scores" in parts:
                            pe.matmul(PS[:, at:at + n_q], KST[:, j * P:(j + 1) * P], QST[n0 + n][:, j * P:T],
                                      start=False, stop=False, skip_group_check=True)
                        if "maxima" in parts:
                            mm = pe.matmul(PS[:, at:at + n_q], sel[:, n0 + n, :], RM[:, j * P:T], start=False,
                                           stop=True, skip_group_check=True)
                    if "maxima" in parts:
                        mm.then_inc(S["st_ps"], 1)

                def times_v(gi, *units):
                    for u in units:
                        j, n0, nh = PROB_UNITS[u]
                        if u == 0:
                            pe.wait_ge(S["v_ready"], 1 + gi + 1)
                        if u == 0:
                            pe.wait_ge(S["out_sb"], 1 + 2 * gi)
                            pe.wait_ge(S["sums_sb"], 1 + 2 * gi)
                        pe.wait_ge(S["pt_ready"], 1 + PU * gi + u + 1)
                        for n in range(n0, n0 + nh):
                            mm = pe.matmul(bank(6 + n // 2, j * P, T), V8[:, j, n * P:(n + 1) * P], PTj(j)[:, n, :],
                                           start=(j == 0 and n % 2 == 0), stop=(j == NT - 1), skip_group_check=True)
                        if u == PU - 1:
                            mm.then_inc(S["pv_ps"], 1)

                def divisors(gi, part):
                    if part == "sums":
                        pe.wait_ge(S["sums_sb"], 1 + 2 * (gi + 1))
                        for t in range(NT):
                            mm = pe.transpose(bank(0, t * P, (t + 1) * P), SUMS[:, t * P:(t + 1) * P], ident[:, :])
                        mm.then_inc(S["sums_T"], 1)
                    else:
                        pe.wait_ge(S["sums_inv"], 1 + gi + 1)
                        for t in range(NT):
                            mm = pe.matmul(bank(1, t * P, (t + 1) * P), RDB[:, t * HPG:(t + 1) * HPG, :].rearrange(
                                "p n d -> p (n d)"), ident[:, :], start=True, stop=True)
                        mm.then_inc(S["inv_ps"], 1)

                def open_group(gi, before=None):
                    prob_unit(gi, 0, "scores")
                    prob_unit(gi, 1, "scores")
                    if before is not None:
                        divisors(before, "sums")
                    pe.wait_ge(S["rm_ready"], 1 + gi + 1)
                    prob_unit(gi, 0, "maxima")
                    prob_unit(gi, 1, "maxima")

                def group(gi, g, following):
                    prob_unit(gi, 2)
                    times_v(gi, 0)
                    prob_unit(gi, 3)
                    prob_unit(gi, 4)
                    times_v(gi, 1)
                    prob_unit(gi, 5)
                    prob_unit(gi, 6)
                    times_v(gi, 2)
                    if following:
                        pe.wait_ge(S["o_ready"], 1 + gi)
                    for u in (7, 8, 9, 10):
                        prob_unit(gi, u)
                        if following and u > 7:
                            stack_T(gi + 1, ((u - 8, u - 8),))
                    if following:
                        stack_T(gi + 1, ((3, 3),))
                    times_v(gi, 3)
                    if following:
                        pe.wait_ge(S["pt_ready"], 1 + PU * gi + 10)
                        stack_T(gi + 1, ((4, 5),))
                    times_v(gi, 4)
                    if following:
                        pe.wait_ge(S["stack_sb_a"], 1 + ACT_STACKS * b + 5 + 3 * (g + 1))
                        pe.wait_ge(S["stack_sb_d"], 1 + DVE_STACKS * b + 2 * (g + 1))
                        max_unit(gi + 1, 0)
                        max_unit(gi + 1, 1)
                        times_v(gi, 5)
                        max_unit(gi + 1, 2)
                        times_v(gi, 6)
                        max_unit(gi + 1, 3)
                        times_v(gi, 7)
                        max_unit(gi + 1, 4)
                        times_v(gi, 8)
                        max_unit(gi + 1, 5)
                        times_v(gi, 9, 10)
                        rows_of_maxima(gi + 1)
                        open_group(gi + 1, gi)
                        divisors(gi, "inverses")
                    else:
                        times_v(gi, 5, 6, 7, 8, 9, 10)
                        divisors(gi, "sums")

                def rows_of_maxima(gi):
                    pe.wait_ge(S["nm_ready"], 1 + gi + 1)
                    pe.transpose(bank(3, 0, P), NM2[:, :], ident[:, :]).then_inc(S["mt_ps"], 1)
                for i in range(2, MU):
                    max_unit(b * G, i)
                rows_of_maxima(b * G)
                open_group(b * G)
                alone(pe, "pe")
                with pe.Fori(0, G - 1) as g:
                    group(b * G + g, g, True)
                group(b * G + G - 1, G - 1, False)
                for k0, k1 in ((0, KC - 1), (KC - 1, KC)):
                    if k1 < KC:
                        pe.wait_ge(S["oT_lo"], 1 + (G - 1) * (b + 1))
                    else:
                        pe.wait_ge(S["oT_last_lo"], 1 + b + 1)
                    for t in range(NT):
                        if k1 < KC and t == 1:
                            divisors(b * G + G - 1, "inverses")
                        sl = slice(t * P, (t + 1) * P)
                        for k in range(k0, k1):
                            mm = three(bank(2 + t), (OTH[:, k, sl], OTL[:, k, sl]), (woH[:, k, :], woL[:, k, :]),
                                       k == 0, k == KC - 1)
                        if k1 == KC:
                            mm.then_inc(S["op_ps"], 1)
                for t in range(NT):
                    pe.wait_ge(S["xn_ready"], 1 + NT * b + t + 1)
                    for k in range(KC):
                        mm = pe.transpose(bank(4 + t, k * P, (k + 1) * P), XN[:, t, k * P:(k + 1) * P], ident[:, :])
                    mm.then_inc(S["xT_ps"], 1)
                for t in range(NT):
                    pe.wait_ge(S["xT_lo"], 1 + NT * b + t + 1)
                    sl = slice(t * P, (t + 1) * P)
                    for k in range(KC):
                        mm = three(bank(2 + t // 2, (t % 2) * 256, (t % 2) * 256 + PJ),
                                   (XTH[:, k, sl], XTL[:, k, sl]), (acH[:, k, :], acL[:, k, :]), k == 0, k == KC - 1)
                    if t % 2:
                        mm.then_inc(S["pj_ps"], 1)

                def gate_up(f, slot, parts="weights lora"):
                    hi, lo = WHI[slot], WLO[slot]
                    pe.wait_ge(S["wg_lo"], 1 + b * NF + f + 1)
                    for h, (bk, free, done) in enumerate(((0, "sil_ready", "gate_ps"), (1, "hid_ready", "up_ps"))):
                        if "weights" in parts:
                            pe.wait_ge(S[free], 1 + b * NF + f)
                            for k in range(KC):
                                c0 = k * 2 * P + h * P
                                three(bank(bk), (hi[:, c0:c0 + P], lo[:, c0:c0 + P]), (XTH[:, k, :], XTL[:, k, :]),
                                      k == 0, False)
                        if "lora" in parts:
                            c0 = WBG + h * P
                            three(bank(bk), (hi[0:LR, c0:c0 + P], lo[0:LR, c0:c0 + P]), (LXH[:, h, :], LXL[:, h, :]),
                                  False, True).then_inc(S[done], 1)

                def down(f, slot):
                    hi, lo = WHI[slot], WLO[slot]
                    pe.wait_ge(S["wd_lo"], 1 + b * NF + f + 1)
                    pe.wait_ge(S["hl_ready"], 1 + b * NF + f + 1)
                    three(bank(2, parts=LR), (hi[:, WAD:WAD + LR], lo[:, WAD:WAD + LR]),
                          (HH[slot][:, :], HL[slot][:, :]), False, False, skip_group_check=True)
                    for t in range(NT):
                        sl = slice(t * P, (t + 1) * P)
                        mm = three(bank(4 + t), (HH[slot][:, sl], HL[slot][:, sl]),
                                   (hi[:, WD:WD + C], lo[:, WD:WD + C]), False, False, skip_group_check=True)
                    mm.then_inc(S["dn_ps"], 1)

                gate_up(0, 0, "weights")
                pe.wait_ge(S["lg_ready"], 1 + b + 1)
                for h in range(2):
                    for t in range(NT):
                        mm = pe.transpose(bank(6 + h, t * P, (t + 1) * P, parts=LR), LG[:, t, h, :], ident[:, :])
                    mm.then_inc(S["lx_ps"], 1)
                for t in range(NT):
                    mm = pe.transpose(bank(3, t * P, (t + 1) * P, parts=LR), WX[:, t, :], ident[:, :])
                mm.then_inc(S["wxT_ps"], 1)
                pe.wait_ge(S["lx_lo"], 1 + 2 * (b + 1))
                gate_up(0, 0, "lora")
                for bk in (2, 4, 5, 6, 7):
                    pe.matmul(bank(bk), zrow[:, 0:P], zrow[:, :], start=True, stop=False, skip_group_check=True)
                alone(pe, "pe")
                with pe.Fori(0, NF // 2) as i:
                    for d in (1, 2):
                        gate_up(2 * i + d, d % 2)
                        down(2 * i + d - 1, (d + 1) % 2)
                slot = (NF - 1) % 2
                hi, lo = WHI[slot], WLO[slot]
                pe.wait_ge(S["wd_lo"], 1 + b * NF + NF)
                pe.wait_ge(S["hl_ready"], 1 + b * NF + NF)
                three(bank(2, parts=LR), (hi[:, WAD:WAD + LR], lo[:, WAD:WAD + LR]), (HH[slot][:, :], HL[slot][:, :]),
                      False, True, skip_group_check=True).then_inc(S["ha_ps"], 1)
                for t in range(NT):
                    sl = slice(t * P, (t + 1) * P)
                    mm = three(bank(4 + t), (HH[slot][:, sl], HL[slot][:, sl]),
                               (hi[:, WD:WD + C], lo[:, WD:WD + C]), False, False, skip_group_check=True)
                mm.then_inc(S["dn_ps"], 1)
                pe.wait_ge(S["ld_lo"], 1 + b + 1)
                for t in range(NT):
                    sl = slice(t * P, (t + 1) * P)
                    three(bank(4 + t), (LDH[:, sl], LDL[:, sl]), (bdH[:, :], bdL[:, :]), False, True,
                          skip_group_check=True).then_inc(S["ffn_ps"], 1)
                for t in range(NT):
                    pe.wait_ge(S["xn3_ready"], 1 + NT * b + t + 1)
                    for k in range(KC):
                        mm = pe.transpose(bank(t, k * P, (k + 1) * P), XN[:, t, k * P:(k + 1) * P], ident[:, :])
                    mm.then_inc(S["xT3_ps"], 1)
                pe.wait_ge(S["xT3_sb"], 1 + NT * (b + 1))
                for k in range(KC):
                    mm = pe.matmul(bank(4), KV[:, k, :], XTF[:, k, :], start=(k == 0), stop=(k == KC - 1))
                mm.then_inc(S["o1_ps"], 1)
                pe.wait_ge(S["o1_sb"], 1 + b + 1)
                for t in range(NT):
                    pe.matmul(bank(t), OT1[:, t * P:(t + 1) * P], KVT[:, :], start=True,
                              stop=True).then_inc(S["sim_ps"], 1)
                first_group(b + 1, 1 + b + 1)
                pe.wait_ge(S["stack_sb_a"], 1 + ACT_STACKS * (b + 1) + 5)
                pe.wait_ge(S["kv_act"], 1 + b + 2)
                pe.wait_ge(S["kv_row"], 1 + b + 2)
                for t in range(NT):
                    pe.wait_ge(S["xn4_ready"], 1 + NT * b + t + 1)
                    for k in range(KC):
                        mm = pe.transpose(bank(4 + t, k * P, (k + 1) * P), HN[:, t, k * P:(k + 1) * P], ident[:, :])
                    mm.then_inc(S["xT4_ps"], 1)
                for t in range(NT):
                    pe.wait_ge(S["xT4_sb"], 1 + NT * b + t + 1)
                    for k in range(KC):
                        mm = pe.matmul(bank(4, t * E1, (t + 1) * E1), XTF[:, k, t * P:(t + 1) * P], rw[:, k, :],
                                       start=(k == 0), stop=(k == KC - 1))
                mm.then_inc(S["lgt_ps"], 1)
                max_unit((b + 1) * G, 0)
                max_unit((b + 1) * G, 1)
                pe.wait_ge(S["mk_ready"], 1 + b + 1)
                alone(pe, "pe")
                for t in range(NT):
                    mm = pe.transpose(bank(5, t * P, (t + 1) * P, parts=E1), MK[:, t, :], ident[:, :])
                mm.then_inc(S["mk_ps"], 1)

    place["at"] = part3_base
    LT = sb("LT", [P, E1])
    lv = sb("lv", [P, E1])
    NW = NX = 12
    W1 = [sb(f"W1_{s}", [P, KC, 2 * F1]) for s in range(NW)]
    W2 = [sb(f"W2_{s}", [FH, 2, C]) for s in range(NW)]
    IDX1 = [sb(f"IDX1_{s}", [P, 1], U32) for s in range(NX)]
    XG = [sb(f"XG{s}", [P, HROW]) for s in range(NX)]
    XGT = [sb(f"XGT{s}", [P, KC, P]) for s in range(2)]
    WC = [sb(f"WC{s}", [P, 1]) for s in range(2)]
    SL = [sb(f"SL{s}", [P, F1]) for s in range(2)]
    HM = [sb(f"HM{s}", [P, F1]) for s in range(2)]
    HMT = [sb(f"HMT{s}", [FH, 2, P]) for s in range(2)]
    YE = [sb(f"YE{s}", [P, C]) for s in range(4)]
    lst_ready, lst_ps, idx_ready = sem("lst_ready"), sem("lst_ps"), sem("idx_ready")
    expert_loaded = [sem(f"expert_loaded{s}") for s in range(NW)]
    gathered = [sem(f"gathered{s}") for s in range(NX)]
    AHEAD = 4

    def experts(engine, body, start, stop):
        rounds = (stop - start) // NW

        def call(i, d):
            body((i * NW + start + d), (start + d) % NW, i + (start + d) // NW)
        with engine.Fori(0, rounds) as i:
            for d in range(NW):
                call(i, d)
        for e in range(start + rounds * NW, stop):
            body(e, e % NW, e // NW)

    with nc.Block() as block:
        @block.sync
        def _(sp):
            def load(e, s):
                sp.dma_start(W1[s][:, :, :], w["w1"][span(e, P), :].rearrange(
                    "p (k f) -> p k f", k=KC)).then_inc(expert_loaded[s], 16)
                sp.dma_start(W2[s][:, :, :], w["w2"][span(e, FH), :].rearrange(
                    "p (h c) -> p h c", h=2)).then_inc(expert_loaded[s], 16)
            for s in range(NW):
                load(s, s)

            def reload(e, s, r):
                sp.wait_ge(M["y_ps"], 1 + e + 1 - NW)
                alone(sp, "sp")
                sp.wait_ge(expert_loaded[s], 32 * r)
                alone(sp, "sp")
                load(e, s)
            experts(sp, reload, NW, E1)

        @block.gpsimd
        def _(pool):
            def gather(e, s):
                alone(pool, "pool")
                pool.tensor_copy(IDX1[s][:, :], IDX[:, bass.ds(e, 1)]).then_inc(M["idx"], 1)
                pool.wait_ge(M["idx"], 1 + e + 1)
                alone(pool, "pool")
                pool.indirect_dma_start(out=XG[s][:, :], out_offset=None, in_=hx,
                                        in_offset=bass.IndirectOffsetOnAxis(ap=IDX1[s][:, 0:1], axis=0),
                                        ).then_inc(gathered[s], 16)

            def scatter(e, s, first=False):
                if not first:
                    pool.wait_ge(scattered, 16 * e)
                    alone(pool, "pool")
                pool.sem_inc(M["added"], 1)
                pool.wait_ge(M["y_sb"], 1 + e + 1)
                alone(pool, "pool")
                pool.indirect_dma_start(out=out, out_offset=bass.IndirectOffsetOnAxis(ap=IDX1[s][:, 0:1], axis=0),
                                        in_=YE[s % 4][:, :], in_offset=None, compute_op=ALU.add,
                                        ).then_inc(scattered, 16)

            def expert(e, s, r):
                scatter(e, s)
                pool.wait_ge(M["hm"], 1 + e + AHEAD - NX + 1)
                gather(e + AHEAD, (s + AHEAD) % NX)
            pool.wait_ge(idx_ready, 1)
            for e in range(AHEAD):
                gather(e, e)
            for e in range(NX - AHEAD):
                scatter(e, e, first=(e == 0))
                gather(e + AHEAD, e + AHEAD)
            alone(pool, "pool")
            experts(pool, expert, NX - AHEAD, E1 - AHEAD)
            for e in range(E1 - AHEAD, E1):
                scatter(e, e % NX)
            pool.wait_ge(scattered, 16 * E1)

        @block.tensor
        def _(pe):
            def rows_T(e, s, r):
                pe.wait_ge(gathered[s], 16 * (r + 1))
                pe.wait_ge(M["xgt_sb"], 1 + e - 1 if not isinstance(e, int) or e > 1 else 1)
                for k in range(KC):
                    mm = pe.transpose(bank(s % 2, k * P, (k + 1) * P), XG[s][:, k * P:(k + 1) * P], ident[:, :])
                mm.then_inc(M["xgt_ps"], 1)

            def gate_up(e, s, r, between=lambda: None):
                pe.wait_ge(expert_loaded[s], 32 * (r + 1))
                pe.wait_ge(M["xgt_sb"], 1 + e + 1)
                pe.wait_ge(M["hm"], 1 + e - 1 if not isinstance(e, int) or e > 1 else 1)
                for k in range(KC):
                    if k == KC // 2:
                        between()
                    mm = pe.matmul(bank(2 + s % 2, 0, 2 * F1), XGT[s % 2][:, k, :], W1[s][:, k, :], start=(k == 0),
                                   stop=(k == KC - 1))
                mm.then_inc(M["gu_ps"], 1)

            def hidden_T(e, s):
                pe.wait_ge(M["hm"], 1 + e + 1)
                pe.wait_ge(M["hmt_sb"], 1 + e)
                for h in range(2):
                    mm = pe.transpose(bank(4 + s % 2, h * P, (h + 1) * P, parts=FH), HM[s % 2][:, h * FH:(h + 1) * FH],
                                      ident[:, :])
                mm.then_inc(M["hmt_ps"], 1)

            def down(e, s, r):
                pe.wait_ge(M["hmt_sb"], 1 + e + 1)
                pe.wait_ge(M["y_sb"], 1 + e)
                for h in range(2):
                    mm = pe.matmul(bank(6 + s % 2), HMT[s % 2][:, h, :], W2[s][:, h, :], start=(h == 0), stop=(h == 1))
                mm.then_inc(M["y_ps"], 1)

            pe.wait_ge(lst_ready, 2)
            pe.transpose(bank(0, 0, E1), LST[:, :], ident[0:E1, 0:E1]).then_inc(lst_ps, 1)
            pe.wait_ge(idx_ready, 1)
            rows_T(0, 0, 0)
            gate_up(0, 0, 0)
            rows_T(1, 1, 0)

            def expert(e, s, r):
                last = isinstance(e, int) and e == E1 - 1
                gate_up(e, s, r, lambda: hidden_T(e - 1, (s - 1) % NW))
                if not last:
                    rows_T(e + 1, (s + 1) % NW, r + (s + 1) // NW)
                down(e - 1, (s - 1) % NW, r if s else r - 1)
            experts(pe, expert, 1, E1)
            hidden_T(E1 - 1, (E1 - 1) % NW)
            down(E1 - 1, (E1 - 1) % NW, (E1 - 1) // NW)

        @block.scalar
        def _(act):
            def rows_T(e, u):
                act.wait_ge(M["xgt_ps"], 1 + e + 1)
                act.wait_ge(M["gu_ps"], 1 + e - 1 if not isinstance(e, int) or e > 1 else 1)
                act.activation(XGT[u][:, :, :], bank(u).rearrange("p (k q) -> p k q", k=KC),
                               ACT.Copy).then_inc(M["xgt_sb"], 1)

            def silu(e, u):
                act.wait_ge(M["gu_ps"], 1 + e + 1)
                act.wait_ge(M["hm"], 1 + e - 1 if not isinstance(e, int) or e > 1 else 1)
                act.activation(SL[u][:, :], bank(2 + u, 0, F1), ACT.Silu).then_inc(M["sil"], 1)

            def down(e, s):
                act.wait_ge(M["y_ps"], 1 + e + 1)
                if not isinstance(e, int) or e > 3:
                    act.wait_ge(M["added"], 1 + e - 3)
                act.activation(YE[s % 4][:, :], bank(6 + s % 2), ACT.Copy).then_inc(M["y_sb"], 1)

            rows_T(0, 0)
            silu(0, 0)
            rows_T(1, 1)

            def expert(e, s, r):
                silu(e, s % 2)
                if not (isinstance(e, int) and e == E1 - 1):
                    rows_T(e + 1, (s + 1) % 2)
                down(e - 1, (s - 1) % NW)
            for e in range(1, 5):
                expert(e, e, 0)
            experts(act, expert, 5, E1)
            down(E1 - 1, (E1 - 1) % NW)

        @block.vector
        def _(dve):
            dve.tensor_copy(KEYS[0][:, 0:CAP], LST[:, :]).then_inc(lst_ready, 1)
            dve.wait_ge(lst_ready, 1)
            done = 6 * B * (NF // 2 - 1) * 2
            step = Chain(dve, S["list_dve"], 2 * CAP // 8, done)
            for c in range(CAP // 8):
                src, dst, group = KEYS[c % 2], KEYS[1 - c % 2], LST[:, 8 * c:8 * c + 8]
                step(dve.max(group, src[:, :]))
                step(dve.match_replace(dst[:, :], group, src[:, :], -1.0))
            step.end()
            dve.memset(lv[:, :], 0.0).then_inc(lst_ready, 1)
            dve.wait_ge(lst_ps, 1)
            dve.wait_ge(lst_ready, 2)
            step = Chain(dve, S["list_dve"], 4, done + 2 * CAP // 8)
            lt = bank(0, 0, E1)
            step(dve.tensor_scalar(lv[:, :], lt, 0.0, None, ALU.is_gt))
            step(dve.tensor_scalar(LT[:, :], lt, -1.0, float(2 * NTOK), ALU.mult, ALU.add))
            step(dve.tensor_scalar(LT[:, :], LT[:, :], dummy[:, 0:1], None, ALU.subtract))
            step(dve.tensor_tensor(LT[:, :], LT[:, :], lv[:, :], ALU.mult))
            dve.tensor_scalar(IDX[:, :], LT[:, :], dummy[:, 0:1], None, ALU.add).then_inc(idx_ready, 1)

            def gated(e, s, r):
                u = s % 2
                dve.wait_ge(M["hm"], 1 + e - 1 if not isinstance(e, int) or e > 1 else 1)
                dve.tensor_copy(WC[u][:, :], XG[s][:, bass.ds(C + e, 1)]).then_inc(M["wc"], 1)
                dve.wait_ge(M["wc"], 1 + e + 1)
                dve.wait_ge(M["sil"], 1 + e + 1)
                dve.scalar_tensor_tensor(out=HM[u][:, :], in0=SL[u][:, :], scalar=WC[u][:, 0:1],
                                         in1=bank(2 + u, F1, 2 * F1), op0=ALU.mult,
                                         op1=ALU.mult).then_inc(M["hm"], 1)

            def hidden_T(e, u):
                dve.wait_ge(M["hmt_ps"], 1 + e + 1)
                dve.wait_ge(M["y_ps"], 1 + e - 1 if not isinstance(e, int) or e > 1 else 1)
                dve.tensor_copy(HMT[u][:, :, :], bank(4 + u, 0, 2 * P, parts=FH).rearrange(
                    "p (h q) -> p h q", h=2)).then_inc(M["hmt_sb"], 1)
            dve.wait_ge(gathered[0], 16)
            gated(0, 0, 0)

            def expert(e, s, r):
                hidden_T(e - 1, (s - 1) % 2)
                dve.wait_ge(gathered[s], 16 * (r + 1))
                gated(e, s, r)
            experts(dve, expert, 1, E1)
            hidden_T(E1 - 1, 1)


BY_DMA = {"x_loaded", "ctx_loaded", "hx_stored", "out_stored", "dve_step", "g_dve", "g_pool", "list_dve", "f_dve", "rev_loaded"}
KSTEPS = {"f_dve": 38, "dve": 81, "g_dve": 2, "g_pool": 5}


def shape_constants():
    import numpy as np
    p = np.arange(P)
    c = {}
    c["ident"] = np.eye(P, dtype=np.float32)
    bf = mybir.dt.np(BF16)
    c["identb"] = np.eye(P).astype(bf)
    later = p[None, :] > p[:, None]
    c["mask_qk"] = np.where(later, -1e30, 0.0).astype(bf)
    c["mask_kq"] = np.where(later.T, -1e30, 0.0).astype(bf)
    c["dummy"] = (NTOK + p).astype(np.float32)[:, None]
    c["revt"] = np.tile(2 * NTOK - np.arange(NTOK, dtype=np.float32), (E1, 1))
    r = p % 32
    live = (r < NT * HPG) & (p < 64)
    c["blockmask"] = ((r[:, None] // HPG == np.arange(NT)) & live[:, None]).astype(np.float32)[:, :, None] * np.ones(
        (1, 1, P), np.float32)
    c["sel"] = ((r[:, None] % HPG == np.arange(HPG)) & live[:, None]).astype(np.float32)[:, :, None] * np.ones(
        (1, 1, P), np.float32)
    inv = (np.float32(1.0) / np.float32(10000.0) ** (np.arange(0, HD, 2, dtype=np.float32) / np.float32(HD)))
    fr = np.outer(np.arange(T, dtype=np.float32), inv.astype(np.float32)).astype(np.float32)
    emb = np.concatenate([fr, fr], -1)
    cos, sin = np.cos(emb.astype(np.float64)), np.sin(emb.astype(np.float64))
    sin = sin * np.where(np.arange(HD) < ROT, -1.0, 1.0)
    tiled = lambda a: np.ascontiguousarray(a.astype(np.float32).reshape(NT, P, HD).transpose(1, 0, 2))
    scale = float(HD) ** -0.5
    c["cos_q"], c["sin_q"], c["cos_k"], c["sin_k"] = tiled(cos * scale), tiled(sin * scale), tiled(cos), tiled(sin)
    return c


def lay_out(i):
    import numpy as np
    a = {k: np.asarray(v) for k, v in i.items()}
    kp = lambda m: np.ascontiguousarray(m.reshape(KC, P, -1).transpose(1, 0, 2))
    o = {}
    o["wo"] = kp(a["L0_xattn_w_out"].T)
    ex = lambda m: m.transpose(1, 0, 2).reshape(m.shape[1], -1)
    o["acat"] = kp(np.concatenate([a["L0_ffn_W_router"], a["L0_ffn_sA_gate"], ex(a["L0_ffn_A_gate"]),
                                   a["L0_ffn_sA_up"], ex(a["L0_ffn_A_up"])], 1))
    rowsb = lambda s, m: np.concatenate([s, m.reshape(E0 * R0, -1)], 0)
    o["bdown"] = np.ascontiguousarray(rowsb(a["L0_ffn_sB_down"], a["L0_ffn_B_down"]))
    st = np.zeros((NF, P, WCOLS), np.float32)
    bg, bu = rowsb(a["L0_ffn_sB_gate"], a["L0_ffn_B_gate"]), rowsb(a["L0_ffn_sB_up"], a["L0_ffn_B_up"])
    ad = np.concatenate([a["L0_ffn_sA_down"], ex(a["L0_ffn_A_down"])], 1)
    for f in range(NF):
        f0, f1 = f * P, min((f + 1) * P, DFF)
        n = f1 - f0
        for h, m in enumerate((a["L0_ffn_W_gate"], a["L0_ffn_W_up"])):
            for k in range(KC):
                st[f, :, k * 2 * P + h * P:k * 2 * P + h * P + n] = m[k * P:(k + 1) * P, f0:f1]
        st[f, 0:n, WD:WD + C] = a["L0_ffn_W_down"][f0:f1]
        st[f, 0:LR, WBG:WBG + n] = bg[:, f0:f1]
        st[f, 0:LR, WBU:WBU + n] = bu[:, f0:f1]
        st[f, 0:n, WAD:WAD + LR] = ad[f0:f1]
    o["ffn"] = st.reshape(NF * P, WCOLS)
    o["wk"] = np.ascontiguousarray(a["L1_xattn_W_k"].T)
    o["rw"] = kp(a["L1_ffn_router_w"].T)
    o["bk"], o["gamma"], o["beta"] = a["L1_xattn_b_k"], a["L1_xattn_ln_gamma"], a["L1_xattn_ln_beta"]
    o["ebias"], o["wq"], o["wkn"] = a["L0_ffn_expert_bias"], a["L0_xattn_q_norm_w"], a["L0_xattn_k_norm_w"]
    gu = np.concatenate([a["L1_ffn_w_gate"], a["L1_ffn_w_up"]], 2)
    o["w1"] = np.ascontiguousarray(gu.reshape(E1, KC, P, 2 * F1).transpose(0, 2, 1, 3)).reshape(E1 * P, -1)
    o["w2"] = np.ascontiguousarray(a["L1_ffn_w_down"].reshape(E1, 2, FH, C).transpose(0, 2, 1, 3)).reshape(
        E1 * FH, -1)
    o["x"] = np.concatenate([a["x"].reshape(NTOK, C), np.zeros((T, C), np.float32)], 0)
    o["ctx"] = np.concatenate([a["ctx_512"].reshape(NTOK, CKV), np.zeros((T, CKV), np.float32)], 0)
    return o


def kernel(**inputs):
    import numpy as np
    import concourse.bacc as bacc
    from concourse.bass_utils import run_bass_kernel_spmd as run

    nc = bacc.Bacc("TRN2", target_bir_lowering=False, num_devices=1)
    arrays = {"in_" + k: np.ascontiguousarray(v) for k, v in {**lay_out(inputs), **shape_constants()}.items()}
    ap = {k[3:]: nc.dram_tensor(k, v.shape, mybir.dt.from_np(v.dtype), kind="ExternalInput").ap()
          for k, v in arrays.items()}
    out = nc.dram_tensor("out", (ROWS, C), F32, kind="ExternalOutput").ap()
    hx = nc.dram_tensor("hx", (ROWS, HROW), F32, kind="Internal").ap()
    build(nc, ap["x"], ap["ctx"], ap, out, hx)
    r = run(nc, [arrays], core_ids=[0])
    return r.results[0]["out"][0:NTOK].reshape(B, T, C)
```
